# Optimizing a Trainium2 kernel written in Bass

```python
import numpy as np
import jax
import jax.numpy as jnp

def _softmax(x, axis=-1):
    return jax.nn.softmax(x, axis=axis)

def _gelu(x):
    return jax.nn.gelu(x, approximate=True)

def _silu(x):
    return jax.nn.silu(x)

def _sigmoid(x):
    return jax.nn.sigmoid(x)

def _layernorm(x, axis=-1, eps=1e-05):
    m = jnp.mean(x, axis=axis, keepdims=True)
    v = jnp.var(x, axis=axis, keepdims=True)
    return (x - m) / jnp.sqrt(v + eps)

def _scatter_add(tgt, idx, src, axis=0):
    return tgt.at[idx].add(src)

def _segment_sum(src, seg, n):
    return jax.ops.segment_sum(src, seg, n)
kernel_name = 'mk_flamingo_gated_d2_seqx_r4_308b7f'

def setup_inputs(seed: int=0):
    np.random.seed(seed)
    _w = jnp.asarray

    def _rec_inputs():
        import jax
        import jax.numpy as jnp
        _rk = jax.random.key(seed)
        x = 2.818e-05 + 1 * jax.random.normal(jax.random.fold_in(_rk, 1), (4, 512, 512), jnp.float32)
        _lenS = 512 - jax.random.randint(jax.random.fold_in(_rk, 7), (4,), 0, max(1, 512 // 4) + 1, jnp.int32)
        _lenS2 = 512 - jax.random.randint(jax.random.fold_in(_rk, 8), (4,), 0, max(1, 512 // 4) + 1, jnp.int32)
        _ctx_1024P = jax.random.normal(jax.random.fold_in(_rk, 11), (4, 16, 256), jnp.float32)
        _ctx_1024c = jax.random.dirichlet(jax.random.fold_in(_rk, 511), 0.3 * jnp.ones((16,), jnp.float32), (4, 512))
        _ctx_1024t = jnp.einsum('bsk,bkd->bsd', _ctx_1024c, _ctx_1024P)
        _ctx_1024t = _ctx_1024t * jax.lax.rsqrt(jnp.mean(jnp.square(_ctx_1024t)) + 1e-12) * 0.953939
        ctx_1024 = 7.22013e-05 + 1.00017 * (_ctx_1024t + 0.3 * jax.random.normal(jax.random.fold_in(_rk, 611), (4, 512, 256), jnp.float32))
        fside_BxSx2_0 = jax.random.uniform(jax.random.fold_in(_rk, 12), (4, 512, 2), jnp.float32, 0.0, 0.999707)
        _g = jax.random.normal(jax.random.fold_in(_rk, 9001), (2, 2), jnp.float32)
        _g = jnp.sign(_g) * jnp.maximum(jnp.abs(_g), 1.0) + (_g == 0) * 1.0
        g_xattn = _g[0]
        g_ffn = _g[1]
        return (x, ctx_1024, fside_BxSx2_0, g_xattn, g_ffn)
    x, ctx_1024, fside_BxSx2_0, g_xattn, g_ffn = _rec_inputs()

    def _L0_xattn_setup():
        import jax, jax.numpy as jnp
        import numpy as np
        B_, L_, D_MODEL = (4, 512, 256)
        D_STATE, D_CONV, EXPAND = (16, 4, 2)
        D_INNER = EXPAND * D_MODEL
        DT_RANK = (D_MODEL + 15) // 16

        def silu(x):
            return x * jax.nn.sigmoid(x)
        key = jax.random.key(seed)
        ks = jax.random.split(key, 10)
        f32 = jnp.float32
        hidden_states = jax.random.normal(ks[0], (B_, L_, D_MODEL), dtype=f32)
        z = jax.random.normal(ks[1], (B_, D_INNER, L_), dtype=f32)
        in_proj_w = jax.random.normal(ks[2], (D_INNER, D_MODEL), dtype=f32) * 0.02
        conv_w = jax.random.normal(ks[3], (D_INNER, 1, D_CONV), dtype=f32) * 0.1
        conv_b = jax.random.normal(ks[4], (D_INNER,), dtype=f32) * 0.02
        x_proj_w = jax.random.normal(ks[5], (DT_RANK + 2 * D_STATE, D_INNER), dtype=f32) * 0.02
        dt_proj_w = jax.random.uniform(ks[6], (D_INNER, DT_RANK), dtype=f32, minval=-DT_RANK ** (-0.5), maxval=DT_RANK ** (-0.5))
        dt = jnp.exp(jax.random.uniform(ks[7], (D_INNER,), dtype=f32, minval=np.log(0.001), maxval=np.log(0.1)))
        dt_proj_b = jnp.log(jnp.expm1(dt))
        A_log = jnp.log(jnp.broadcast_to(jnp.arange(1, D_STATE + 1, dtype=f32), (D_INNER, D_STATE)))
        D = jnp.ones((D_INNER,), f32)
        return {'hidden_states': hidden_states, 'z': z, 'in_proj_w': in_proj_w, 'conv_w': conv_w, 'conv_b': conv_b, 'x_proj_w': x_proj_w, 'dt_proj_w': dt_proj_w, 'dt_proj_b': dt_proj_b, 'A_log': A_log, 'D': D}
    _L0_xattn_all = _L0_xattn_setup()
    _L0_xattn_in = {k: v for k, v in _L0_xattn_all.items() if k in ('in_proj_w', 'conv_w', 'conv_b', 'x_proj_w', 'dt_proj_w', 'dt_proj_b', 'A_log', 'D')}
    del _L0_xattn_all

    def _L0_ffn_setup():
        import jax, jax.numpy as jnp
        import numpy as np
        B, S, H = (1, 256, 512)
        F = 256
        E = 16
        K = 2
        NS = 1
        ROUTE_SCALE = 1.0
        key = jax.random.key(seed)
        ks = jax.random.split(key, 8)

        def w(k, shape, fan_in):
            return jax.random.normal(k, shape, jnp.float32) * fan_in ** (-0.5)
        return {'hidden_states': jax.random.normal(ks[0], (B, S, H), jnp.float32), 'gate_w': w(ks[1], (H, E), H), 'expert_bias': jnp.zeros((E,), jnp.float32), 'shared_gate_w': w(ks[2], (H, F * NS), H), 'shared_up_w': w(ks[3], (H, F * NS), H), 'shared_down_w': w(ks[4], (F * NS, H), F * NS), 'experts_gate_up': w(ks[5], (E, H, 2 * F), H), 'experts_down': w(ks[6], (E, F, H), F)}
    _L0_ffn_all = _L0_ffn_setup()
    _L0_ffn_in = {k: v for k, v in _L0_ffn_all.items() if k in ('gate_w', 'expert_bias', 'shared_gate_w', 'shared_up_w', 'shared_down_w', 'experts_gate_up', 'experts_down')}
    del _L0_ffn_all

    def _L1_xattn_setup():
        import jax, jax.numpy as jnp
        import numpy as np
        DIM = 512
        CTX_DIM = 256
        N_HEADS = 32
        HEAD_DIM = DIM // N_HEADS
        POS_DIM = 2
        B, N, CTXN = (2, 512, 512)
        ROPE_BASE = 10000.0

        def apply_axial_rope(x, pos):
            b, n, h, d = x.shape
            p = pos.shape[-1]
            dpa = d // p
            half = dpa // 2
            freqs = ROPE_BASE ** (-jnp.arange(half, dtype=x.dtype) / half)
            ang = pos[..., :, None] * freqs
            cos = jnp.cos(ang)[:, :, None, :, :]
            sin = jnp.sin(ang)[:, :, None, :, :]
            xr = x.reshape(b, n, h, p, half, 2)
            x1, x2 = (xr[..., 0], xr[..., 1])
            out = jnp.stack([x1 * cos - x2 * sin, x1 * sin + x2 * cos], axis=-1)
            return out.reshape(b, n, h, d)
        key = jax.random.key(seed)
        ks = jax.random.split(key, 8)
        x = jax.random.normal(ks[0], (B, N, DIM), jnp.float32)
        ctx = jax.random.normal(ks[1], (B, CTXN, CTX_DIM), jnp.float32)
        pos_map = jax.random.uniform(ks[2], (B, N, POS_DIM), jnp.float32)
        ctx_pos_map = jax.random.uniform(ks[3], (B, CTXN, POS_DIM), jnp.float32)
        Wq = jax.random.normal(ks[4], (DIM, DIM), jnp.float32) / np.sqrt(DIM)
        Wkv = jax.random.normal(ks[5], (CTX_DIM, 2 * DIM), jnp.float32) / np.sqrt(CTX_DIM)
        Wout = jax.random.normal(ks[6], (DIM, DIM), jnp.float32) / np.sqrt(DIM)
        bout = jnp.zeros((DIM,), jnp.float32)
        return {'x': x, 'ctx': ctx, 'pos_map': pos_map, 'ctx_pos_map': ctx_pos_map, 'Wq': Wq, 'Wkv': Wkv, 'Wout': Wout, 'bout': bout}
    _L1_xattn_all = _L1_xattn_setup()
    _L1_xattn_in = {k: v for k, v in _L1_xattn_all.items() if k in ('Wq', 'Wkv', 'Wout', 'bout')}
    del _L1_xattn_all

    def _L1_ffn_setup():
        import jax, jax.numpy as jnp
        import numpy as np
        EPS = 1e-05

        def _bitlinear(x, w):
            rms = jax.lax.rsqrt(jnp.maximum(jnp.mean(w * w), EPS))
            w_quant = jnp.clip(jnp.round(w * rms), -1.0, 1.0) / rms
            w_quant = jax.lax.stop_gradient(w_quant - w) + w
            scale = 127.0 / jnp.maximum(jnp.max(jnp.abs(x), axis=-1, keepdims=True), EPS)
            x_quant = jnp.clip(jnp.round(x * scale), -128.0, 127.0) / scale
            x_quant = jax.lax.stop_gradient(x_quant - x) + x
            return jnp.einsum('bsd,fd->bsf', x_quant, w_quant)
        key = jax.random.key(seed)
        k1, k2, k3 = jax.random.split(key, 3)
        n_embd, d_ff = (512, 2048)
        B, S = (4, 512)
        x = jax.random.normal(k1, (B, S, n_embd), dtype=jnp.float32)
        w1 = jax.random.normal(k2, (d_ff, n_embd), dtype=jnp.float32) * 0.02
        w2 = jax.random.normal(k3, (n_embd, d_ff), dtype=jnp.float32) * 0.02
        return {'x': x, 'w1': w1, 'w2': w2}
    _L1_ffn_all = _L1_ffn_setup()
    _L1_ffn_in = {k: v for k, v in _L1_ffn_all.items() if k in ('w1', 'w2')}
    del _L1_ffn_all
    return {'x': x, 'ctx_1024': ctx_1024, 'fside_BxSx2_0': fside_BxSx2_0, 'g_xattn': g_xattn, 'g_ffn': g_ffn, 'L0_xattn_in_proj_w': _L0_xattn_in['in_proj_w'], 'L0_xattn_conv_w': _L0_xattn_in['conv_w'], 'L0_xattn_conv_b': _L0_xattn_in['conv_b'], 'L0_xattn_x_proj_w': _L0_xattn_in['x_proj_w'], 'L0_xattn_dt_proj_w': _L0_xattn_in['dt_proj_w'], 'L0_xattn_dt_proj_b': _L0_xattn_in['dt_proj_b'], 'L0_xattn_A_log': _L0_xattn_in['A_log'], 'L0_xattn_D': _L0_xattn_in['D'], 'L0_ffn_gate_w': _L0_ffn_in['gate_w'], 'L0_ffn_expert_bias': _L0_ffn_in['expert_bias'], 'L0_ffn_shared_gate_w': _L0_ffn_in['shared_gate_w'], 'L0_ffn_shared_up_w': _L0_ffn_in['shared_up_w'], 'L0_ffn_shared_down_w': _L0_ffn_in['shared_down_w'], 'L0_ffn_experts_gate_up': _L0_ffn_in['experts_gate_up'], 'L0_ffn_experts_down': _L0_ffn_in['experts_down'], 'L1_xattn_Wq': _L1_xattn_in['Wq'], 'L1_xattn_Wkv': _L1_xattn_in['Wkv'], 'L1_xattn_Wout': _L1_xattn_in['Wout'], 'L1_xattn_bout': _L1_xattn_in['bout'], 'L1_ffn_w1': _L1_ffn_in['w1'], 'L1_ffn_w2': _L1_ffn_in['w2']}

def reference(x, ctx_1024, fside_BxSx2_0, g_xattn, g_ffn, L0_xattn_in_proj_w, L0_xattn_conv_w, L0_xattn_conv_b, L0_xattn_x_proj_w, L0_xattn_dt_proj_w, L0_xattn_dt_proj_b, L0_xattn_A_log, L0_xattn_D, L0_ffn_gate_w, L0_ffn_expert_bias, L0_ffn_shared_gate_w, L0_ffn_shared_up_w, L0_ffn_shared_down_w, L0_ffn_experts_gate_up, L0_ffn_experts_down, L1_xattn_Wq, L1_xattn_Wkv, L1_xattn_Wout, L1_xattn_bout, L1_ffn_w1, L1_ffn_w2):
    import jax
    import jax.numpy as jnp

    def _L0_xattn_ref(hidden_states, z, in_proj_w, conv_w, conv_b, x_proj_w, dt_proj_w, dt_proj_b, A_log, D):
        import jax, jax.numpy as jnp
        import numpy as np
        B_, L_, D_MODEL = (4, 512, 256)
        D_STATE, D_CONV, EXPAND = (16, 4, 2)
        D_INNER = EXPAND * D_MODEL
        DT_RANK = (D_MODEL + 15) // 16

        def silu(x):
            return x * jax.nn.sigmoid(x)
        Bsz, L, _ = hidden_states.shape
        d_inner, _, d_conv = conv_w.shape
        dt_rank = dt_proj_w.shape[1]
        d_state = A_log.shape[1]
        x = jnp.einsum('bld,ed->bel', hidden_states, in_proj_w)
        xc = jax.lax.conv_general_dilated(x, conv_w, window_strides=(1,), padding=[(d_conv - 1, 0)], feature_group_count=d_inner, dimension_numbers=('NCH', 'OIH', 'NCH'))
        x = silu(xc + conv_b[None, :, None])
        x_dbl = jnp.einsum('bdl,ed->bel', x, x_proj_w)
        dt_low, Bm, Cm = jnp.split(x_dbl, [dt_rank, dt_rank + d_state], axis=1)
        dt = jnp.einsum('brl,dr->bdl', dt_low, dt_proj_w)
        dt = jax.nn.softplus(dt + dt_proj_b[None, :, None])
        A = -jnp.exp(A_log)
        dt_t = jnp.moveaxis(dt, -1, 0)
        B_t = jnp.moveaxis(Bm, -1, 0)
        C_t = jnp.moveaxis(Cm, -1, 0)
        u_t = jnp.moveaxis(x, -1, 0)

        def step(state, inp):
            d, b, c, u = inp
            dA = jnp.exp(d[..., None] * A)
            state = state * dA + (d * u)[..., None] * b[:, None, :]
            y = jnp.einsum('bdn,bn->bd', state, c)
            return (state, y)
        state0 = jnp.zeros((Bsz, d_inner, d_state), x.dtype)
        _, ys = jax.lax.scan(step, state0, (dt_t, B_t, C_t, u_t))
        y = jnp.moveaxis(ys, 0, 2)
        y = y + D[None, :, None] * x
        y = y * silu(z)
        return jnp.swapaxes(y, 1, 2)

    def _L0_ffn_ref(hidden_states, gate_w, expert_bias, shared_gate_w, shared_up_w, shared_down_w, experts_gate_up, experts_down):
        import jax, jax.numpy as jnp
        import numpy as np
        B, S, H = (1, 256, 512)
        F = 256
        E = 16
        K = 2
        NS = 1
        ROUTE_SCALE = 1.0
        b, s, h = hidden_states.shape
        x = hidden_states.reshape(-1, h)
        T = x.shape[0]
        router_logits = (x @ gate_w).astype(jnp.float32)
        scores = jax.nn.sigmoid(router_logits)
        _, selected = jax.lax.top_k(scores + expert_bias[None, :], K)
        top_scores = jnp.take_along_axis(scores, selected, axis=1)
        top_scores = top_scores / (top_scores.sum(-1, keepdims=True) + 1e-20)
        top_scores = top_scores * ROUTE_SCALE
        shared = jax.nn.silu(x @ shared_gate_w) * (x @ shared_up_w) @ shared_down_w
        comb = jnp.zeros((T, E), jnp.float32).at[jnp.arange(T)[:, None], selected].add(top_scores)
        routed = jnp.zeros_like(x)
        for e in range(E):
            gu = x @ experts_gate_up[e]
            g, u = jnp.split(gu, 2, axis=-1)
            routed = routed + comb[:, e:e + 1] * (jax.nn.silu(g) * u @ experts_down[e])
        return (shared + routed).reshape(b, s, h)

    def _L1_xattn_ref(x, ctx, pos_map, ctx_pos_map, Wq, Wkv, Wout, bout):
        import jax, jax.numpy as jnp
        import numpy as np
        DIM = 512
        CTX_DIM = 256
        N_HEADS = 32
        HEAD_DIM = DIM // N_HEADS
        POS_DIM = 2
        B, N, CTXN = (2, 512, 512)
        ROPE_BASE = 10000.0

        def apply_axial_rope(x, pos):
            b, n, h, d = x.shape
            p = pos.shape[-1]
            dpa = d // p
            half = dpa // 2
            freqs = ROPE_BASE ** (-jnp.arange(half, dtype=x.dtype) / half)
            ang = pos[..., :, None] * freqs
            cos = jnp.cos(ang)[:, :, None, :, :]
            sin = jnp.sin(ang)[:, :, None, :, :]
            xr = x.reshape(b, n, h, p, half, 2)
            x1, x2 = (xr[..., 0], xr[..., 1])
            out = jnp.stack([x1 * cos - x2 * sin, x1 * sin + x2 * cos], axis=-1)
            return out.reshape(b, n, h, d)
        b, n, _ = x.shape
        ctx_n = ctx.shape[1]
        q = (x @ Wq).reshape(b, n, N_HEADS, HEAD_DIM)
        k, v = jnp.split(ctx @ Wkv, 2, axis=-1)
        k = k.reshape(b, ctx_n, N_HEADS, HEAD_DIM)
        v = v.reshape(b, ctx_n, N_HEADS, HEAD_DIM)
        q = apply_axial_rope(q, pos_map)
        k = apply_axial_rope(k, ctx_pos_map)
        scale = 1.0 / np.sqrt(HEAD_DIM).astype(np.float32)
        logits = jnp.einsum('bqhd,bkhd->bhqk', q, k) * scale
        w = jax.nn.softmax(logits, axis=-1)
        attn = jnp.einsum('bhqk,bkhd->bqhd', w, v)
        attn = attn.reshape(b, n, N_HEADS * HEAD_DIM)
        return attn @ Wout + bout

    def _L1_ffn_ref(x, w1, w2):
        import jax, jax.numpy as jnp
        import numpy as np
        EPS = 1e-05

        def _bitlinear(x, w):
            rms = jax.lax.rsqrt(jnp.maximum(jnp.mean(w * w), EPS))
            w_quant = jnp.clip(jnp.round(w * rms), -1.0, 1.0) / rms
            w_quant = jax.lax.stop_gradient(w_quant - w) + w
            scale = 127.0 / jnp.maximum(jnp.max(jnp.abs(x), axis=-1, keepdims=True), EPS)
            x_quant = jnp.clip(jnp.round(x * scale), -128.0, 127.0) / scale
            x_quant = jax.lax.stop_gradient(x_quant - x) + x
            return jnp.einsum('bsd,fd->bsf', x_quant, w_quant)
        h = _bitlinear(x, w1)
        h = jax.nn.gelu(h, approximate=False)
        out = _bitlinear(h, w2)
        return out
    x = x + jnp.tanh(g_xattn[0]) * _L0_xattn_ref(ctx_1024, _layernorm(x, axis=-1), L0_xattn_in_proj_w, L0_xattn_conv_w, L0_xattn_conv_b, L0_xattn_x_proj_w, L0_xattn_dt_proj_w, L0_xattn_dt_proj_b, L0_xattn_A_log, L0_xattn_D)
    x = x + jnp.tanh(g_ffn[0]) * _L0_ffn_ref(_layernorm(x, axis=-1), L0_ffn_gate_w, L0_ffn_expert_bias, L0_ffn_shared_gate_w, L0_ffn_shared_up_w, L0_ffn_shared_down_w, L0_ffn_experts_gate_up, L0_ffn_experts_down)
    x = x + jnp.tanh(g_xattn[1]) * _L1_xattn_ref(_layernorm(x, axis=-1), ctx_1024, fside_BxSx2_0, fside_BxSx2_0, L1_xattn_Wq, L1_xattn_Wkv, L1_xattn_Wout, L1_xattn_bout)
    x = x + jnp.tanh(g_ffn[1]) * _L1_ffn_ref(_layernorm(x, axis=-1), L1_ffn_w1, L1_ffn_w2)
    return x

_drawn_inputs = setup_inputs


def setup_inputs(seed=0):
    import zlib

    import numpy as np

    out = dict(_drawn_inputs(seed))
    spreads = {'g_ffn': (-1.0, 0.6),
     'L0_xattn_D': (1.0, 0.6),
     'L0_ffn_expert_bias': (0.0, 0.1),
     'L1_xattn_bout': (0.0, 0.1)}
    factors = {'L0_xattn_conv_b': 3.154,
     'L0_xattn_x_proj_w': 8.0,
     'L0_xattn_dt_proj_w': 8.0,
     'L0_xattn_dt_proj_b': 8.0,
     'L0_xattn_A_log': 8.0}
    for name, (base, spread) in spreads.items():
        noise = np.random.default_rng([zlib.crc32(name.encode()), seed]).standard_normal(out[name].shape)
        drawn = base * np.exp(spread * noise) if base else spread * noise
        out[name] = jnp.asarray(drawn.astype(out[name].dtype))
    for name, factor in factors.items():
        out[name] = (out[name] * factor).astype(out[name].dtype)
    return out
```

```python
from contextlib import ExitStack

import numpy as np

import concourse.bass as bass
from concourse import mybir

F32 = mybir.dt.float32
BF16 = mybir.dt.bfloat16
I32 = mybir.dt.int32
U32 = mybir.dt.uint32
U8 = mybir.dt.uint8
ALU = mybir.AluOpType
ACT = mybir.ActivationFunctionType
AX = mybir.AxisListType

P = 128
B, L, D = 4, 512, 512
DC = 256
T = B * L
NT = T // P
TB = L // P
KD = D // P
KC = DC // P
E4 = D // P
NS = 16
R = 16
EPS = 1e-5

LN_VAR = 2 * NT + 1
LN_RSTD = 2 * NT + 2
LN_READY = 2 * NT + 3


def mamba(nc, x_sb, ident, tg, a, bc_dram):
    JOBS = 2 * E4
    STEPS = NS // 4
    with ExitStack() as ctx:
        def sb(name, shape, dt=F32):
            return ctx.enter_context(nc.sbuf_tensor("m_" + name, shape, dt))

        def sem(name):
            return ctx.enter_context(nc.semaphore("m_" + name))

        ctxT = sb("ctxT", [P, 2, KC, L])
        w_in = sb("w_in", [P, KC, D])
        w_xp = sb("w_xp", [P, E4, R + 2 * NS])
        w_dt = sb("w_dt", [R, D])
        conv_w = sb("conv_w", [P, E4, 4])
        conv_b = sb("conv_b", [P, E4])
        dt_b = sb("dt_b", [P, E4])
        negA = sb("negA", [P, E4 * NS])
        Dcol = sb("Dcol", [P, E4])
        diagD = sb("diagD", [P, E4, P])
        stats = sb("stats", [P, NT, 6])
        mv = sb("mv", [P, NT, 2])
        rstd = sb("rstd", [P, NT])
        nmr = sb("nmr", [P, NT])
        xpad = sb("xpad", [P, E4, L + 3])
        conv = sb("conv", [P, E4, L])
        u = sb("u", [P, 2, E4, L])
        dt = sb("dt", [P, 2, E4, L])
        dtu = sb("dtu", [P, 2, E4, L])
        gate = sb("gate", [P, 2, TB, L])
        xdbl = sb("xdbl", [R + 2 * NS, 2, L])
        ee = sb("ee", [P, E4, L])
        ll = sb("ll", [P, E4, L])
        small = sb("small", [P, E4, L], U8)
        bch = sb("bch", [P, 2, 2, 2, L])
        dA = sb("dA", [P, 2, 2, L])
        dBu = sb("dBu", [P, 2, 2, L])
        hs = sb("hs", [P, 2, 2, L])
        hc = sb("hc", [P, 2, 2, L])
        ty = sb("ty", [P, 2, L])
        py = [ctx.enter_context(nc.psum_tensor(f"m_y{i}", [P, L], F32)) for i in range(E4)]
        pp = [ctx.enter_context(nc.psum_tensor(f"m_p{i}", [P, L], F32)) for i in range(2)]
        px = ctx.enter_context(nc.psum_tensor("m_x", [P, L], F32))
        pt = ctx.enter_context(nc.psum_tensor("m_t", [P, TB, P], F32))

        s_wld = sem("weights_loaded")
        s_ctx = [sem(f"ctx_loaded{i}") for i in range(2)]
        s_bc = [sem(f"bc_loaded{i}") for i in range(2)]
        s_bcst = sem("bc_stored")
        s_pad = sem("pad_zeroed")
        s_dz = sem("da_zeroed")
        s_ln = sem("ln_steps")
        s_sd = sem("ln_std")
        s_negA0 = sem("expA")
        s_negA = sem("negA_ready")
        s_diag = sem("diagD_ready")
        s_xin = sem("inproj_done")
        s_xc = sem("inproj_copied")
        s_cv = sem("conv_steps")
        s_u = sem("u_ready")
        s_gate = sem("gate_ready")
        s_xd = sem("xdbl_done")
        s_xdc = sem("xdbl_copied")
        s_dtp = sem("dt_product")
        s_abs = sem("dt_abs")
        s_rel = sem("dt_relu")
        s_e = sem("exp_neg_abs")
        s_l = sem("ln1p")
        s_q = sem("series_steps")
        s_m = sem("small_mask")
        s_pick = sem("picked")
        s_dt = sem("dt_ready")
        s_dtu = sem("dtu_ready")
        s_dA = sem("decay_ready")
        s_dbu = sem("input_ready")
        s_scan = sem("scanned")
        s_hc = sem("output_terms")
        s_y = sem("summed")
        s_y0 = sem("sum_started")
        s_g = sem("gated")
        s_t = sem("transposed")
        s_add = sem("added")

        block = ctx.enter_context(nc.Block())

        def job0(b):
            return b * STEPS * JOBS

        @block.sync
        def _(sp):
            sp.dma_start(w_in[:], a["in_wT"].rearrange("(k p) e -> p k e", p=P)).then_inc(s_wld, 16)
            sp.dma_start(conv_w[:], a["conv_w"].rearrange("(t p) o k -> p t (o k)", p=P)).then_inc(s_wld, 16)
            sp.dma_start(conv_b[:], a["conv_b"]).then_inc(s_wld, 16)
            sp.dma_start(w_xp[:], a["xp_wT"].rearrange("(k p) e -> p k e", p=P)).then_inc(s_wld, 16)
            sp.dma_start(w_dt[:], a["dt_wT"]).then_inc(s_wld, 16)
            sp.dma_start(dt_b[:], a["dt_b"]).then_inc(s_wld, 16)
            sp.dma_start(negA[:].rearrange("p (t n) -> p t n", t=E4),
                         a["A_log"].rearrange("(t p) n -> p t n", p=P)).then_inc(s_wld, 16)
            sp.dma_start(Dcol[:], a["Dv"]).then_inc(s_wld, 16)

            def load_ctx(b):
                if b >= 2:
                    sp.wait_ge(s_xin, E4 * (b - 1))
                sp.dma_start(ctxT[:, b % 2], a["ctxT"][:, b * L:(b + 1) * L].rearrange("(k p) l -> p k l", p=P))\
                    .then_inc(s_ctx[b % 2], 16)

            load_ctx(0)
            load_ctx(1)
            for b in range(B):
                sp.wait_ge(s_xdc, b + 1)
                sp.dma_start(bc_dram[b], xdbl[R:R + 2 * NS, b % 2, :]).then_inc(s_bcst, 16)
                sp.wait_ge(s_bcst, 16 * (b + 1))
                if b + 2 < B:
                    load_ctx(b + 2)

                def load_chunk(b, k, i, first):
                    c = b * 8 + i * 2 + k
                    if not first:
                        sp.wait_ge(s_dbu, c * E4 - E4)
                        sp.wait_ge(s_hc, c * E4 - E4)
                    for m in range(2):
                        src = bc_dram[b:b + 1, bass.ds(i * 4 + m * NS + k * 2, 2), :].rearrange(
                            "o k l -> o (k l)").partition_broadcast(P)
                        sp.dma_start(bch[:, k, m].rearrange("p s l -> p (s l)"), src).then_inc(s_bc[k], 16)

                if b == 0:
                    load_chunk(b, 0, 0, True)
                    load_chunk(b, 1, 0, True)
                    with sp.Fori(1, STEPS) as i:
                        for k in range(2):
                            load_chunk(b, k, i, False)
                else:
                    with sp.Fori(0, STEPS) as i:
                        for k in range(2):
                            load_chunk(b, k, i, False)

        @block.gpsimd
        def _(pool):
            pool.memset(xpad[:, :, 0:3], 0.0).then_inc(s_pad, 1)
            pool.memset(dA[:], 0.0).then_inc(s_dz, 1)

            def prep_b(b):
                p = b % 2
                pool.wait_ge(s_e, b + 1)
                if b >= 1:
                    pool.wait_ge(s_pick, b)
                pool.tensor_scalar(small[:], ee[:], 1.0 / 32, None, ALU.is_lt).then_inc(s_m, 1)
                pool.wait_ge(s_pick, b + 1)
                pool.tensor_tensor(dt[:, p], dt[:, p], ll[:], ALU.add).then_inc(s_dt, 1)
                pool.wait_ge(s_dt, b + 1)
                pool.tensor_tensor(dtu[:, p], dt[:, p], u[:, p], ALU.mult).then_inc(s_dtu, 1)

            def step(b, i):
                for k in range(2):
                    pool.wait_ge(s_bc[k], (i + b * STEPS) * 32 + 32)
                    for et in range(E4):
                        n = (i + b * STEPS) * JOBS + k * E4 + et
                        if not (b == 0 and isinstance(i, int) and i == 0 and k == 0 and et < 2):
                            pool.wait_ge(s_scan, n - 1)
                        pool.tensor_tensor(dBu[:, et % 2], bch[:, k, 0],
                                           dtu[:, b % 2, et].unsqueeze(1).broadcast_to([P, 2, L]),
                                           ALU.mult).then_inc(s_dbu, 1)

            prep_b(0)
            for b in range(B):
                if b == 0:
                    pool.wait_ge(s_dtu, 1)
                    step(b, 0)
                    with pool.Fori(1, 2) as i:
                        step(b, i)
                else:
                    pool.wait_ge(s_dtu, b + 1)
                    with pool.Fori(0, 2) as i:
                        step(b, i)
                with pool.Fori(2, STEPS) as i:
                    step(b, i)
                if b + 1 < B:
                    prep_b(b + 1)

        @block.scalar
        def _(act):
            act.wait_ge(s_wld, 16 * 8)
            act.activation(negA[:], negA[:], ACT.Exp).then_inc(s_negA0, 1)
            act.wait_ge(s_ln, LN_VAR)
            act.activation(rstd[:], rstd[:], ACT.Sqrt).then_inc(s_sd, 1)
            act.wait_ge(s_pad, 1)

            def prep_a(b):
                p = b % 2
                if b == 0:
                    act.wait_ge(s_ln, LN_READY)
                for et in range(E4):
                    act.wait_ge(s_xin, E4 * b + et + 1)
                    if b >= 1:
                        act.wait_ge(s_cv, 4 * (E4 * (b - 1) + et + 1))
                    act.activation(xpad[:, et, 3:3 + L], pp[et % 2][:], ACT.Copy).then_inc(s_xc, 1)
                if b >= 2:
                    act.wait_ge(s_g, E4 * (b - 1))
                for t in range(TB):
                    n = b * TB + t
                    act.activation(gate[:, p, t], x_sb[:, n], ACT.Silu, scale=rstd[:, n:n + 1],
                                   bias=nmr[:, n:n + 1]).then_inc(s_gate, 1)
                if b >= 2:
                    act.wait_ge(s_y0, E4 * (b - 1))
                for et in range(E4):
                    act.wait_ge(s_cv, 4 * (E4 * b + et + 1))
                    act.activation(u[:, p, et], conv[:, et], ACT.Silu, bias=conv_b[:, et:et + 1]).then_inc(s_u, 1)
                act.wait_ge(s_xd, b + 1)
                if b >= 2:
                    act.wait_ge(s_bcst, 16 * (b - 1))
                    act.wait_ge(s_dtp, E4 * (b - 1))
                act.activation(xdbl[:, p, :], px[0:R + 2 * NS, :], ACT.Copy).then_inc(s_xdc, 1)

            def prep_b(b):
                for et in range(E4):
                    act.wait_ge(s_dtp, E4 * b + et + 1)
                    if b >= 1 and et == 0:
                        act.wait_ge(s_m, b)
                        act.wait_ge(s_q, 4 * b)
                    act.activation(ee[:, et], pp[et % 2][:], ACT.Abs, bias=dt_b[:, et:et + 1]).then_inc(s_abs, 1)
                act.wait_ge(s_abs, E4 * (b + 1))
                act.activation(ee[:], ee[:], ACT.Exp, scale=-1.0).then_inc(s_e, 1)
                act.wait_ge(s_e, b + 1)
                if b >= 1:
                    act.wait_ge(s_dt, b)
                act.activation(ll[:], ee[:], ACT.Ln, bias=1.0).then_inc(s_l, 1)

            def step(b, i):
                for k in range(2):
                    for et in range(E4):
                        n = (i + b * STEPS) * JOBS + k * E4 + et
                        if not (b == 0 and isinstance(i, int) and i == 0 and k == 0 and et < 2):
                            act.wait_ge(s_scan, n - 1)
                        for m in range(2):
                            last = act.activation(dA[:, et % 2, m, 1:L], dt[:, b % 2, et, 1:L], ACT.Exp,
                                                  scale=negA[:, bass.ds(i * 4 + (et * NS + k * 2 + m), 1)])
                        last.then_inc(s_dA, 1)

            prep_a(0)
            prep_b(0)
            act.wait_ge(s_negA, 1)
            act.wait_ge(s_dz, 1)
            for b in range(B):
                act.wait_ge(s_dt, b + 1)
                if b == 0:
                    step(b, 0)
                    with act.Fori(1, 2) as i:
                        step(b, i)
                else:
                    with act.Fori(0, 2) as i:
                        step(b, i)
                if b + 1 < B:
                    prep_a(b + 1)
                with act.Fori(2, STEPS) as i:
                    step(b, i)
                if b + 1 < B:
                    prep_b(b + 1)

        @block.vector
        def _(dve):
            for t in range(NT):
                dve.bn_stats(stats[:, t], x_sb[:, t]).then_inc(s_ln, 1)
            dve.wait_ge(s_ln, NT)
            for t in range(NT):
                dve.bn_aggr(mv[:, t], stats[:, t]).then_inc(s_ln, 1)
            dve.wait_ge(s_ln, 2 * NT)
            dve.tensor_scalar(rstd[:], mv[:, :, 1], EPS, None, ALU.add).then_inc(s_ln, 1)
            dve.wait_ge(s_sd, 1)
            dve.reciprocal(rstd[:], rstd[:]).then_inc(s_ln, 1)
            dve.wait_ge(s_ln, LN_RSTD)
            dve.scalar_tensor_tensor(nmr[:], mv[:, :, 0], -1.0, rstd[:], ALU.mult, ALU.mult).then_inc(s_ln, 1)
            dve.wait_ge(s_negA0, 1)
            dve.tensor_scalar(negA[:], negA[:], -1.0, None, ALU.mult).then_inc(s_negA, 1)
            for et in range(E4):
                dve.tensor_scalar(diagD[:, et], ident[:], Dcol[:, et:et + 1], None, ALU.mult).then_inc(s_diag, 1)

            def prep_a(b):
                for et in range(E4):
                    dve.wait_ge(s_xc, E4 * b + et + 1)
                    if b >= 1 and et == 0:
                        dve.wait_ge(s_pick, b)
                    for k in range(4):
                        if k == 0:
                            dve.tensor_scalar(conv[:, et], xpad[:, et, 0:L], conv_w[:, et, 0:1], None, ALU.mult)\
                                .then_inc(s_cv, 1)
                        else:
                            dve.wait_ge(s_cv, 4 * (E4 * b + et) + k)
                            dve.scalar_tensor_tensor(conv[:, et], xpad[:, et, k:k + L], conv_w[:, et, k:k + 1],
                                                     conv[:, et], ALU.mult, ALU.add).then_inc(s_cv, 1)

            def prep_b(b):
                p = b % 2
                for et in range(E4):
                    dve.wait_ge(s_abs, E4 * b + et + 1)
                    dve.tensor_scalar(dt[:, p, et], pp[et % 2][:], dt_b[:, et:et + 1], 0.0, ALU.add, ALU.max)\
                        .then_inc(s_rel, 1)
                dve.wait_ge(s_e, b + 1)
                dve.wait_ge(s_u, E4 * (b + 1))
                dve.tensor_scalar(conv[:], ee[:], -0.25, None, ALU.mult).then_inc(s_q, 1)
                for k, c in enumerate((1.0 / 3, -0.5, 1.0)):
                    dve.wait_ge(s_q, 4 * b + k + 1)
                    dve.scalar_tensor_tensor(conv[:], conv[:], c, ee[:], ALU.add, ALU.mult).then_inc(s_q, 1)
                dve.wait_ge(s_q, 4 * b + 4)
                dve.wait_ge(s_m, b + 1)
                dve.wait_ge(s_l, b + 1)
                dve.copy_predicated(ll[:], small[:], conv[:]).then_inc(s_pick, 1)

            def scan(b, i, k, et):
                n = (i + b * STEPS) * JOBS + k * E4 + et
                dve.wait_ge(s_dA, n + 1)
                dve.wait_ge(s_dbu, n + 1)
                if not (b == 0 and isinstance(i, int) and i == 0 and k == 0 and et < 2):
                    dve.wait_ge(s_hc, n - 1)
                dve.tensor_tensor_scan(hs[:, et % 2].rearrange("p s l -> p (s l)"),
                                       dA[:, et % 2].rearrange("p s l -> p (s l)"),
                                       dBu[:, et % 2].rearrange("p s l -> p (s l)"), 0.0, ALU.mult, ALU.add)\
                    .then_inc(s_scan, 1)

            def terms(b, i, k, et):
                n = (i + b * STEPS) * JOBS + k * E4 + et
                dve.wait_ge(s_scan, n + 1)
                if not (b == 0 and isinstance(i, int) and i == 0 and k == 0 and et < 2):
                    dve.wait_ge(s_y, n - 1)
                dve.tensor_tensor(hc[:, et % 2], hs[:, et % 2], bch[:, k, 1], ALU.mult).then_inc(s_hc, 1)

            def step(b, i):
                jobs = [(k, et) for k in range(2) for et in range(E4)]
                scan(b, i, *jobs[0])
                for m in range(1, JOBS):
                    scan(b, i, *jobs[m])
                    terms(b, i, *jobs[m - 1])
                terms(b, i, *jobs[-1])

            def finish(b):
                for et in range(E4):
                    dve.wait_ge(s_y, (b + 1) * STEPS * JOBS - E4 + et + 1)
                    dve.wait_ge(s_gate, TB * (b + 1))
                    if E4 * b + et >= 2:
                        dve.wait_ge(s_t, E4 * b + et - 1)
                    dve.tensor_tensor(ty[:, et % 2], py[et][:], gate[:, b % 2, et], ALU.mult).then_inc(s_g, 1)
                    if et >= 1:
                        add(b, et - 1)
                add(b, E4 - 1)

            def add(b, et):
                dve.wait_ge(s_t, E4 * b + et + 1)
                xv = x_sb[:, b * TB:(b + 1) * TB, et * P:(et + 1) * P]
                dve.scalar_tensor_tensor(xv, pt[:], tg[:, 0:1], xv, ALU.mult, ALU.add).then_inc(s_add, 1)

            prep_a(0)
            prep_b(0)
            for b in range(B):
                if b == 0:
                    step(b, 0)
                    with dve.Fori(1, 2) as i:
                        step(b, i)
                else:
                    with dve.Fori(0, 2) as i:
                        step(b, i)
                if b + 1 < B:
                    prep_a(b + 1)
                with dve.Fori(2, STEPS) as i:
                    step(b, i)
                finish(b)
                if b + 1 < B:
                    prep_b(b + 1)

        @block.tensor
        def _(pe):
            pe.wait_ge(s_wld, 16 * 8)

            def prep_a(b):
                pe.wait_ge(s_ctx[b % 2], 16 * (b // 2 + 1))
                for et in range(E4):
                    if b == 0 and et >= 2:
                        pe.wait_ge(s_xc, et - 1)
                    if b >= 1:
                        if et < 2:
                            pe.wait_ge(s_abs, E4 * b)
                            pe.wait_ge(s_rel, E4 * b)
                        else:
                            pe.wait_ge(s_xc, E4 * b + et - 1)
                    for k in range(KC):
                        last = pe.matmul(pp[et % 2][:], w_in[:, k, et * P:(et + 1) * P], ctxT[:, b % 2, k],
                                         start=(k == 0), stop=(k == KC - 1))
                    last.then_inc(s_xin, 1)
                for et in range(E4):
                    pe.wait_ge(s_u, E4 * b + et + 1)
                    if b >= 1 and et == 0:
                        pe.wait_ge(s_xdc, b)
                    last = pe.matmul(px[0:R + 2 * NS, :], w_xp[:, et], u[:, b % 2, et], start=(et == 0),
                                     stop=(et == E4 - 1))
                last.then_inc(s_xd, 1)

            def prep_b(b):
                pe.wait_ge(s_xdc, b + 1)
                for et in range(E4):
                    if et < 2:
                        pe.wait_ge(s_xc, E4 * (b + 1))
                    else:
                        pe.wait_ge(s_abs, E4 * b + et - 1)
                        pe.wait_ge(s_rel, E4 * b + et - 1)
                    pe.matmul(pp[et % 2][:], w_dt[:, et * P:(et + 1) * P], xdbl[0:R, b % 2, :], start=True,
                              stop=True).then_inc(s_dtp, 1)

            def step(b, i):
                for k in range(2):
                    for et in range(E4):
                        n = (i + b * STEPS) * JOBS + k * E4 + et
                        pe.wait_ge(s_hc, n + 1)
                        for m in range(2):
                            last = pe.matmul(py[et][:], ident[:], hc[:, et % 2, m], start=False, stop=True,
                                             skip_group_check=True)
                        last.then_inc(s_y, 1)

            prep_a(0)
            prep_b(0)
            pe.wait_ge(s_diag, E4)
            for b in range(B):
                for et in range(E4):
                    if b >= 1:
                        pe.wait_ge(s_g, E4 * (b - 1) + et + 1)
                    pe.matmul(py[et][:], diagD[:, et], u[:, b % 2, et], start=True, stop=True,
                              skip_group_check=True).then_inc(s_y0, 1)
                with pe.Fori(0, 2) as i:
                    step(b, i)
                if b + 1 < B:
                    prep_a(b + 1)
                with pe.Fori(2, STEPS) as i:
                    step(b, i)
                for et in range(E4):
                    pe.wait_ge(s_g, E4 * b + et + 1)
                    if E4 * b + et >= 1:
                        pe.wait_ge(s_add, E4 * b + et)
                    for t in range(TB):
                        last = pe.transpose(pt[:, t, :], ty[:, et % 2, t * P:(t + 1) * P], ident[:])
                    last.then_inc(s_t, 1)
                if b + 1 < B:
                    prep_b(b + 1)


NE = 16
F = 256
KF = F // P
ST = 2 * NT + NE - 1
RING = 4


def moe(nc, x_sb, ident, tg, a, xg_dram, yg_dram, s_zero):
    with ExitStack() as ctx:
        def sb(name, shape, dt=F32):
            return ctx.enter_context(nc.sbuf_tensor("e_" + name, shape, dt))

        def sem(name):
            return ctx.enter_context(nc.semaphore("e_" + name))

        xn = sb("xn", [P, NT, D])
        xnT = sb("xnT", [P, KD, T])
        stats = sb("stats", [P, NT, 6])
        mv = sb("mv", [P, NT, 2])
        rstd = sb("rstd", [P, NT])
        nmr = sb("nmr", [P, NT])
        w_gate = sb("w_gate", [P, KD, NE])
        bias = sb("bias", [P, NE])
        iota = sb("iota", [P, 64])
        lower = sb("lower", [P, P])
        tri = sb("tri", [P, 2, P], BF16)
        ws1 = sb("ws1", [P, KD, 2 * F])
        ws2 = sb("ws2", [P, KF, D])
        w1 = sb("w1", [P, RING, KD, 2 * F])
        w2 = sb("w2", [P, RING, KF, D])
        xg = sb("xg", [P, 2, D])
        xgT = sb("xgT", [P, 2, KD, P])
        sg = sb("sg", [P, 2, F])
        hm = sb("hm", [P, 2, F])
        hT = sb("hT", [P, 2, KF, P])
        yo = sb("yo", [P, 2, D])
        score = sb("score", [P, NT, NE])
        biased = sb("biased", [P, NT, NE])
        top8 = sb("top8", [P, NT, 8])
        idx8 = sb("idx8", [P, NT, 8], U32)
        idxf = sb("idxf", [P, NT, 2])
        onehot = sb("onehot", [P, 2, NT, NE])
        member = sb("member", [P, NT, NE], BF16)
        tot = sb("tot", [P, NT, NE])
        cum = sb("cum", [P, NT + 1, NE])
        cnt = sb("cnt", [P, 4, NE])
        cnti = sb("cnti", [P, 2, NE], I32)
        pos = sb("pos", [P, NT, NE])
        prod = sb("prod", [P, 4, NT, NE])
        slotf = sb("slotf", [P, 2, NT])
        slot = sb("slot", [P, 2, NT], U32)
        sk = sb("sk", [P, 2, NT])
        den = sb("den", [P, NT])
        wk = sb("wk", [P, 2, NT])
        over = sb("over", [P, ST + 1, NE])
        ejf = sb("ejf", [P, ST + 1])
        ej = sb("ej", [P, ST + 1], I32)
        ends = sb("ends", [P, NE], I32)
        yk = xn[:, 0:4].rearrange("p (t k) d -> p t k d", k=2)

        pxt = [ctx.enter_context(nc.psum_tensor(f"e_xt{i}", [P, KD, P], F32)) for i in range(2)]
        pgu = [ctx.enter_context(nc.psum_tensor(f"e_gu{i}", [P, 2 * F], F32)) for i in range(2)]
        pht = ctx.enter_context(nc.psum_tensor("e_ht", [P, 4, P], F32))
        pyo = [ctx.enter_context(nc.psum_tensor(f"e_y{i}", [P, D], F32)) for i in range(2)]
        prt = ctx.enter_context(nc.psum_tensor("e_rt", [P, 2, NT, NE], F32))

        s_w = sem("weights_loaded")
        s_ln = sem("ln_steps")
        s_sd = sem("ln_std")
        s_xn = sem("normalised")
        s_xt = sem("x_transposed")
        s_xtc = sem("x_transposed_copied")
        s_lg = sem("logits")
        s_sc = sem("scores")
        s_tri = sem("tri_ready")
        s_r = sem("routing_steps")
        s_cnt = sem("counted")
        s_slot = sem("slots_ready")
        s_ej = sem("tile_experts")
        s_sct = sem("scattered")
        s_gu = sem("up_done")
        s_sg = sem("silu_done")
        s_hm = sem("hidden_ready")
        s_ht = sem("hidden_transposed")
        s_htc = sem("hidden_copied")
        s_y = sem("down_done")
        s_yc = sem("down_copied")
        s_ld = [sem(f"tile_loaded{i}") for i in range(2)]
        s_wl = [sem(f"expert_loaded{i}") for i in range(RING)]
        s_wr = sem("experts_ready")
        s_yst = [sem(f"stored{i}") for i in range(2)]
        s_gat = [sem(f"gathered{i}") for i in range(2)]
        s_cmb = sem("combined")

        block = ctx.enter_context(nc.Block())

        @block.sync
        def _(sp):
            sp.dma_start(w_gate[:], a["gate_w"].rearrange("(k p) e -> p k e", p=P)).then_inc(s_w, 16)
            sp.dma_start(bias[:], a["ex_bias"].partition_broadcast(P)).then_inc(s_w, 16)
            sp.dma_start(iota[:], a["iota"].partition_broadcast(P)).then_inc(s_w, 16)
            sp.dma_start(lower[:], a["lower"]).then_inc(s_w, 16)
            sp.dma_start(ws1[:, :, 0:F], a["sh_gate"].rearrange("(k p) e -> p k e", p=P)).then_inc(s_w, 16)
            sp.dma_start(ws1[:, :, F:2 * F], a["sh_up"].rearrange("(k p) e -> p k e", p=P)).then_inc(s_w, 16)
            sp.dma_start(ws2[:], a["sh_down"].rearrange("(k p) e -> p k e", p=P)).then_inc(s_w, 16)

            def load_expert(e, r):
                sp.dma_start(w1[:, r], a["ex_gu"][bass.ds(e, 1)].rearrange("o (k p) f -> p (o k) f", p=P))\
                    .then_inc(s_wl[r], 16)
                sp.dma_start(w2[:, r], a["ex_dn"][bass.ds(e, 1)].rearrange("o (k p) f -> p (o k) f", p=P))\
                    .then_inc(s_wl[r], 16)

            def ready(r, turn):
                sp.wait_ge(s_wl[r], turn * 32)
                sp.sem_inc(s_wr, 1)

            for r in range(RING):
                load_expert(r, r)
            for r in range(RING):
                ready(r, 1)
            sp.wait_ge(s_ej, 2)
            with sp.Fori(1, NE // RING) as i:
                for r in range(RING):
                    sp.wait_ge(s_y, sp.value_load(ends[0:1, bass.ds(i * RING + (r - RING), 1)], min_val=NT,
                                                  max_val=NT + ST))
                    load_expert(i * RING + r, r)
                    if r >= 1:
                        ready(r - 1, i + 1)
                ready(RING - 1, i + 1)

        @block.gpsimd
        def _(pool):
            pool.wait_ge(s_slot, 1)
            pool.wait_ge(s_zero, 16)
            for k in range(2):
                for t in range(NT):
                    pool.indirect_dma_start(xg_dram.rearrange("j p d -> (j p) d"),
                                            bass.IndirectOffsetOnAxis(ap=slot[:, k, t:t + 1], axis=0),
                                            xn[:, t, :], None).then_inc(s_sct, 16)

            def store(j, par):
                pool.wait_ge(s_yc, j + 1 + NT)
                pool.dma_start(yg_dram[bass.ds(j, 1)].rearrange("o p d -> (o p) d"), yo[:, par])\
                    .then_inc(s_yst[par], 16)

            with pool.Fori(0, ST // 2) as i:
                for par in range(2):
                    store(i * 2 + par, par)
            store(ST - 1, 0)
            pool.wait_ge(s_yst[0], 16 * (ST - ST // 2))
            pool.wait_ge(s_yst[1], 16 * (ST // 2))
            for t in range(NT):
                if t >= 2:
                    pool.wait_ge(s_cmb, 2 * (t - 1))
                for k in range(2):
                    pool.indirect_dma_start(yk[:, t % 2, k, :], None, yg_dram.rearrange("j p d -> (j p) d"),
                                            bass.IndirectOffsetOnAxis(ap=slot[:, k, t:t + 1], axis=0))\
                        .then_inc(s_gat[t % 2], 16)

        def silu_step(act, n, par):
            act.wait_ge(s_gu, n + 1)
            act.activation(sg[:, par], pgu[par][:, 0:F], ACT.Silu).then_inc(s_sg, 1)

        @block.scalar
        def _(act):
            act.wait_ge(s_ln, LN_VAR)
            act.activation(rstd[:], rstd[:], ACT.Sqrt).then_inc(s_sd, 1)
            act.wait_ge(s_ln, LN_READY)
            for t in range(NT):
                act.activation(xn[:, t], x_sb[:, t], ACT.Identity, scale=rstd[:, t:t + 1], bias=nmr[:, t:t + 1])\
                    .then_inc(s_xn, 1)
            act.wait_ge(s_lg, 1)
            act.activation(score[:], prt[:, 0], ACT.Sigmoid).then_inc(s_sc, 1)
            for t in range(NT):
                if t >= 2:
                    act.wait_ge(s_hm, t - 1)
                silu_step(act, t, t % 2)

            def load(j, par):
                act.dma_start(xg[:, par], xg_dram[bass.ds(j, 1)].rearrange("o p d -> (o p) d"))\
                    .then_inc(s_ld[par], 16)

            def tile(j, par, more=True):
                act.wait_ge(s_xt, NT + 1 + j)
                act.wait_ge(s_gu, NT + j - 1)
                act.activation(xgT[:, par], pxt[par][:], ACT.Copy).then_inc(s_xtc, 1)
                if more:
                    load(j + 2, par)

            def silu(j, par):
                act.wait_ge(s_hm, NT + j - 1)
                silu_step(act, NT + j, par)

            act.wait_ge(s_sct, 16 * 2 * NT)
            load(0, 0)
            load(1, 1)
            tile(0, 0)
            silu(0, 0)
            tile(1, 1)
            with act.Fori(0, (ST - 5) // 2) as i:
                for m in range(2):
                    silu(i * 2 + (m + 1), (m + 1) % 2)
                    tile(i * 2 + (m + 2), m)
            for j in range(ST - 3, ST):
                silu(j - 1, (j - 1) % 2)
                tile(j, j % 2, more=(j < ST - 2))
            silu(ST - 1, 0)

        @block.vector
        def _(dve):
            for t in range(NT):
                dve.bn_stats(stats[:, t], x_sb[:, t]).then_inc(s_ln, 1)
            dve.wait_ge(s_ln, NT)
            for t in range(NT):
                dve.bn_aggr(mv[:, t], stats[:, t]).then_inc(s_ln, 1)
            dve.wait_ge(s_ln, 2 * NT)
            dve.tensor_scalar(rstd[:], mv[:, :, 1], EPS, None, ALU.add).then_inc(s_ln, 1)
            dve.wait_ge(s_sd, 1)
            dve.reciprocal(rstd[:], rstd[:]).then_inc(s_ln, 1)
            dve.wait_ge(s_ln, LN_RSTD)
            dve.scalar_tensor_tensor(nmr[:], mv[:, :, 0], -1.0, rstd[:], ALU.mult, ALU.mult).then_inc(s_ln, 1)
            dve.wait_ge(s_w, 16 * 7)
            dve.tensor_copy(tri[:, 0], lower[:]).then_inc(s_tri, 1)
            dve.memset(tri[:, 1], 1.0).then_inc(s_tri, 1)
            for t in range(NT):
                dve.wait_ge(s_xt, t + 1)
                dve.tensor_copy(xnT[:, :, t * P:(t + 1) * P], pxt[t % 2][:]).then_inc(s_xtc, 1)

            step = [0]

            def done(ins):
                step[0] += 1
                ins.then_inc(s_r, 1)
                dve.wait_ge(s_r, step[0])

            dve.wait_ge(s_sc, 1)
            done(dve.tensor_tensor(biased[:], score[:], bias[:].unsqueeze(1).broadcast_to([P, NT, NE]), ALU.add))
            for t in range(NT):
                last = dve.max(top8[:, t], biased[:, t])
            done(last)
            for t in range(NT):
                last = dve.max_index(idx8[:, t], top8[:, t], biased[:, t])
            done(last)
            done(dve.tensor_copy(idxf[:], idx8[:, :, 0:2]))
            for k in range(2):
                last = dve.tensor_tensor(onehot[:, k], iota[:, 0:NE].unsqueeze(1).broadcast_to([P, NT, NE]),
                                         idxf[:, :, k:k + 1].broadcast_to([P, NT, NE]), ALU.is_equal)
            done(last)
            done(dve.tensor_tensor(member[:], onehot[:, 0], onehot[:, 1], ALU.add))
            dve.wait_ge(s_cnt, 1)
            dve.memset(cum[:, 0], 0.0)
            done(dve.tensor_copy(tot[:], prt[:, 1]))
            for t in range(NT):
                done(dve.tensor_tensor(cum[:, t + 1], cum[:, t], tot[:, t], ALU.add))
            done(dve.tensor_scalar(cnti[:, 0], cum[:, NT], float(P - 1), None, ALU.add))
            done(dve.tensor_scalar(cnti[:, 1], cnti[:, 0], 7, None, ALU.logical_shift_right))
            done(dve.tensor_copy(cnt[:, 0], cnti[:, 1]))
            done(dve.memset(cnt[:, 3], 1.0))
            done(dve.tensor_tensor_scan(cnt[:, 1], cnt[:, 3], cnt[:, 0], 0.0, ALU.mult, ALU.add))
            done(dve.tensor_tensor(cnt[:, 2], cnt[:, 1], cnt[:, 0], ALU.subtract))
            done(dve.tensor_scalar(cnt[:, 2], cnt[:, 2], float(P), None, ALU.mult))
            done(dve.tensor_tensor(over[:], iota[:, 0:ST + 1].unsqueeze(2).broadcast_to([P, ST + 1, NE]),
                                   cnt[:, 1].unsqueeze(1).broadcast_to([P, ST + 1, NE]), ALU.is_ge))
            done(dve.tensor_reduce(ejf[:], over[:], AX.X, ALU.add))
            dve.tensor_scalar(ej[:], ejf[:], float(NE - 1), None, ALU.min).then_inc(s_ej, 1)
            dve.tensor_scalar(ends[:], cnt[:, 1], float(NT), None, ALU.add).then_inc(s_ej, 1)
            done(dve.tensor_tensor(pos[:], prt[:, 0], cum[:, 0:NT], ALU.add))
            done(dve.tensor_tensor(pos[:], pos[:], cnt[:, 2].unsqueeze(1).broadcast_to([P, NT, NE]), ALU.add))
            for k in range(2):
                dve.tensor_tensor(prod[:, k], onehot[:, k], pos[:], ALU.mult)
                last = dve.tensor_tensor(prod[:, 2 + k], onehot[:, k], score[:], ALU.mult)
            done(last)
            for k in range(2):
                dve.tensor_reduce(slotf[:, k], prod[:, k], AX.X, ALU.add)
                last = dve.tensor_reduce(sk[:, k], prod[:, 2 + k], AX.X, ALU.add)
            done(last)
            dve.tensor_copy(slot[:], slotf[:]).then_inc(s_slot, 1)
            done(dve.tensor_tensor(den[:], sk[:, 0], sk[:, 1], ALU.add))
            done(dve.tensor_scalar(den[:], den[:], 1e-20, None, ALU.add))
            done(dve.reciprocal(den[:], den[:]))
            for k in range(2):
                last = dve.scalar_tensor_tensor(wk[:, k], sk[:, k], tg[:, 0:1], den[:], ALU.mult, ALU.mult)
            done(last)

            def hidden(n, par):
                dve.wait_ge(s_sg, n + 1)
                if not (isinstance(n, int) and n < 2):
                    dve.wait_ge(s_ht, n - 1)
                dve.tensor_tensor(hm[:, par], sg[:, par], pgu[par][:, F:2 * F], ALU.mult).then_inc(s_hm, 1)

            def hidden_copy(n, par):
                dve.wait_ge(s_ht, n + 1)
                if not (isinstance(n, int) and n < 2):
                    dve.wait_ge(s_y, n - 1)
                dve.tensor_copy(hT[:, par], pht[:, 2 * par:2 * par + 2]).then_inc(s_htc, 1)

            def shared_out(t):
                dve.wait_ge(s_y, t + 1)
                dve.scalar_tensor_tensor(x_sb[:, t], pyo[t % 2][:], tg[:, 0:1], x_sb[:, t], ALU.mult, ALU.add)\
                    .then_inc(s_yc, 1)

            hidden(0, 0)
            for t in range(1, NT):
                hidden_copy(t - 1, (t - 1) % 2)
                hidden(t, t % 2)
                shared_out(t - 1)
            hidden_copy(NT - 1, 1)
            shared_out(NT - 1)

            def step_dve(i2, m, first=False):
                j = i2 + m
                hidden_copy(NT + j - 1, (m - 1) % 2)
                hidden(NT + j, m % 2)
                dve.wait_ge(s_y, NT + j)
                if not first:
                    dve.wait_ge(s_yst[(m - 1) % 2], i2 * 8 + ((m - 1) // 2) * 16)
                dve.tensor_copy(yo[:, (m - 1) % 2], pyo[(m - 1) % 2][:]).then_inc(s_yc, 1)

            hidden(NT, 0)
            step_dve(0, 1, True)
            step_dve(0, 2, True)
            with dve.Fori(1, ST // 2) as i:
                step_dve(i * 2, 1)
                step_dve(i * 2, 2)
            hidden_copy(NT + ST - 1, 0)
            dve.wait_ge(s_y, NT + ST)
            dve.wait_ge(s_yst[0], 16 * (ST // 2))
            dve.tensor_copy(yo[:, 0], pyo[0][:]).then_inc(s_yc, 1)
            for t in range(NT):
                dve.wait_ge(s_gat[t % 2], 32 * (t // 2 + 1))
                for k in range(2):
                    if k == 1:
                        dve.wait_ge(s_cmb, 2 * t + 1)
                    dve.scalar_tensor_tensor(x_sb[:, t], yk[:, t % 2, k], wk[:, k, t:t + 1], x_sb[:, t],
                                             ALU.mult, ALU.add).then_inc(s_cmb, 1)

        def logits_tile(pe, t):
            pe.wait_ge(s_xtc, t + 1)
            for k in range(KD):
                last = pe.matmul(prt[:, 0, t], xnT[:, k, t * P:(t + 1) * P], w_gate[:, k], start=(k == 0),
                                 stop=(k == KD - 1))
            return last

        @block.tensor
        def _(pe):
            pe.wait_ge(s_w, 16 * 7)
            for t in range(NT):
                pe.wait_ge(s_xn, t + 1)
                if t >= 2:
                    pe.wait_ge(s_xtc, t - 1)
                for k in range(KD):
                    last = pe.transpose(pxt[t % 2][:, k], xn[:, t, k * P:(k + 1) * P], ident[:])
                last.then_inc(s_xt, 1)
                if t >= 1:
                    logits_tile(pe, t - 1)
            logits_tile(pe, NT - 1).then_inc(s_lg, 1)

            def up(n, lhs, rhs, par):
                if not (isinstance(n, int) and n < 2):
                    pe.wait_ge(s_hm, n - 1)
                for k in range(KD):
                    last = pe.matmul(pgu[par][:], lhs(k), rhs(k), start=(k == 0), stop=(k == KD - 1))
                last.then_inc(s_gu, 1)

            def turn(n, par):
                pe.wait_ge(s_hm, n + 1)
                if not (isinstance(n, int) and n < 2):
                    pe.wait_ge(s_htc, n)
                for k in range(KF):
                    last = pe.transpose(pht[:, 2 * par + k], hm[:, par, k * P:(k + 1) * P], ident[:])
                last.then_inc(s_ht, 1)

            def down(n, rhs, par):
                pe.wait_ge(s_htc, n + 1)
                if not (isinstance(n, int) and n < 2):
                    pe.wait_ge(s_yc, n - 1)
                for k in range(KF):
                    last = pe.matmul(pyo[par][:], hT[:, par, k], rhs(k), start=(k == 0), stop=(k == KF - 1))
                last.then_inc(s_y, 1)

            def shared_up(t):
                up(t, lambda k: xnT[:, k, t * P:(t + 1) * P], lambda k: ws1[:, k], t % 2)

            pe.wait_ge(s_tri, 2)
            shared_up(0)
            shared_up(1)
            pe.wait_ge(s_r, 6)
            pe.matmul(prt[:, 0].rearrange("p t e -> p (t e)"), tri[:, 0], member[:].rearrange("p t e -> p (t e)"),
                      start=True, stop=True)
            pe.matmul(prt[:, 1].rearrange("p t e -> p (t e)"), tri[:, 1], member[:].rearrange("p t e -> p (t e)"),
                      start=True, stop=True, skip_group_check=True).then_inc(s_cnt, 1)
            turn(0, 0)
            for t in range(1, NT):
                if t >= 2:
                    shared_up(t)
                down(t - 1, lambda k: ws2[:, k], (t - 1) % 2)
                turn(t, t % 2)
            down(NT - 1, lambda k: ws2[:, k], 1)

            def fetch(j, par, nload):
                pe.wait_ge(s_ld[par], nload)
                if not (isinstance(j, int) and j < 2):
                    pe.wait_ge(s_xtc, NT + j - 1)
                for k in range(KD):
                    last = pe.transpose(pxt[par][:, k], xg[:, par, k * P:(k + 1) * P], ident[:])
                last.then_inc(s_xt, 1)

            def routed_up(j, par, e):
                pe.wait_ge(s_wr, e + 1)
                pe.wait_ge(s_xtc, NT + j + 1)
                up(NT + j, lambda k: xgT[:, par, k],
                   lambda k: w1[:, bass.ds(e % RING, 1), k].rearrange("p o f -> p (o f)"), par)

            def routed_down(j, par, e):
                down(NT + j, lambda k: w2[:, bass.ds(e % RING, 1), k].rearrange("p o f -> p (o f)"), par)

            def expert(j):
                return pe.value_load(ej[0:1, bass.ds(j, 1)], min_val=0, max_val=NE - 1)

            def step(i, m, before, e, last=False):
                turn(NT + i * 2 + (m - 1), (m - 1) % 2)
                routed_up(i * 2 + m, m % 2, e)
                if not last:
                    fetch(i * 2 + (m + 1), (m + 1) % 2, (i + (m + 1) // 2) * 16 + 16)
                routed_down(i * 2 + (m - 1), (m - 1) % 2, before)

            def pair(i, last=False):
                before, e1 = expert(i * 2), expert(i * 2 + 1)
                step(i, 1, before, e1)
                e2 = expert(i * 2 + 2)
                step(i, 2, e1, e2, last)

            fetch(0, 0, 16)
            pe.wait_ge(s_ej, 2)
            routed_up(0, 0, expert(0))
            fetch(1, 1, 16)
            with pe.Fori(0, (ST - 1) // 2 - 1) as i:
                pair(i)
            pair((ST - 1) // 2 - 1, last=True)
            e = expert(ST - 1)
            turn(NT + ST - 1, 0)
            routed_down(ST - 1, 0, e)


NH, HD = 32, 16
G4 = 4
NG = B * NH // G4
SCALE = HD ** -0.5
TURN_HIGH = 6.28125
TURN_LOW = float(2 * np.pi - TURN_HIGH)
TWO_PI = float(2 * np.pi)
SIN_MAX = 3.1415925
MAGIC = 12582912.0
VW = HD + 1


def attention_inputs(nc, x_sb, ident, a, qk_dram, v_dram):
    ITEMS = 2 * KD
    N = B * ITEMS
    with ExitStack() as ctx:
        def sb(name, shape, dt=F32):
            return ctx.enter_context(nc.sbuf_tensor("q_" + name, shape, dt))

        def sem(name):
            return ctx.enter_context(nc.semaphore("q_" + name))

        stats = sb("stats", [P, NT, 6])
        mv = sb("mv", [P, NT, 2])
        rstd = sb("rstd", [P, NT])
        nmr = sb("nmr", [P, NT])
        xn = sb("xn", [P, 2, D])
        xnT = sb("xnT", [P, KD, T])
        ctxT = sb("ctxT", [P, KC, T])
        wq = sb("wq", [P, KD, D])
        wkv = sb("wkv", [P, KC, 2 * D])
        posT = sb("posT", [2, T])
        freq = sb("freq", [2, P])
        swap = sb("swap", [P, P])
        sign = sb("sign", [P, 1])
        ang = sb("ang", [P, 2, T])
        turns = sb("turns", [P, 2, T])
        qs = sb("qs", [P, 4, L])
        t1 = sb("t1", [P, 4, L])
        t2 = sb("t2", [P, 4, L])
        qr = sb("qr", [P, 4, L])
        r1 = sb("r1", [P, 4, L])
        parts = sb("parts", [P, 4, 3, L], BF16)
        va = sb("va", [P, 2, NH, VW])

        pxt = [ctx.enter_context(nc.psum_tensor(f"q_xt{i}", [P, KD, P], F32)) for i in range(2)]
        pq = [ctx.enter_context(nc.psum_tensor(f"q_q{i}", [P, L], F32)) for i in range(2)]
        pw = [ctx.enter_context(nc.psum_tensor(f"q_w{i}", [P, L], F32)) for i in range(2)]
        pv = [ctx.enter_context(nc.psum_tensor(f"q_v{i}", [P, NH, HD], F32)) for i in range(2)]

        s_w = sem("weights_loaded")
        s_ln = sem("ln_steps")
        s_sd = sem("ln_std")
        s_xn = sem("normalised")
        s_xt = sem("x_transposed")
        s_xtc = sem("x_transposed_copied")
        s_ang = sem("angles")
        s_ar = sem("angles_read")
        s_a = sem("angle_steps")
        s_sin = sem("sines")
        s_tab = sem("tables_ready")
        s_one = sem("ones_set")
        s_vm = sem("v_done")
        s_vc = sem("v_copied")
        s_vs = [sem(f"v_stored{i}") for i in range(2)]
        s_qm = sem("projected")
        s_qc = sem("projection_copied")
        s_sw = sem("swapped")
        s_t1 = sem("cos_term")
        s_t2 = sem("sin_term")
        s_qr = sem("rotated")
        s_p1 = sem("part1")
        s_r1 = sem("rest1")
        s_p2 = sem("part2")
        s_p3 = sem("part3")
        s_ps = [sem(f"parts_stored{i}") for i in range(4)]

        block = ctx.enter_context(nc.Block())

        def late(n, k):
            return not isinstance(n, int) or n >= k

        @block.sync
        def _(sp):
            sp.dma_start(posT[:], a["posT"]).then_inc(s_w, 16)
            sp.dma_start(freq[:], a["freq"]).then_inc(s_w, 16)
            sp.dma_start(swap[:], a["swap"]).then_inc(s_w, 16)
            sp.dma_start(sign[:], a["sign"]).then_inc(s_w, 16)
            sp.dma_start(ctxT[:], a["ctxT"].rearrange("(k p) t -> p k t", p=P)).then_inc(s_w, 16)
            sp.dma_start(wkv[:], a["wkv"].rearrange("(k p) e -> p k e", p=P)).then_inc(s_w, 16)
            sp.dma_start(wq[:], a["wq"].rearrange("(k p) e -> p k e", p=P)).then_inc(s_w, 16)
            for t in range(NT):
                sp.wait_ge(s_vc, t + 1)
                sp.dma_start(v_dram[(t // TB) * 8:(t // TB + 1) * 8, :, t % TB, :].rearrange("g p c -> p g c"),
                             va[:, t % 2].rearrange("p (g h) c -> p g (h c)", g=8)).then_inc(s_vs[t % 2], 16)

            def store(i, m):
                n = i * ITEMS + m
                sp.wait_ge(s_p3, n + 1)
                dst = qk_dram[m % 2, :, bass.ds(i, 1), m // 2].rearrange("a o p t -> p (a o) t")
                sp.dma_start(dst, parts[:, m % 4]).then_inc(s_ps[m % 4], 16)

            with sp.Fori(0, B) as i:
                for m in range(ITEMS):
                    store(i, m)
            for r in range(4):
                sp.wait_ge(s_ps[r], 16 * N // 4)
            for r in range(2):
                sp.wait_ge(s_vs[r], 16 * NT // 2)

        def run(eng, steps, lag):
            for m in range(ITEMS):
                steps(0, m)
            with eng.Fori(1, B) as i:
                for m in range(ITEMS):
                    steps(i, m)
            for m in range(lag):
                steps(B, m)

        def at(i, m, k):
            if m >= k:
                return (i, m - k) if not isinstance(i, int) or i < B else None
            if isinstance(i, int) and i == 0:
                return None
            return i - 1, m - k + ITEMS

        @block.gpsimd
        def _(pool):
            pool.memset(va[:, :, :, HD:VW], 1.0).then_inc(s_one, 1)

            def steps(i, m):
                if it := at(i, m, 1):
                    n, r = it[0] * ITEMS + it[1], it[1] % 4
                    pool.wait_ge(s_t2, n + 1)
                    if late(n, 4):
                        pool.wait_ge(s_p1, n - 3)
                    pool.tensor_tensor(qr[:, r], t1[:, r], t2[:, r], ALU.add).then_inc(s_qr, 1)
                    pool.wait_ge(s_p1, n + 1)
                    if late(n, 4):
                        pool.wait_ge(s_p3, n - 3)
                    pool.tensor_tensor(r1[:, r], qr[:, r], parts[:, r, 0], ALU.subtract).then_inc(s_r1, 1)
                if it := at(i, m, 2):
                    n, r = it[0] * ITEMS + it[1], it[1] % 4
                    pool.wait_ge(s_p2, n + 1)
                    pool.tensor_tensor(parts[:, r, 2], r1[:, r], parts[:, r, 1], ALU.subtract).then_inc(s_p3, 1)

            run(pool, steps, 2)

        @block.scalar
        def _(act):
            act.wait_ge(s_ln, LN_VAR)
            act.activation(rstd[:], rstd[:], ACT.Sqrt).then_inc(s_sd, 1)
            act.wait_ge(s_one, 1)
            for t in range(NT):
                act.wait_ge(s_vm, t + 1)
                if t >= 2:
                    act.wait_ge(s_vs[t % 2], 16 * (t // 2))
                act.activation(va[:, t % 2, :, 0:HD], pv[t % 2][:], ACT.Copy).then_inc(s_vc, 1)
            act.wait_ge(s_ln, LN_READY)
            for t in range(NT):
                if t >= 2:
                    act.wait_ge(s_xt, t - 1)
                act.activation(xn[:, t % 2], x_sb[:, t], ACT.Identity, scale=rstd[:, t:t + 1], bias=nmr[:, t:t + 1])\
                    .then_inc(s_xn, 1)
            act.wait_ge(s_a, 5)
            act.activation(ang[:], ang[:], ACT.Sin).then_inc(s_sin, 1)

            def steps(i, m):
                if at(i, m, 0):
                    n = i * ITEMS + m
                    act.wait_ge(s_qm, n + 1)
                    if late(n, 4):
                        act.wait_ge(s_sw, n - 3)
                        act.wait_ge(s_t1, n - 3)
                    act.activation(qs[:, m % 4], pq[m % 2][:], ACT.Copy, scale=SCALE if m % 2 == 0 else 1.0)\
                        .then_inc(s_qc, 1)
                if it := at(i, m, 1):
                    n, r = it[0] * ITEMS + it[1], it[1] % 4
                    act.wait_ge(s_qr, n + 1)
                    if late(n, 4):
                        act.wait_ge(s_ps[r], 16 * (it[0] * 2 + it[1] // 4))
                    act.activation(parts[:, r, 0], qr[:, r], ACT.Copy).then_inc(s_p1, 1)
                if it := at(i, m, 2):
                    n, r = it[0] * ITEMS + it[1], it[1] % 4
                    act.wait_ge(s_r1, n + 1)
                    act.activation(parts[:, r, 1], r1[:, r], ACT.Copy).then_inc(s_p2, 1)

            run(act, steps, 2)

        @block.vector
        def _(dve):
            for t in range(NT):
                dve.bn_stats(stats[:, t], x_sb[:, t]).then_inc(s_ln, 1)
            dve.wait_ge(s_ln, NT)
            for t in range(NT):
                dve.bn_aggr(mv[:, t], stats[:, t]).then_inc(s_ln, 1)
            dve.wait_ge(s_ln, 2 * NT)
            dve.tensor_scalar(rstd[:], mv[:, :, 1], EPS, None, ALU.add).then_inc(s_ln, 1)
            dve.wait_ge(s_sd, 1)
            dve.reciprocal(rstd[:], rstd[:]).then_inc(s_ln, 1)
            dve.wait_ge(s_ln, LN_RSTD)
            dve.scalar_tensor_tensor(nmr[:], mv[:, :, 0], -1.0, rstd[:], ALU.mult, ALU.mult).then_inc(s_ln, 1)
            for b in range(B):
                dve.wait_ge(s_ang, b + 1)
                cols = slice(b * L, (b + 1) * L)
                dve.tensor_copy(ang[:, 1, cols], pw[b % 2][:])
                dve.tensor_scalar(ang[:, 0, cols], pw[b % 2][:], float(np.pi / 2), None, ALU.add).then_inc(s_ar, 1)
            dve.wait_ge(s_ar, B)
            dve.tensor_scalar(turns[:], ang[:], 1.0 / TWO_PI, MAGIC, ALU.mult, ALU.add).then_inc(s_a, 1)
            dve.wait_ge(s_a, 1)
            dve.tensor_scalar(turns[:], turns[:], MAGIC, None, ALU.subtract).then_inc(s_a, 1)
            dve.wait_ge(s_a, 2)
            dve.scalar_tensor_tensor(ang[:], turns[:], -TURN_HIGH, ang[:], ALU.mult, ALU.add).then_inc(s_a, 1)
            dve.wait_ge(s_a, 3)
            dve.scalar_tensor_tensor(ang[:], turns[:], -TURN_LOW, ang[:], ALU.mult, ALU.add).then_inc(s_a, 1)
            dve.wait_ge(s_a, 4)
            dve.tensor_scalar(ang[:], ang[:], SIN_MAX, -SIN_MAX, ALU.min, ALU.max).then_inc(s_a, 1)
            for t in range(NT):
                dve.wait_ge(s_xt, t + 1)
                dve.tensor_copy(xnT[:, :, t * P:(t + 1) * P], pxt[t % 2][:]).then_inc(s_xtc, 1)
            dve.wait_ge(s_sin, 1)
            dve.tensor_scalar(ang[:, 1], ang[:, 1], sign[:, 0:1], None, ALU.mult).then_inc(s_tab, 1)
            dve.wait_ge(s_tab, 1)

            def steps(i, m):
                if it := at(i, m, 0):
                    n = i * ITEMS + m
                    dve.wait_ge(s_qc, n + 1)
                    if late(n, 4):
                        dve.wait_ge(s_qr, n - 3)
                    dve.tensor_tensor(t1[:, m % 4], qs[:, m % 4], ang[:, 0, bass.ds(i * L, L)], ALU.mult)\
                        .then_inc(s_t1, 1)
                if it := at(i, m, 1):
                    n, r = it[0] * ITEMS + it[1], it[1] % 4
                    dve.wait_ge(s_sw, n + 1)
                    dve.tensor_tensor(t2[:, r], pw[r % 2][:], ang[:, 1, bass.ds(it[0] * L, L)], ALU.mult)\
                        .then_inc(s_t2, 1)

            run(dve, steps, 1)

        @block.tensor
        def _(pe):
            pe.wait_ge(s_w, 16 * 7)
            for b in range(B):
                if b >= 2:
                    pe.wait_ge(s_ar, b - 1)
                pe.matmul(pw[b % 2][:], freq[:], posT[:, b * L:(b + 1) * L], start=True, stop=True).then_inc(s_ang, 1)
            for t in range(NT):
                if t >= 2:
                    pe.wait_ge(s_vc, t - 1)
                for k in range(KC):
                    last = pe.matmul(pv[t % 2][:].rearrange("p h d -> p (h d)"), ctxT[:, k, t * P:(t + 1) * P],
                                     wkv[:, k, D:2 * D], start=(k == 0), stop=(k == KC - 1))
                last.then_inc(s_vm, 1)
            for t in range(NT):
                pe.wait_ge(s_xn, t + 1)
                if t >= 2:
                    pe.wait_ge(s_xtc, t - 1)
                for k in range(KD):
                    last = pe.transpose(pxt[t % 2][:, k], xn[:, t % 2, k * P:(k + 1) * P], ident[:])
                last.then_inc(s_xt, 1)
            pe.wait_ge(s_xtc, NT)
            pe.wait_ge(s_tab, 1)

            def steps(i, m):
                if at(i, m, 0):
                    n = i * ITEMS + m
                    ft = slice(m // 2 * P, (m // 2 + 1) * P)
                    if late(n, 2):
                        pe.wait_ge(s_qc, n - 1)
                    w, src, kn = (wq, xnT, KD) if m % 2 == 0 else (wkv, ctxT, KC)
                    for k in range(kn):
                        last = pe.matmul(pq[m % 2][:], w[:, k, ft], src[:, k, bass.ds(i * L, L)], start=(k == 0),
                                         stop=(k == kn - 1))
                    last.then_inc(s_qm, 1)
                if it := at(i, m, 1):
                    n, r = it[0] * ITEMS + it[1], it[1] % 4
                    pe.wait_ge(s_qc, n + 1)
                    if late(n, 2):
                        pe.wait_ge(s_t2, n - 1)
                    pe.matmul(pw[r % 2][:], swap[:], qs[:, r], start=True, stop=True).then_inc(s_sw, 1)

            run(pe, steps, 1)


Q_PART = (0, 0, 1, 1, 0, 2)
K_PART = (0, 1, 0, 1, 2, 0)
KR = HD * len(Q_PART)
KM = KR + 3


def attention(nc, ident, identb, a, qk_dram, v_dram, m_dram, at_dram):
    RG = 4
    with ExitStack() as ctx:
        def sb(name, shape, dt=F32):
            return ctx.enter_context(nc.sbuf_tensor("a_" + name, shape, dt))

        def sem(name):
            return ctx.enter_context(nc.semaphore("a_" + name))

        qs = sb("qs", [P, RG, G4, L], BF16)
        ks = sb("ks", [P, RG, G4, L], BF16)
        va = sb("va", [P, RG, TB, G4 * VW])
        pr = sb("pr", [P, 2, G4, TB, L])
        mx = sb("mx", [P, 2, G4 * TB])
        mr = sb("mr", [P, 2, G4 * TB])
        m3 = sb("m3", [P, 2, P // (G4 * TB), G4 * TB], BF16)
        mT = sb("mT", [3 * G4 * TB, 2, P], BF16)
        sel = sb("sel", [P, P])
        ones = sb("ones", [P, L])
        aT = sb("aT", [P, 2, L])
        rd = sb("rd", [P, 2, TB, G4])
        rw = sb("rw", [P, 2, TB, G4, 32])
        an = sb("an", [P, 2, L])

        psc = [ctx.enter_context(nc.psum_tensor(f"a_s{i}", [P, 2, L], F32)) for i in range(2)]
        pst = [ctx.enter_context(nc.psum_tensor(f"a_t{i}", [P, L], F32)) for i in range(2)]
        ppv = ctx.enter_context(nc.psum_tensor("a_pv", [P, L], F32))
        pmi = ctx.enter_context(nc.psum_tensor("a_mi", [P, L], F32))
        pmt = pmi[:].bitcast(BF16)[:, 0:P]

        s_sel = sem("sel_loaded")
        s_one = sem("ones_and_zeros_set")
        s_ld = [sem(f"operands_loaded{i}") for i in range(RG)]
        s_lv = [sem(f"values_loaded{i}") for i in range(RG)]
        s_s = sem("scores_by_query")
        s_mx = sem("maxima")
        s_n = sem("minus_max_parts")
        s_mt = sem("maxima_transposed")
        s_mc = sem("maxima_copied")
        s_md = sem("maxima_in_dram")
        s_mq = [sem(f"maxima_loaded{i}") for i in range(RG)]
        s_t = sem("scores_by_key")
        s_e = sem("exps")
        s_pv = sem("values_summed")
        s_pc = sem("values_copied")
        s_d = sem("denominators")
        s_r = sem("reciprocals")
        s_rw = sem("reciprocals_repeated")
        s_w = sem("reciprocals_spread")
        s_a = sem("normalised")
        s_o = [sem(f"stored{i}") for i in range(2)]

        block = ctx.enter_context(nc.Block())

        def no(i, r):
            return i * RG + r

        def after(i, r, k):
            return not isinstance(i, int) or no(i, r) >= k

        def run(eng, step):
            for r in range(RG):
                step(0, r)
            with eng.Fori(1, NG // RG - 1) as i:
                for r in range(RG):
                    step(i, r)
            for r in range(RG):
                step(NG // RG - 1, r)

        def inside(i, r):
            return not isinstance(i, int) or 0 <= no(i, r) < NG

        @block.sync
        def _(sp):
            sp.dma_start(sel[:], a["sel"]).then_inc(s_sel, 16)

            def load_qk(i, r):
                g = no(i, r)
                if after(i, r, RG):
                    sp.wait_ge(s_t, 16 * (g - RG + 1))
                for j, (qp, kp) in enumerate(zip(Q_PART, K_PART)):
                    rows = slice(j * HD, (j + 1) * HD)
                    for m, (dst, part) in enumerate(((qs, qp), (ks, kp))):
                        src = qk_dram[m, part].rearrange("b f (h d) t -> (b f h) d t", d=HD)[bass.ds(g * G4, G4)]
                        sp.dma_start(dst[rows, r % RG], src.rearrange("h d t -> d h t")).then_inc(s_ld[r % RG], 16)

            def load_v(i, r):
                g = no(i, r)
                if after(i, r, RG):
                    sp.wait_ge(s_pv, g - RG + 1)
                sp.dma_start(va[:, r % RG], v_dram[bass.ds(g, 1)].rearrange("o p k c -> p (o k) c"))\
                    .then_inc(s_lv[r % RG], 16)

            def maxima(i, r):
                g = no(i, r)
                sp.wait_ge(s_mc, g + 1)
                sp.dma_start(m_dram[bass.ds(g, 1)].rearrange("o r c -> (o r) c"), mT[:, r % 2]).then_inc(s_md, 16)
                sp.wait_ge(s_md, 16 * g + 16)
                sp.dma_start(qs[KR:KM, r % RG].rearrange("a h t -> a (h t)"),
                             m_dram[bass.ds(g, 1)].rearrange("o (a r) c -> (o a) (r c)", a=3))\
                    .then_inc(s_mq[r % RG], 16)

            def step(i, r):
                if inside(i, r + 3):
                    load_qk(i, r + 3)
                if inside(i, r + 1):
                    load_v(i, r + 1)
                    if after(i, r, 1):
                        maxima(i, r + 1)

            for g in range(3):
                load_qk(0, g)
            load_v(0, 0)
            for g in range(2):
                maxima(0, g)
            run(sp, step)

        @block.gpsimd
        def _(pool):
            pool.memset(ks[KR:P, :, :, :], 1.0).then_inc(s_one, 1)
            pool.wait_ge(s_one, 3)
            pool.memset(ones[:], 1.0).then_inc(s_one, 1)
            pool.wait_ge(s_one, 4)

            def repeat(i, r):
                g = no(i, r)
                pool.wait_ge(s_r, g + 1)
                if after(i, r, 2):
                    pool.wait_ge(s_w, g - 1)
                pool.tensor_tensor(rw[:, r % 2], rd[:, r % 2].unsqueeze(3).broadcast_to([P, TB, G4, 32]),
                                   ones[:].rearrange("p (t h c) -> p t h c", t=TB, h=G4), ALU.mult).then_inc(s_rw, 1)

            def step(i, r):
                g, r2 = no(i, r), r % 2
                repeat(i, r)
                pool.wait_ge(s_a, g + 1)
                for j in range(G4):
                    dst = at_dram.rearrange("b (h d) t -> (b h) d t", d=HD)[bass.ds(g * G4 + j, 1)]
                    pool.dma_start(dst.rearrange("o d t -> (o d) t"), an[32 * j:32 * j + HD, r2])\
                        .then_inc(s_o[r2], 16)

            run(pool, step)
            for r2 in range(2):
                pool.wait_ge(s_o[r2], 64 * NG // 2)

        @block.scalar
        def _(act):
            def copy_max(i, r):
                g = no(i, r)
                act.wait_ge(s_mt, g + 1)
                if after(i, r, 2):
                    act.wait_ge(s_md, 16 * (g - 1))
                act.activation(mT[:, r % 2], pmt[0:3 * G4 * TB], ACT.Copy).then_inc(s_mc, 1)

            def exps(i, r, h):
                g = no(i, r)
                for kt in range(TB):
                    act.wait_ge(s_t, g * 16 + (h * TB + kt + 1))
                    if h == 0 and kt == 0 and after(i, r, 2):
                        act.wait_ge(s_pv, g - 1)
                    act.activation(pr[:, r % 2, h, kt], pst[kt % 2][:], ACT.Exp).then_inc(s_e, 1)

            def copy_values(i, r):
                g = no(i, r)
                act.wait_ge(s_pv, g + 1)
                if after(i, r, 2):
                    act.wait_ge(s_d, g - 1)
                    act.wait_ge(s_a, g - 1)
                act.activation(aT[:, r % 2], ppv[:], ACT.Copy).then_inc(s_pc, 1)

            def step(i, r):
                for h in range(G4):
                    exps(i, r, h)
                    if h == 0 and after(i, r, 1) and inside(i, r + 1):
                        copy_max(i, r + 1)
                if after(i, r, 1):
                    copy_values(i, r - 1)

            copy_max(0, 0)
            copy_max(0, 1)
            run(act, step)
            copy_values(NG // RG, -1)

        @block.vector
        def _(dve):
            dve.memset(m3[:], 0.0).then_inc(s_one, 1)
            dve.memset(ppv[:], 0.0).then_inc(s_one, 1)
            dve.wait_ge(s_one, 3)

            def maxes(i, r, h):
                g = no(i, r)
                for c in range(2):
                    dve.wait_ge(s_s, g * 8 + (h * 2 + c + 1))
                    dve.tensor_reduce(mx[:, r % 2, h * TB + 2 * c:h * TB + 2 * c + 2], psc[c][:], AX.X, ALU.max)\
                        .then_inc(s_mx, 1)

            def split(i, r):
                g, r2 = no(i, r), r % 2
                dve.wait_ge(s_mx, g * 8 + 8)
                if after(i, r, 2):
                    dve.wait_ge(s_mt, g - 1)
                dve.tensor_scalar(m3[:, r2, 0], mx[:, r2], -1.0, None, ALU.mult).then_inc(s_n, 1)
                dve.wait_ge(s_n, g * 4 + 1)
                dve.scalar_tensor_tensor(mr[:, r2], mx[:, r2], -1.0, m3[:, r2, 0], ALU.mult, ALU.subtract)\
                    .then_inc(s_n, 1)
                dve.wait_ge(s_n, g * 4 + 2)
                dve.tensor_copy(m3[:, r2, 1], mr[:, r2]).then_inc(s_n, 1)
                dve.wait_ge(s_n, g * 4 + 3)
                dve.tensor_tensor(m3[:, r2, 2], mr[:, r2], m3[:, r2, 1], ALU.subtract).then_inc(s_n, 1)

            def recip(i, r):
                g = no(i, r)
                dve.wait_ge(s_d, g + 1)
                if after(i, r, 2):
                    dve.wait_ge(s_rw, g - 1)
                dve.reciprocal(rd[:, r % 2], pmi[:, 0:TB * G4].rearrange("p (t h) -> p t h", h=G4)).then_inc(s_r, 1)

            def normalise(i, r):
                g, r2 = no(i, r), r % 2
                dve.wait_ge(s_w, g + 1)
                if after(i, r, 2):
                    dve.wait_ge(s_o[r2], 64 * (i * (RG // 2) + r // 2))
                dve.tensor_tensor(an[:, r2], aT[:, r2], pmi[:], ALU.mult).then_inc(s_a, 1)

            def step(i, r):
                for h in range(G4):
                    if inside(i, r + 2):
                        maxes(i, r + 2, h)
                    if h == 1 and after(i, r, 2):
                        recip(i, r - 2)
                    if h == 2 and after(i, r, 2):
                        normalise(i, r - 2)
                if inside(i, r + 2):
                    split(i, r + 2)

            for g in range(2):
                for h in range(G4):
                    maxes(0, g, h)
                split(0, g)
            run(dve, step)
            for r in (-2, -1):
                recip(NG // RG, r)
                normalise(NG // RG, r)

        @block.tensor
        def _(pe):
            pe.wait_ge(s_sel, 16)
            pe.wait_ge(s_one, 4)

            def scores(i, r, h, c):
                g, ring = no(i, r), r % RG
                if h == 0 and c == 0:
                    pe.wait_ge(s_ld[ring], (i + r // RG) * 192 + 192)
                if h >= 1 or after(i, r, 1):
                    pe.wait_ge(s_mx, g * 8 + (h * 2 + c - 1))
                for q in range(2):
                    qt = 2 * c + q
                    last = pe.matmul(psc[c][:, q], qs[0:KR, ring, h, qt * P:(qt + 1) * P], ks[0:KR, ring, h],
                                     start=True, stop=True)
                last.then_inc(s_s, 1)

            def turn(i, r):
                g = no(i, r)
                pe.wait_ge(s_n, g * 4 + 4)
                if after(i, r, 1):
                    pe.wait_ge(s_mc, g)
                if after(i, r, 4):
                    pe.wait_ge(s_a, g - 3)
                pe.transpose(pmt, m3[:, r % 2].rearrange("p a c -> p (a c)"), identb[:]).then_inc(s_mt, 1)

            def by_key(i, r, h, kt):
                g, ring = no(i, r), r % RG
                if h == 0 and kt == 0:
                    pe.wait_ge(s_mq[ring], (i + r // RG) * 16 + 16)
                if h >= 1 or kt >= 2 or after(i, r, 1):
                    pe.wait_ge(s_e, g * 16 + (h * TB + kt - 1))
                pe.matmul(pst[kt % 2][:], ks[0:KM, ring, h, kt * P:(kt + 1) * P], qs[0:KM, ring, h],
                          start=True, stop=True).then_inc(s_t, 1)

            def values(i, r, kt):
                g, ring = no(i, r), r % RG
                if kt == 0:
                    pe.wait_ge(s_lv[ring], (i + r // RG) * 16 + 16)
                    pe.wait_ge(s_e, g * 16 + 16)
                    if after(i, r, 1):
                        pe.wait_ge(s_pc, g)
                for h in range(G4):
                    last = pe.matmul(ppv[32 * h:32 * h + VW], va[:, ring, kt, h * VW:(h + 1) * VW],
                                     pr[:, r % 2, h, kt], start=(kt == 0), stop=(kt == TB - 1),
                                     tile_position=(0, 32 * h))
                if kt == TB - 1:
                    last.then_inc(s_pv, 1)

            def denominators(i, r):
                g = no(i, r)
                pe.wait_ge(s_pc, g + 1)
                pe.wait_ge(s_mc, min(g + 4, NG) if isinstance(g, int) else g + 4)
                if after(i, r, 1):
                    pe.wait_ge(s_a, g)
                for t in range(TB):
                    last = pe.matmul(pmi[:, t * G4:(t + 1) * G4], aT[:, r % 2, t * P:(t + 1) * P],
                                     sel[:, 0:P:32], start=True, stop=True, skip_group_check=True)
                last.then_inc(s_d, 1)

            def spread(i, r):
                pe.wait_ge(s_rw, no(i, r) + 1)
                for t in range(TB):
                    last = pe.matmul(pmi[:, t * P:(t + 1) * P], rw[:, r % 2, t].rearrange("p h c -> p (h c)"),
                                     ident[:], start=True, stop=True, skip_group_check=True)
                last.then_inc(s_w, 1)

            def step(i, r):
                for h in range(G4):
                    for kt in range(TB):
                        by_key(i, r, h, kt)
                        if kt == 1 and after(i, r, 1):
                            values(i, r - 1, h)
                        if kt % 2 == 0 and inside(i, r + 2):
                            scores(i, r + 2, h, kt // 2)
                    if h == 0 and after(i, r, 1) and inside(i, r + 1):
                        turn(i, r + 1)
                    if h == 1 and after(i, r, 2):
                        denominators(i, r - 2)
                    if h == 2 and after(i, r, 2):
                        spread(i, r - 2)

            for g in range(2):
                for h in range(G4):
                    for c in range(2):
                        scores(0, g, h, c)
                turn(0, g)
            run(pe, step)
            for kt in range(TB):
                values(NG // RG, -1, kt)
            for r in (-2, -1):
                denominators(NG // RG, r)
                spread(NG // RG, r)


FF = 2048
KH = FF // P
QMAX, QMIN = 127.0, -128.0


def attention_out_and_ffn(nc, x_sb, ident, identb, tg, a, at_dram, out):
    with ExitStack() as ctx:
        def sb(name, shape, dt=F32):
            return ctx.enter_context(nc.sbuf_tensor("f_" + name, shape, dt))

        def sem(name):
            return ctx.enter_context(nc.semaphore("f_" + name))

        at = sb("at", [P, 2, KD, L])
        wo = sb("wo", [P, KD, D])
        bo = sb("bo", [P, D])
        w1 = sb("w1", [P, KD, FF])
        w2 = sb("w2", [P, KH, D])
        w1q = sb("w1q", [P, KD, FF], BF16)
        w2q = sb("w2q", [P, KH, D], BF16)
        ones = sb("ones", [P, P])
        ssq = sb("ssq", [P, 2])
        sd = sb("sd", [P, 2])
        rms = sb("rms", [P, 2])
        back = sb("back", [P, 2])
        stats = sb("stats", [P, NT, 6])
        mv = sb("mv", [P, NT, 2])
        rstd = sb("rstd", [P, NT])
        nmr = sb("nmr", [P, NT])
        xn = w1[:].rearrange("p k (t d) -> p (k t) d", d=D)
        am = sb("am", [P, NT + 2])
        c1r = sb("c1r", [P, 2])
        sc = sb("sc", [P, NT])
        magic = sb("magic", [P, 1])
        xq = w2[:].rearrange("p t d -> p (t d)").bitcast(BF16)[:, 0:NT * D].rearrange("p (t d) -> p t d", d=D)
        xqT = sb("xqT", [P, KD, T], BF16)
        h = sb("h", [P, 2, FF])
        am2 = sb("am2", [P, 2, 1])
        sc2 = sb("sc2", [P, 2, 1])
        c2 = sb("c2", [P, 2, 1])
        hq = sb("hq", [P, 2, FF], BF16)
        hqT = sb("hqT", [P, 2, KH, P], BF16)

        pup = [ctx.enter_context(nc.psum_tensor(f"f_u{i}", [P, 2, L], F32)) for i in range(2)]
        pht = ctx.enter_context(nc.psum_tensor("f_t", [P, KH, P], BF16))
        pdn = [ctx.enter_context(nc.psum_tensor(f"f_d{i}", [P, D], F32)) for i in range(2)]

        s_w = sem("weights_loaded")
        s_w1 = sem("w1_loaded")
        s_at = [sem(f"attention_loaded{i}") for i in range(2)]
        s_c = sem("constants_set")
        s_xb = sem("bias_added")
        s_po = sem("attention_projected")
        s_xa = sem("attention_added")
        s_sq = sem("squares_summed")
        s_ms = sem("mean_squares")
        s_sd = sem("weight_std")
        s_k = sem("scale_steps")
        s_q1 = sem("w1_rounding")
        s_q2 = sem("w2_rounding")
        s_ln = sem("ln_steps")
        s_lsd = sem("ln_std")
        s_xn = sem("normalised")
        s_am = sem("token_scale_steps")
        s_c1 = sem("first_scale")
        s_xs = sem("x_scaled")
        s_xq = sem("x_rounded")
        s_xt = sem("x_transposed")
        s_xtc = sem("x_transposed_copied")
        s_up = sem("up_done")
        s_h = sem("gelu_done")
        s_a2 = sem("hidden_scale_steps")
        s_v = sem("hidden_scaled")
        s_cl = sem("hidden_clamped")
        s_hq = sem("hidden_rounded")
        s_ht = sem("hidden_transposed")
        s_htc = sem("hidden_copied")
        s_dn = sem("down_done")
        s_x = sem("x_ready")
        s_o = sem("stored")

        block = ctx.enter_context(nc.Block())

        def run(eng, step, lag):
            for i in range(lag // 2 + 1):
                for r in range(2):
                    step(i, r)
            with eng.Fori(lag // 2 + 1, NT // 2) as i:
                for r in range(2):
                    step(i, r)
            for i in range(NT // 2, NT // 2 + lag // 2):
                for r in range(2):
                    step(i, r)

        def has(i, k=0):
            return not isinstance(i, int) or k <= i < NT // 2 + k

        @block.sync
        def _(sp):
            sp.dma_start(wo[:], a["wo"].rearrange("(k p) e -> p k e", p=P)).then_inc(s_w, 16)
            sp.dma_start(bo[:], a["bo"].partition_broadcast(P)).then_inc(s_w, 16)
            for b in range(2):
                sp.dma_start(at[:, b], at_dram[b].rearrange("(k p) t -> p k t", p=P)).then_inc(s_at[b], 16)
            sp.dma_start(w1[:], a["w1T"].rearrange("(k p) e -> p k e", p=P)).then_inc(s_w1, 16)
            sp.dma_start(w2[:], a["w2T"].rearrange("(k p) e -> p k e", p=P)).then_inc(s_w1, 16)
            for b in range(2, B):
                sp.wait_ge(s_po, TB * (b - 1))
                sp.dma_start(at[:, b % 2], at_dram[b].rearrange("(k p) t -> p k t", p=P)).then_inc(s_at[b % 2], 16)

            with sp.Fori(0, NT) as t:
                sp.wait_ge(s_x, t + 1)
                sp.dma_start(out.rearrange("(t p) d -> t p d", p=P)[bass.ds(t, 1)].rearrange("o p d -> (o p) d"),
                             x_sb[:, bass.ds(t, 1), :].rearrange("p o d -> p (o d)")).then_inc(s_o, 16)
            sp.wait_ge(s_o, 16 * NT)

        @block.gpsimd
        def _(pool):
            pool.memset(ones[:], 1.0).then_inc(s_c, 1)
            pool.memset(magic[:], MAGIC).then_inc(s_c, 1)
            pool.wait_ge(s_k, 1)
            for t in range(NT):
                pool.tensor_tensor(x_sb[:, t], x_sb[:, t], bo[:], ALU.add).then_inc(s_xb, 1)
            pool.wait_ge(s_k, 3)
            pool.tensor_scalar(w2[:], w2[:], rms[:, 1:2], MAGIC, ALU.mult, ALU.add).then_inc(s_q2, 1)
            pool.wait_ge(s_q2, 1)
            pool.tensor_scalar(w2[:], w2[:], MAGIC + 1, MAGIC - 1, ALU.min, ALU.max).then_inc(s_q2, 1)
            pool.wait_ge(s_q2, 2)
            pool.tensor_scalar(w2q[:], w2[:], MAGIC, None, ALU.subtract).then_inc(s_q2, 1)

        @block.scalar
        def _(act):
            act.wait_ge(s_w1, 32)
            act.activation(w1q[:], w1[:], ACT.Square, accum_out=ssq[:, 0:1]).then_inc(s_sq, 1)
            act.activation(w2q[:], w2[:], ACT.Square, accum_out=ssq[:, 1:2]).then_inc(s_sq, 1)
            act.wait_ge(s_k, 2)
            act.activation(sd[:], sd[:], ACT.Sqrt).then_inc(s_sd, 1)
            act.wait_ge(s_ln, LN_VAR)
            act.activation(rstd[:], rstd[:], ACT.Sqrt).then_inc(s_lsd, 1)
            act.wait_ge(s_ln, LN_READY)
            act.wait_ge(s_q1, 3)
            for t in range(NT):
                act.activation(xn[:, t], x_sb[:, t], ACT.Identity, scale=rstd[:, t:t + 1], bias=nmr[:, t:t + 1])\
                    .then_inc(s_xn, 1)
            act.wait_ge(s_am, 4)
            act.wait_ge(s_c, 2)
            for t in range(NT):
                act.activation(xn[:, t], xn[:, t], ACT.Identity, scale=sc[:, t:t + 1], bias=magic[:, 0:1])\
                    .then_inc(s_xs, 1)
            for t in range(NT):
                act.wait_ge(s_xt, t + 1)
                act.activation(xqT[:, :, t * P:(t + 1) * P], pht[:, KH // 2 * (t % 2):KH // 2 * (t % 2) + KD], ACT.Copy)\
                    .then_inc(s_xtc, 1)

            def step(i, r):
                if has(i):
                    t = i * 2 + r
                    for c in range(2):
                        act.wait_ge(s_c1, t + 1)
                        act.wait_ge(s_up, t * 2 + (c + 1))
                        if c == 0 and has(i, 1):
                            act.wait_ge(s_hq, t - 1)
                        act.activation(h[:, r, c * 2 * L:(c + 1) * 2 * L], pup[c][:].rearrange("p a l -> p (a l)"),
                                       ACT.Gelu, scale=c1r[:, r:r + 1]).then_inc(s_h, 1)
                if has(i, 1):
                    t = i * 2 + (r - 2)
                    act.wait_ge(s_ht, t + 1)
                    if has(i, 2):
                        act.wait_ge(s_dn, t - 1)
                    act.activation(hqT[:, r], pht[:], ACT.Copy).then_inc(s_htc, 1)
                if has(i):
                    t = i * 2 + r
                    act.wait_ge(s_a2, t * 5 + 4)
                    act.activation(h[:, r], h[:, r], ACT.Identity, scale=sc2[:, r], bias=magic[:, 0:1]).then_inc(s_v, 1)

            run(act, step, 2)

        @block.vector
        def _(dve):
            dve.wait_ge(s_w, 32)
            dve.tensor_scalar(bo[:], bo[:], tg[:, 0:1], None, ALU.mult).then_inc(s_k, 1)
            for t in range(NT):
                dve.wait_ge(s_po, t + 1)
                dve.wait_ge(s_xb, t + 1)
                dve.scalar_tensor_tensor(x_sb[:, t], pdn[t % 2][:], tg[:, 0:1], x_sb[:, t], ALU.mult, ALU.add)\
                    .then_inc(s_xa, 1)
                if t == 3:
                    dve.wait_ge(s_ms, 1)
                    dve.tensor_scalar(sd[:], pup[0][:, 0, 0:2], 1.0 / (D * FF), EPS, ALU.mult, ALU.max).then_inc(s_k, 1)
                    dve.wait_ge(s_sd, 1)
                    dve.reciprocal(rms[:], sd[:]).then_inc(s_k, 1)
                    dve.tensor_scalar(back[:], sd[:], 1.0 / QMAX, None, ALU.mult).then_inc(s_k, 1)
                    dve.wait_ge(s_k, 4)
                    dve.tensor_scalar(back[:, 1:2], back[:, 1:2], tg[:, 1:2], None, ALU.mult).then_inc(s_k, 1)
                    dve.tensor_scalar(w1[:], w1[:], rms[:, 0:1], MAGIC, ALU.mult, ALU.add).then_inc(s_q1, 1)
                    dve.wait_ge(s_q1, 1)
                    dve.tensor_scalar(w1[:], w1[:], MAGIC + 1, MAGIC - 1, ALU.min, ALU.max).then_inc(s_q1, 1)
                    dve.wait_ge(s_q1, 2)
                    dve.tensor_scalar(w1q[:], w1[:], MAGIC, None, ALU.subtract).then_inc(s_q1, 1)
            for t in range(NT):
                dve.wait_ge(s_xa, t + 1)
                dve.bn_stats(stats[:, t], x_sb[:, t]).then_inc(s_ln, 1)
            dve.wait_ge(s_ln, NT)
            for t in range(NT):
                dve.bn_aggr(mv[:, t], stats[:, t]).then_inc(s_ln, 1)
            dve.wait_ge(s_ln, 2 * NT)
            dve.tensor_scalar(rstd[:], mv[:, :, 1], EPS, None, ALU.add).then_inc(s_ln, 1)
            dve.wait_ge(s_lsd, 1)
            dve.reciprocal(rstd[:], rstd[:]).then_inc(s_ln, 1)
            dve.wait_ge(s_ln, LN_RSTD)
            dve.scalar_tensor_tensor(nmr[:], mv[:, :, 0], -1.0, rstd[:], ALU.mult, ALU.mult).then_inc(s_ln, 1)
            dve.memset(am[:, NT:NT + 2], 1.0)
            for t in range(NT):
                dve.wait_ge(s_xn, t + 1)
                last = dve.tensor_reduce(am[:, t:t + 1], xn[:, t], AX.X, ALU.max, apply_absolute_value=True)
            last.then_inc(s_am, 1)
            dve.wait_ge(s_am, 1)
            dve.tensor_scalar(am[:], am[:], EPS, None, ALU.max).then_inc(s_am, 1)
            dve.wait_ge(s_am, 2)
            dve.reciprocal(sc[:], am[:, 0:NT]).then_inc(s_am, 1)
            dve.wait_ge(s_am, 3)
            dve.tensor_scalar(sc[:], sc[:], QMAX, None, ALU.mult).then_inc(s_am, 1)
            dve.wait_ge(s_k, 5)
            dve.tensor_scalar(c1r[:], am[:, 0:2], back[:, 0:1], None, ALU.mult).then_inc(s_c1, 2)
            dve.wait_ge(s_q2, 3)
            for t in range(NT):
                dve.wait_ge(s_xs, t + 1)
                dve.tensor_scalar(xn[:, t], xn[:, t], MAGIC + QMAX, MAGIC + QMIN, ALU.min, ALU.max).then_inc(s_xq, 1)
            for t in range(NT):
                dve.wait_ge(s_xq, t + 1)
                dve.tensor_scalar(xq[:, t], xn[:, t], MAGIC, None, ALU.subtract).then_inc(s_xq, 1)

            def step(i, r):
                if has(i):
                    t = i * 2 + r
                    dve.wait_ge(s_h, t * 2 + 2)
                    if not isinstance(i, int) or i + 1 < NT // 2:
                        dve.tensor_tensor(c1r[:, r:r + 1], am[:, bass.ds(t + 2, 1)], back[:, 0:1], ALU.mult)\
                            .then_inc(s_c1, 1)
                    if has(i, 1):
                        dve.wait_ge(s_v, t - 1)
                    dve.tensor_reduce(am2[:, r], h[:, r], AX.X, ALU.max, apply_absolute_value=True).then_inc(s_a2, 1)
                    dve.wait_ge(s_a2, t * 5 + 1)
                    dve.tensor_scalar(am2[:, r], am2[:, r], EPS, None, ALU.max).then_inc(s_a2, 1)
                    dve.wait_ge(s_a2, t * 5 + 2)
                    dve.reciprocal(sc2[:, r], am2[:, r]).then_inc(s_a2, 1)
                    dve.wait_ge(s_a2, t * 5 + 3)
                    dve.tensor_scalar(sc2[:, r], sc2[:, r], QMAX, None, ALU.mult).then_inc(s_a2, 1)
                if has(i, 1):
                    t = i * 2 + (r - 2)
                    dve.wait_ge(s_dn, t + 1)
                    xt = x_sb[:, bass.ds(t, 1), :].rearrange("p o d -> p (o d)")
                    dve.scalar_tensor_tensor(xt, pdn[r][:], c2[:, r], xt, ALU.mult, ALU.add).then_inc(s_x, 1)
                if has(i):
                    t = i * 2 + r
                    if has(i, 1):
                        dve.wait_ge(s_x, t - 1)
                    dve.tensor_scalar(c2[:, r], am2[:, r], back[:, 1:2], None, ALU.mult).then_inc(s_a2, 1)
                    dve.wait_ge(s_v, t + 1)
                    dve.tensor_scalar(h[:, r], h[:, r], MAGIC + QMAX, MAGIC + QMIN, ALU.min, ALU.max).then_inc(s_cl, 1)
                    dve.wait_ge(s_cl, t + 1)
                    if has(i, 1):
                        dve.wait_ge(s_ht, t - 1)
                    dve.tensor_scalar(hq[:, r], h[:, r], MAGIC, None, ALU.subtract).then_inc(s_hq, 1)

            run(dve, step, 2)

        @block.tensor
        def _(pe):
            pe.wait_ge(s_w, 32)
            pe.wait_ge(s_c, 2)
            for t in range(NT):
                b = t // TB
                if t % TB == 0:
                    pe.wait_ge(s_at[b % 2], 16 * (b // 2 + 1))
                if t >= 2:
                    pe.wait_ge(s_xa, t - 1)
                for k in range(KD):
                    last = pe.matmul(pdn[t % 2][:], at[:, b % 2, k, (t % TB) * P:(t % TB + 1) * P], wo[:, k],
                                     start=(k == 0), stop=(k == KD - 1))
                last.then_inc(s_po, 1)
                if t == 3:
                    pe.wait_ge(s_sq, 2)
                    pe.matmul(pup[0][:, 0, 0:2], ones[:], ssq[:], start=True, stop=True).then_inc(s_ms, 1)
            for t in range(NT):
                pe.wait_ge(s_xq, NT + t + 1)
                if t >= 2:
                    pe.wait_ge(s_xtc, t - 1)
                for k in range(KD):
                    last = pe.transpose(pht[:, KH // 2 * (t % 2) + k], xq[:, t, k * P:(k + 1) * P], identb[:])
                last.then_inc(s_xt, 1)
            pe.wait_ge(s_xtc, NT)

            def step(i, r):
                if has(i):
                    t = i * 2 + r
                    for c in range(2):
                        if has(i, 1) or r == 1:
                            pe.wait_ge(s_h, t * 2 + (c - 1))
                        for q in range(2):
                            f = (2 * c + q) * L
                            for k in range(KD):
                                last = pe.matmul(pup[c][:, q], xqT[:, k, bass.ds(t * P, P)], w1q[:, k, f:f + L],
                                                 start=(k == 0), stop=(k == KD - 1))
                        last.then_inc(s_up, 1)
                if has(i, 1):
                    t = i * 2 + (r - 2)
                    pe.wait_ge(s_hq, t + 1)
                    if has(i, 2) or r == 1:
                        pe.wait_ge(s_htc, t)
                    for k in range(KH):
                        last = pe.transpose(pht[:, k], hq[:, r, k * P:(k + 1) * P], identb[:])
                    last.then_inc(s_ht, 1)
                    pe.wait_ge(s_htc, t + 1)
                    if has(i, 2):
                        pe.wait_ge(s_x, t - 1)
                    for k in range(KH):
                        last = pe.matmul(pdn[r][:], hqT[:, r, k], w2q[:, k], start=(k == 0), stop=(k == KH - 1))
                    last.then_inc(s_dn, 1)

            run(pe, step, 2)


def build(nc, a, out):
    def dram(name, shape, dt=F32):
        return nc.dram_tensor(name, shape, dt, kind="Internal").ap()

    bc_dram = dram("bc_dram", (B, 2 * NS, L))
    xg_dram = dram("xg_dram", (ST, P, D))
    yg_dram = dram("yg_dram", (ST, P, D))
    qk_dram = dram("qk_dram", (2, 3, B, KD, P, L), BF16)
    v_dram = dram("v_dram", (NG, P, TB, G4 * VW))
    m_dram = dram("m_dram", (NG, 3 * G4 * TB, P), BF16)
    at_dram = dram("at_dram", (B, D, L))

    with ExitStack() as ctx:
        x_sb = ctx.enter_context(nc.sbuf_tensor("x_sb", [P, NT, D], F32))
        ident = ctx.enter_context(nc.sbuf_tensor("ident_sb", [P, P], F32))
        identb = ctx.enter_context(nc.sbuf_tensor("identb_sb", [P, P], BF16))
        tg = ctx.enter_context(nc.sbuf_tensor("tg_sb", [P, 4], F32))
        zeros = ctx.enter_context(nc.sbuf_tensor("zeros_sb", [P, D], F32))
        s_x = ctx.enter_context(nc.semaphore("x_loaded"))
        s_z = ctx.enter_context(nc.semaphore("zeros_set"))
        s_zero = ctx.enter_context(nc.semaphore("slots_zeroed"))

        with nc.Block() as block:
            @block.gpsimd
            def _(pool):
                pool.memset(zeros[:], 0.0).then_inc(s_z, 1)
                pool.wait_ge(s_z, 1)
                pool.dma_start(xg_dram.rearrange("j p d -> p j d"),
                               zeros[:].unsqueeze(1).broadcast_to([P, ST, D])).then_inc(s_zero, 16)

            @block.sync
            def _(sp):
                sp.dma_start(tg[:, 0:2], a["g_xattn"].partition_broadcast(P)).then_inc(s_x, 16)
                sp.dma_start(tg[:, 2:4], a["g_ffn"].partition_broadcast(P)).then_inc(s_x, 16)
                sp.dma_start(ident[:], a["ident"]).then_inc(s_x, 16)
                sp.dma_start(x_sb[:], a["x"].rearrange("(t p) d -> p t d", p=P)).then_inc(s_x, 16)

            @block.scalar
            def _(act):
                act.wait_ge(s_x, 64)
                act.activation(tg[:], tg[:], ACT.Tanh)
                act.activation(identb[:], ident[:], ACT.Copy)

        mamba(nc, x_sb, ident, tg[:, 0:1], a, bc_dram)
        moe(nc, x_sb, ident, tg[:, 2:3], a, xg_dram, yg_dram, s_zero)
        mark = ctx.enter_context(nc.semaphore("first_after_moe"))
        with nc.Block() as block:
            @block.gpsimd
            def _(pool):
                pool.sem_clear(range(s_zero.num + 1, mark.num))

        attention_inputs(nc, x_sb, ident, a, qk_dram, v_dram)
        attention(nc, ident, identb, a, qk_dram, v_dram, m_dram, at_dram)
        attention_out_and_ffn(nc, x_sb, ident, identb, tg[:, 1:4:2], a, at_dram, out)


def laid_out(z):
    def cols(v):
        return v.reshape(E4, P).T

    return {
        "x": z["x"].reshape(T, D),
        "ctxT": z["ctx_1024"].reshape(T, DC).T,
        "posT": z["fside_BxSx2_0"].reshape(T, 2).T,
        "g_xattn": z["g_xattn"],
        "g_ffn": z["g_ffn"],
        "in_wT": z["L0_xattn_in_proj_w"].T,
        "conv_w": z["L0_xattn_conv_w"],
        "conv_b": cols(z["L0_xattn_conv_b"]),
        "xp_wT": z["L0_xattn_x_proj_w"].T,
        "dt_wT": z["L0_xattn_dt_proj_w"].T,
        "dt_b": cols(z["L0_xattn_dt_proj_b"]),
        "A_log": z["L0_xattn_A_log"],
        "Dv": cols(z["L0_xattn_D"]),
        "gate_w": z["L0_ffn_gate_w"],
        "ex_bias": z["L0_ffn_expert_bias"],
        "sh_gate": z["L0_ffn_shared_gate_w"],
        "sh_up": z["L0_ffn_shared_up_w"],
        "sh_down": z["L0_ffn_shared_down_w"],
        "ex_gu": z["L0_ffn_experts_gate_up"],
        "ex_dn": z["L0_ffn_experts_down"],
        "wq": z["L1_xattn_Wq"],
        "wkv": z["L1_xattn_Wkv"],
        "wo": z["L1_xattn_Wout"],
        "bo": z["L1_xattn_bout"],
        "w1T": z["L1_ffn_w1"].T,
        "w2T": z["L1_ffn_w2"].T,
    }


def constants():
    f = np.arange(P)
    d = f % HD
    half = HD // 4
    freqs = (10000.0 ** (-np.arange(half) / half)).astype(np.float32)
    freq = np.zeros((2, P), np.float32)
    freq[d // (HD // 2), f] = freqs[d % (HD // 2) // 2]
    swap = np.zeros((P, P), np.float32)
    swap[f ^ 1, f] = 1
    sel = np.zeros((P, P), np.float32)
    sel[f // 32 * 32 + HD, f] = 1
    return {
        "ident": np.eye(P, dtype=np.float32),
        "lower": np.triu(np.ones((P, P), np.float32), 1),
        "iota": np.arange(64, dtype=np.float32),
        "freq": freq,
        "swap": swap,
        "sign": np.where(f % 2, 1, -1).astype(np.float32).reshape(P, 1),
        "sel": sel,
    }


def kernel(**inputs):
    import concourse.bacc as bacc
    from concourse.bass_utils import run_bass_kernel_spmd

    nc = bacc.Bacc("TRN2", target_bir_lowering=False, num_devices=1)
    host = {**laid_out({k: np.asarray(v) for k, v in inputs.items()}), **constants()}
    arrays = {f"in_{k}": np.ascontiguousarray(v) for k, v in host.items()}
    a = {k: nc.dram_tensor(f"in_{k}", host[k].shape, mybir.dt.from_np(host[k].dtype), kind="ExternalInput").ap()
         for k in host}
    out = nc.dram_tensor("out_0", (T, D), F32, kind="ExternalOutput").ap()
    build(nc, a, out)
    r = run_bass_kernel_spmd(nc, [arrays], core_ids=[0])
    return r.results[0]["out_0"].reshape(B, L, D)
```

```python
from contextlib import ExitStack

import numpy as np

import concourse.bass as bass
from concourse import mybir

F32 = mybir.dt.float32
BF16 = mybir.dt.bfloat16
I32 = mybir.dt.int32
U32 = mybir.dt.uint32
U8 = mybir.dt.uint8
ALU = mybir.AluOpType
ACT = mybir.ActivationFunctionType
AX = mybir.AxisListType

P = 128
B, L, D = 4, 512, 512
DC = 256
T = B * L
NT = T // P
TB = L // P
KD = D // P
KC = DC // P
E4 = D // P
NS = 16
R = 16
EPS = 1e-5

LN_VAR = 2 * NT + 1
LN_RSTD = 2 * NT + 2
LN_READY = 2 * NT + 3


def mamba(nc, x_sb, ident, tg, a, bc_dram, xg_dram, zeros, s_zero):
    JOBS = 2 * E4
    STEPS = NS // 4
    with ExitStack() as ctx:
        def sb(name, shape, dt=F32):
            return ctx.enter_context(nc.sbuf_tensor("m_" + name, shape, dt))

        def sem(name):
            return ctx.enter_context(nc.semaphore("m_" + name))

        ctxT = sb("ctxT", [P, 2, KC, L])
        w_in = sb("w_in", [P, KC, D])
        w_xp = sb("w_xp", [P, E4, R + 2 * NS])
        w_dt = sb("w_dt", [R, D])
        conv_w = sb("conv_w", [P, E4, 4])
        conv_b = sb("conv_b", [P, E4])
        dt_b = sb("dt_b", [P, E4])
        negA = sb("negA", [P, E4 * NS])
        Dcol = sb("Dcol", [P, E4])
        diagD = sb("diagD", [P, E4, P])
        stats = sb("stats", [P, NT, 6])
        mv = sb("mv", [P, NT, 2])
        rstd = sb("rstd", [P, NT])
        nmr = sb("nmr", [P, NT])
        xpad = sb("xpad", [P, E4, L + 3])
        conv = sb("conv", [P, E4, L])
        u = sb("u", [P, 2, E4, L])
        dt = sb("dt", [P, 2, E4, L])
        dtu = sb("dtu", [P, 2, E4, L])
        gate = sb("gate", [P, 2, TB, L])
        xdbl = sb("xdbl", [R + 2 * NS, L])
        ee = sb("ee", [P, E4, L])
        ll = sb("ll", [P, E4, L])
        small = sb("small", [P, E4, L], U8)
        bch = sb("bch", [P, 2, 2, 2, L])
        dA = sb("dA", [P, 2, 2, L])
        dBu = sb("dBu", [P, 2, 2, L])
        hs = sb("hs", [P, 2, 2, L])
        hc = sb("hc", [P, 2, 2, L])
        ty = sb("ty", [P, E4, L])
        py = [ctx.enter_context(nc.psum_tensor(f"m_y{i}", [P, L], F32)) for i in range(E4)]
        pp = [ctx.enter_context(nc.psum_tensor(f"m_p{i}", [P, L], F32)) for i in range(2)]
        px = ctx.enter_context(nc.psum_tensor("m_x", [P, L], F32))
        ptb = ctx.enter_context(nc.psum_tensor("m_t", [P, L], F32))
        pt = ptb[:].rearrange("p (t c) -> p t c", t=TB)
        pdt = pp + [px, ptb]

        s_wld = sem("weights_loaded")
        s_xld = sem("x_loaded")
        s_ctx = [sem(f"ctx_loaded{i}") for i in range(2)]
        s_bc = [sem(f"bc_loaded{i}") for i in range(2)]
        s_bcst = sem("bc_stored")
        s_pad = sem("pad_zeroed")
        s_dz = sem("da_zeroed")
        s_ln = sem("ln_steps")
        s_sd = sem("ln_std")
        s_negA0 = sem("expA")
        s_negA = sem("negA_ready")
        s_diag = sem("diagD_ready")
        s_xin = sem("inproj_done")
        s_xc = sem("inproj_copied")
        s_cv = sem("conv_steps")
        s_u = sem("u_ready")
        s_gate = sem("gate_ready")
        s_xd = sem("xdbl_done")
        s_xdc = sem("xdbl_copied")
        s_dtp = sem("dt_product")
        s_dtx = sem("dt_sums")
        s_abs = sem("dt_abs")
        s_rel = sem("dt_relu")
        s_e = sem("exp_neg_abs")
        s_l = sem("ln1p")
        s_q = sem("series_steps")
        s_m = sem("small_mask")
        s_pick = sem("picked")
        s_dt = sem("dt_ready")
        s_dtu = sem("dtu_ready")
        s_dA = sem("decay_ready")
        s_dbu = sem("input_ready")
        s_scan = sem("scanned")
        s_hc = sem("output_terms")
        s_y = sem("summed")
        s_y0 = sem("sum_started")
        s_g = sem("gated")
        s_t = sem("transposed")
        s_add = sem("added")

        block = ctx.enter_context(nc.Block())

        HALVES = NS // 2

        def job(b, q, et):
            return (b * HALVES + q) * E4 + et

        @block.sync
        def _(sp):
            sp.dma_start(w_in[:], a["in_wT"].rearrange("(k p) e -> p k e", p=P)).then_inc(s_wld, 16)
            sp.dma_start(conv_w[:], a["conv_w"].rearrange("(t p) o k -> p t (o k)", p=P)).then_inc(s_wld, 16)
            sp.dma_start(conv_b[:], a["conv_b"]).then_inc(s_wld, 16)
            sp.dma_start(w_xp[:], a["xp_wT"].rearrange("(k p) e -> p k e", p=P)).then_inc(s_wld, 16)
            sp.dma_start(w_dt[:], a["dt_wT"]).then_inc(s_wld, 16)
            sp.dma_start(dt_b[:], a["dt_b"]).then_inc(s_wld, 16)
            sp.dma_start(negA[:].rearrange("p (t n) -> p t n", t=E4),
                         a["A_log"].rearrange("(t p) n -> p t n", p=P)).then_inc(s_wld, 16)
            sp.dma_start(Dcol[:], a["Dv"]).then_inc(s_wld, 16)

            def load_ctx(b):
                if b >= 2:
                    sp.wait_ge(s_xin, E4 * (b - 1))
                sp.dma_start(ctxT[:, b % 2], a["ctxT"][:, b * L:(b + 1) * L].rearrange("(k p) l -> p k l", p=P))\
                    .then_inc(s_ctx[b % 2], 16)

            load_ctx(0)
            load_ctx(1)
            sp.dma_start(x_sb[:], a["x"].rearrange("(t p) d -> p t d", p=P)).then_inc(s_xld, 16)
            for b in range(B):
                sp.wait_ge(s_xdc, b + 1)
                sp.dma_start(bc_dram[b], xdbl[R:R + 2 * NS, :]).then_inc(s_bcst, 16)
                sp.wait_ge(s_bcst, 16 * (b + 1))
                if b + 2 < B:
                    load_ctx(b + 2)

                def load_chunk(b, k, i, first):
                    c = b * 8 + i * 2 + k
                    if not first:
                        sp.wait_ge(s_dbu, c * E4 - E4)
                        sp.wait_ge(s_hc, c * E4 - E4)
                    for m in range(2):
                        src = bc_dram[b:b + 1, bass.ds(i * 4 + m * NS + k * 2, 2), :].rearrange(
                            "o k l -> o (k l)").partition_broadcast(P)
                        sp.dma_start(bch[:, k, m].rearrange("p s l -> p (s l)"), src).then_inc(s_bc[k], 16)

                if b == 0:
                    load_chunk(b, 0, 0, True)
                    load_chunk(b, 1, 0, True)
                    with sp.Fori(1, STEPS) as i:
                        for k in range(2):
                            load_chunk(b, k, i, False)
                else:
                    with sp.Fori(0, STEPS) as i:
                        for k in range(2):
                            load_chunk(b, k, i, False)
            for c in range(2):
                sp.dma_start(xg_dram.rearrange("j p d -> p j d")[:, :, c * D // 2:(c + 1) * D // 2],
                             zeros[:].unsqueeze(1).broadcast_to([P, ST, D // 2])).then_inc(s_zero, 16)

        @block.gpsimd
        def _(pool):
            pool.memset(xpad[:, :, 0:3], 0.0).then_inc(s_pad, 1)
            pool.memset(dA[:], 0.0).then_inc(s_dz, 1)

            def prepare(b):
                pool.wait_ge(s_dt, b + 1)
                pool.tensor_tensor(dtu[:, b % 2], dt[:, b % 2], u[:, b % 2], ALU.mult).then_inc(s_dtu, 1)

            def half(b, q):
                k = q % 2
                pool.wait_ge(s_bc[k], (b * STEPS + q // 2) * 32 + 32)
                for et in range(E4):
                    n = job(b, q, et)
                    if n >= 2:
                        pool.wait_ge(s_scan, n - 1)
                    pool.tensor_tensor(dBu[:, et % 2], bch[:, k, 0],
                                       dtu[:, b % 2, et].unsqueeze(1).broadcast_to([P, 2, L]),
                                       ALU.mult).then_inc(s_dbu, 1)

            for b in range(B):
                prepare(b)
                pool.wait_ge(s_dtu, b + 1)
                for q in range(HALVES):
                    half(b, q)

        @block.scalar
        def _(act):
            act.wait_ge(s_wld, 16 * 8)
            act.activation(negA[:], negA[:], ACT.Exp).then_inc(s_negA0, 1)
            act.wait_ge(s_pad, 1)

            def gates(b):
                if b == 0:
                    act.wait_ge(s_ln, LN_READY)
                if b >= 2:
                    act.wait_ge(s_g, E4 * (b - 1))
                for t in range(TB):
                    n = b * TB + t
                    act.activation(gate[:, b % 2, t], x_sb[:, n], ACT.Silu, scale=rstd[:, n:n + 1],
                                   bias=nmr[:, n:n + 1]).then_inc(s_gate, 1)

            def copy_x(b, parts):
                for et in parts:
                    act.wait_ge(s_xin, E4 * b + et + 1)
                    if b >= 1:
                        act.wait_ge(s_cv, 4 * (E4 * (b - 1) + et + 1))
                    act.activation(xpad[:, et, 3:3 + L], pp[et % 2][:], ACT.Copy).then_inc(s_xc, 1)

            def silu(b):
                if b >= 2:
                    act.wait_ge(s_y0, E4 * (b - 1))
                for et in range(E4):
                    act.wait_ge(s_cv, 4 * (E4 * b + et + 1))
                    act.activation(u[:, b % 2, et], conv[:, et], ACT.Silu, bias=conv_b[:, et:et + 1]).then_inc(s_u, 1)

            def copy_xdbl(b):
                act.wait_ge(s_xd, b + 1)
                if b >= 1:
                    act.wait_ge(s_bcst, 16 * b)
                    act.wait_ge(s_dtp, E4 * b)
                act.activation(xdbl[:], px[0:R + 2 * NS, :], ACT.Copy).then_inc(s_xdc, 1)

            def logs(b):
                act.wait_ge(s_dtx, E4 * (b + 1))
                if b >= 1:
                    act.wait_ge(s_pick, b)
                    act.wait_ge(s_dt, b)
                act.activation(ee[:], dt[:, b % 2], ACT.Abs).then_inc(s_abs, 1)
                act.wait_ge(s_abs, b + 1)
                act.activation(ee[:], ee[:], ACT.Exp, scale=-1.0).then_inc(s_e, 1)
                act.wait_ge(s_e, b + 1)
                act.activation(ll[:], ee[:], ACT.Ln, bias=1.0).then_inc(s_l, 1)

            def half(b, q):
                i, k = q // 2, q % 2
                for et in range(E4):
                    n = job(b, q, et)
                    if n >= 2:
                        act.wait_ge(s_scan, n - 1)
                    for m in range(2):
                        c = et * NS + i * 4 + k * 2 + m
                        last = act.activation(dA[:, et % 2, m, 1:L], dt[:, b % 2, et, 1:L], ACT.Exp,
                                              scale=negA[:, c:c + 1])
                    last.then_inc(s_dA, 1)

            copy_x(0, range(E4))
            silu(0)
            copy_xdbl(0)
            logs(0)
            act.wait_ge(s_negA, 1)
            act.wait_ge(s_dz, 1)
            for b in range(B):
                act.wait_ge(s_dt, b + 1)
                for q in range(HALVES):
                    half(b, q)
                    if b + 1 < B:
                        if q == 0 and b >= 1:
                            gates(b + 1)
                        elif q in (1, 2):
                            copy_x(b + 1, (2 * q - 2, 2 * q - 1))
                        elif q in (3, 4, 5):
                            {3: silu, 4: copy_xdbl, 5: logs}[q](b + 1)
                        if b == 0 and q == 4:
                            act.wait_ge(s_ln, LN_VAR)
                            act.activation(rstd[:], rstd[:], ACT.Sqrt).then_inc(s_sd, 1)
                        if b == 0 and q == 6:
                            gates(0)
                            gates(1)

        @block.vector
        def _(dve):
            dve.wait_ge(s_negA0, 1)
            dve.tensor_scalar(negA[:], negA[:], -1.0, None, ALU.mult).then_inc(s_negA, 1)
            for et in range(E4):
                dve.tensor_scalar(diagD[:, et], ident[:], Dcol[:, et:et + 1], None, ALU.mult).then_inc(s_diag, 1)

            def convolve(b):
                for et in range(E4):
                    dve.wait_ge(s_xc, E4 * b + et + 1)
                    if b >= 1 and et == 0:
                        dve.wait_ge(s_pick, b)
                    for k in range(4):
                        if k == 0:
                            dve.tensor_scalar(conv[:, et], xpad[:, et, 0:L], conv_w[:, et, 0:1], None, ALU.mult)\
                                .then_inc(s_cv, 1)
                        else:
                            dve.wait_ge(s_cv, 4 * (E4 * b + et) + k)
                            dve.scalar_tensor_tensor(conv[:, et], xpad[:, et, k:k + L], conv_w[:, et, k:k + 1],
                                                     conv[:, et], ALU.mult, ALU.add).then_inc(s_cv, 1)

            def dt_sums(b):
                for et in range(E4):
                    dve.wait_ge(s_dtp, E4 * b + et + 1)
                    dve.tensor_scalar(dt[:, b % 2, et], pdt[et][:], dt_b[:, et:et + 1], None, ALU.add)\
                        .then_inc(s_dtx, 1)

            def softplus(b):
                p = b % 2
                dve.wait_ge(s_e, b + 1)
                dve.wait_ge(s_u, E4 * (b + 1))
                dve.tensor_scalar(conv[:], ee[:], -0.25, None, ALU.mult).then_inc(s_q, 1)
                dve.tensor_scalar(dt[:, p], dt[:, p], 0.0, None, ALU.max).then_inc(s_rel, 1)
                for k, c in enumerate((1.0 / 3, -0.5, 1.0)):
                    dve.wait_ge(s_q, 4 * b + k + 1)
                    dve.scalar_tensor_tensor(conv[:], conv[:], c, ee[:], ALU.add, ALU.mult).then_inc(s_q, 1)
                    if k == 0:
                        dve.tensor_scalar(small[:], ee[:], 1.0 / 32, None, ALU.is_lt).then_inc(s_m, 1)
                dve.wait_ge(s_q, 4 * b + 4)
                dve.wait_ge(s_m, b + 1)
                dve.wait_ge(s_l, b + 1)
                dve.copy_predicated(ll[:], small[:], conv[:]).then_inc(s_pick, 1)
                dve.wait_ge(s_rel, b + 1)
                dve.wait_ge(s_pick, b + 1)
                dve.tensor_tensor(dt[:, p], dt[:, p], ll[:], ALU.add).then_inc(s_dt, 1)

            def scan(b, q, et):
                n = job(b, q, et)
                dve.wait_ge(s_dA, n + 1)
                dve.wait_ge(s_dbu, n + 1)
                if n >= 2:
                    dve.wait_ge(s_hc, n - 1)
                dve.tensor_tensor_scan(hs[:, et % 2].rearrange("p s l -> p (s l)"),
                                       dA[:, et % 2].rearrange("p s l -> p (s l)"),
                                       dBu[:, et % 2].rearrange("p s l -> p (s l)"), 0.0, ALU.mult, ALU.add)\
                    .then_inc(s_scan, 1)

            def terms(b, q, et):
                n = job(b, q, et)
                dve.wait_ge(s_scan, n + 1)
                if n >= 2:
                    dve.wait_ge(s_y, n - 1)
                dve.tensor_tensor(hc[:, et % 2], hs[:, et % 2], bch[:, q % 2, 1], ALU.mult).then_inc(s_hc, 1)

            def half(b, q):
                for et in range(E4):
                    scan(b, q, et)
                    if et >= 1:
                        terms(b, q, et - 1)
                terms(b, q, E4 - 1)

            def gate_sums(b):
                dve.wait_ge(s_gate, TB * (b + 1))
                for et in range(E4):
                    dve.wait_ge(s_y, job(b, HALVES - 1, et) + 1)
                    if b >= 1 and et == 0:
                        dve.wait_ge(s_t, E4 * b)
                    dve.tensor_tensor(ty[:, et], py[et][:], gate[:, b % 2, et], ALU.mult).then_inc(s_g, 1)

            def add(b, et):
                dve.wait_ge(s_t, E4 * b + et + 1)
                xv = x_sb[:, b * TB:(b + 1) * TB, et * P:(et + 1) * P]
                dve.scalar_tensor_tensor(xv, pt, tg[:, 0:1], xv, ALU.mult, ALU.add).then_inc(s_add, 1)

            def variances():
                dve.wait_ge(s_xld, 16)
                for t in range(NT):
                    dve.bn_stats(stats[:, t], x_sb[:, t]).then_inc(s_ln, 1)
                dve.wait_ge(s_ln, NT)
                for t in range(NT):
                    dve.bn_aggr(mv[:, t], stats[:, t]).then_inc(s_ln, 1)
                dve.wait_ge(s_ln, 2 * NT)
                dve.tensor_scalar(rstd[:], mv[:, :, 1], EPS, None, ALU.add).then_inc(s_ln, 1)

            def ln_columns():
                dve.wait_ge(s_sd, 1)
                dve.reciprocal(rstd[:], rstd[:]).then_inc(s_ln, 1)
                dve.wait_ge(s_ln, LN_RSTD)
                dve.scalar_tensor_tensor(nmr[:], mv[:, :, 0], -1.0, rstd[:], ALU.mult, ALU.mult).then_inc(s_ln, 1)

            convolve(0)
            dt_sums(0)
            softplus(0)
            for b in range(B):
                for q in range(HALVES):
                    half(b, q)
                    if b >= 1 and 1 <= q <= E4:
                        add(b - 1, q - 1)
                    if b + 1 < B and q in (2, 4, 6):
                        {2: convolve, 4: dt_sums, 6: softplus}[q](b + 1)
                    if b == 0 and q == 3:
                        variances()
                    if b == 0 and q == 5:
                        ln_columns()
                gate_sums(b)
            for et in range(E4):
                add(B - 1, et)

        @block.tensor
        def _(pe):
            pe.wait_ge(s_wld, 16 * 8)

            def project(b, parts):
                pe.wait_ge(s_ctx[b % 2], 16 * (b // 2 + 1))
                for et in parts:
                    if b >= 1 and et < 2:
                        pe.wait_ge(s_dtx, E4 * b)
                    if et >= 2:
                        pe.wait_ge(s_xc, E4 * b + et - 1)
                    for k in range(KC):
                        last = pe.matmul(pp[et % 2][:], w_in[:, k, et * P:(et + 1) * P], ctxT[:, b % 2, k],
                                         start=(k == 0), stop=(k == KC - 1))
                    last.then_inc(s_xin, 1)

            def project_u(b):
                for et in range(E4):
                    pe.wait_ge(s_u, E4 * b + et + 1)
                    if b >= 1 and et == 0:
                        pe.wait_ge(s_dtx, E4 * b)
                    last = pe.matmul(px[0:R + 2 * NS, :], w_xp[:, et], u[:, b % 2, et], start=(et == 0),
                                     stop=(et == E4 - 1))
                last.then_inc(s_xd, 1)

            def dt_product(b, et):
                if et == 0:
                    pe.wait_ge(s_xdc, b + 1)
                    pe.wait_ge(s_xc, E4 * (b + 1))
                if et == 3 and b >= 2:
                    pe.wait_ge(s_add, E4 * (b - 1))
                pe.matmul(pdt[et][:], w_dt[:, et * P:(et + 1) * P], xdbl[0:R, :], start=True,
                          stop=True).then_inc(s_dtp, 1)

            def half(b, q):
                for et in range(E4):
                    pe.wait_ge(s_hc, job(b, q, et) + 1)
                    for m in range(2):
                        last = pe.matmul(py[et][:], ident[:], hc[:, et % 2, m], start=False, stop=True,
                                         skip_group_check=True)
                    last.then_inc(s_y, 1)

            def turn(b, et):
                pe.wait_ge(s_g, E4 * b + et + 1)
                if E4 * b + et >= 1:
                    pe.wait_ge(s_add, E4 * b + et)
                if et == 0:
                    pe.wait_ge(s_dtx, E4 * min(b + 2, B))
                for t in range(TB):
                    last = pe.transpose(pt[:, t, :], ty[:, et, t * P:(t + 1) * P], ident[:])
                last.then_inc(s_t, 1)

            project(0, range(E4))
            project_u(0)
            for et in range(E4):
                dt_product(0, et)
            pe.wait_ge(s_diag, E4)
            for b in range(B):
                for et in range(E4):
                    if b >= 1:
                        pe.wait_ge(s_g, E4 * (b - 1) + et + 1)
                    pe.matmul(py[et][:], diagD[:, et], u[:, b % 2, et], start=True, stop=True,
                              skip_group_check=True).then_inc(s_y0, 1)
                for q in range(HALVES):
                    half(b, q)
                    if b >= 1 and q < E4:
                        turn(b - 1, q)
                    if b + 1 < B:
                        if q in (0, 1):
                            project(b + 1, (2 * q, 2 * q + 1))
                        elif q == 3:
                            project_u(b + 1)
                        elif q == 4:
                            for et in range(E4):
                                dt_product(b + 1, et)
            for et in range(E4):
                turn(B - 1, et)


NE = 16
F = 256
KF = F // P
ST = 2 * NT + NE - 1
RING = 4


def moe(nc, x_sb, ident, tg, a, xg_dram, yg_dram, s_zero, v_dram):
    with ExitStack() as ctx:
        def sb(name, shape, dt=F32):
            return ctx.enter_context(nc.sbuf_tensor("e_" + name, shape, dt))

        def sem(name):
            return ctx.enter_context(nc.semaphore("e_" + name))

        xn = sb("xn", [P, NT, D])
        xnT = sb("xnT", [P, KD, T])
        stats = sb("stats", [P, NT, 6])
        mv = sb("mv", [P, NT, 2])
        rstd = sb("rstd", [P, NT])
        nmr = sb("nmr", [P, NT])
        w_gate = sb("w_gate", [P, KD, NE])
        bias = sb("bias", [P, NE])
        iota = sb("iota", [P, 64])
        lower = sb("lower", [P, P])
        tri = sb("tri", [P, 2, P], BF16)
        ws1 = sb("ws1", [P, KD, 2 * F])
        ws2 = sb("ws2", [P, KF, D])
        w1 = sb("w1", [P, RING, KD, 2 * F])
        w2 = sb("w2", [P, RING, KF, D])
        xg = sb("xg", [P, 2, D])
        xgT = sb("xgT", [P, 2, KD, P])
        sg = sb("sg", [P, 2, F])
        hm = sb("hm", [P, 2, F])
        hT = sb("hT", [P, 2, KF, P])
        yo = sb("yo", [P, 2, D])
        score = sb("score", [P, NT, NE])
        biased = sb("biased", [P, NT, NE])
        top8 = sb("top8", [P, NT, 8])
        idx8 = sb("idx8", [P, NT, 8], U32)
        idxf = sb("idxf", [P, NT, 2])
        onehot = sb("onehot", [P, 2, NT, NE])
        member = sb("member", [P, NT, NE], BF16)
        tot = sb("tot", [P, NT, NE])
        cum = sb("cum", [P, NT + 1, NE])
        cnt = sb("cnt", [P, 4, NE])
        cnti = sb("cnti", [P, 2, NE], I32)
        pos = sb("pos", [P, NT, NE])
        prod = sb("prod", [P, 4, NT, NE])
        slotf = sb("slotf", [P, 2, NT])
        slot = sb("slot", [P, 2, NT], U32)
        sk = sb("sk", [P, 2, NT])
        den = sb("den", [P, NT])
        wk = sb("wk", [P, 2, NT])
        over = sb("over", [P, ST + 1, NE])
        ejf = sb("ejf", [P, ST + 1])
        ej = sb("ej", [P, ST + 1], I32)
        ends = sb("ends", [P, NE], I32)
        ctxT = xnT[:, 0:KC]
        wv = xnT[:, KC, 0:KC * D].rearrange("p (k e) -> p k e", k=KC)
        va = xnT[:, KC + 1, 0:2 * NH * VW].rearrange("p (r h c) -> p r h c", r=2, h=NH)
        yk = xn[:, 0:4].rearrange("p (t k) d -> p t k d", k=2)

        pxt = [ctx.enter_context(nc.psum_tensor(f"e_xt{i}", [P, KD, P], F32)) for i in range(2)]
        pgu = [ctx.enter_context(nc.psum_tensor(f"e_gu{i}", [P, 2 * F], F32)) for i in range(2)]
        pht = ctx.enter_context(nc.psum_tensor("e_ht", [P, 4, P], F32))
        pyo = [ctx.enter_context(nc.psum_tensor(f"e_y{i}", [P, D], F32)) for i in range(2)]
        prt = ctx.enter_context(nc.psum_tensor("e_rt", [P, 2, NT, NE], F32))

        s_w = sem("weights_loaded")
        s_ln = sem("ln_steps")
        s_sd = sem("ln_std")
        s_xn = sem("normalised")
        s_xt = sem("x_transposed")
        s_xtc = sem("x_transposed_copied")
        s_lg = sem("logits")
        s_sc = sem("scores")
        s_tri = sem("tri_ready")
        s_r = sem("routing_steps")
        s_cnt = sem("counted")
        s_slot = sem("slots_ready")
        s_ej = sem("tile_experts")
        s_sct = sem("scattered")
        s_gu = sem("up_done")
        s_sg = sem("silu_done")
        s_hm = sem("hidden_ready")
        s_ht = sem("hidden_transposed")
        s_htc = sem("hidden_copied")
        s_y = sem("down_done")
        s_yc = sem("down_copied")
        s_ld = [sem(f"tile_loaded{i}") for i in range(2)]
        s_wl = [sem(f"expert_loaded{i}") for i in range(RING)]
        s_wr = sem("experts_ready")
        s_yst = [sem(f"stored{i}") for i in range(2)]
        s_gat = [sem(f"gathered{i}") for i in range(2)]
        s_cmb = sem("combined")
        s_cx = sem("context_loaded")
        s_one = sem("ones_set")
        s_vm = sem("v_done")
        s_vc = sem("v_copied")
        s_vs = [sem(f"v_stored{i}") for i in range(2)]

        block = ctx.enter_context(nc.Block())

        @block.sync
        def _(sp):
            sp.dma_start(w_gate[:], a["gate_w"].rearrange("(k p) e -> p k e", p=P)).then_inc(s_w, 16)
            sp.dma_start(bias[:], a["ex_bias"].partition_broadcast(P)).then_inc(s_w, 16)
            sp.dma_start(iota[:], a["iota"].partition_broadcast(P)).then_inc(s_w, 16)
            sp.dma_start(lower[:], a["lower"]).then_inc(s_w, 16)
            sp.dma_start(ws1[:, :, 0:F], a["sh_gate"].rearrange("(k p) e -> p k e", p=P)).then_inc(s_w, 16)
            sp.dma_start(ws1[:, :, F:2 * F], a["sh_up"].rearrange("(k p) e -> p k e", p=P)).then_inc(s_w, 16)
            sp.dma_start(ws2[:], a["sh_down"].rearrange("(k p) e -> p k e", p=P)).then_inc(s_w, 16)

            def load_expert(e, r):
                sp.dma_start(w1[:, r], a["ex_gu"][bass.ds(e, 1)].rearrange("o (k p) f -> p (o k) f", p=P))\
                    .then_inc(s_wl[r], 16)
                sp.dma_start(w2[:, r], a["ex_dn"][bass.ds(e, 1)].rearrange("o (k p) f -> p (o k) f", p=P))\
                    .then_inc(s_wl[r], 16)

            def ready(r, turn):
                sp.wait_ge(s_wl[r], turn * 32)
                sp.sem_inc(s_wr, 1)

            for r in range(RING):
                load_expert(r, r)
            for r in range(RING):
                ready(r, 1)
            sp.wait_ge(s_ej, 2)
            with sp.Fori(1, NE // RING) as i:
                for r in range(RING):
                    sp.wait_ge(s_y, sp.value_load(ends[0:1, bass.ds(i * RING + (r - RING), 1)], min_val=NT,
                                                  max_val=NT + ST))
                    load_expert(i * RING + r, r)
                    if r >= 1:
                        ready(r - 1, i + 1)
                ready(RING - 1, i + 1)
            sp.wait_ge(s_y, NT)
            sp.dma_start(ctxT, a["ctxT"].rearrange("(k p) t -> p k t", p=P)).then_inc(s_cx, 16)
            sp.dma_start(wv, a["wkv"][:, D:2 * D].rearrange("(k p) e -> p k e", p=P)).then_inc(s_cx, 16)
            for t in range(NT):
                sp.wait_ge(s_vc, t + 1)
                sp.dma_start(v_dram[(t // TB) * 8:(t // TB + 1) * 8, :, t % TB, :].rearrange("g p c -> p g c"),
                             va[:, t % 2].rearrange("p (g h) c -> p g (h c)", g=8)).then_inc(s_vs[t % 2], 16)
            for r in range(2):
                sp.wait_ge(s_vs[r], 16 * NT // 2)

        @block.gpsimd
        def _(pool):
            pool.wait_ge(s_slot, 1)
            pool.wait_ge(s_zero, 32)
            for k in range(2):
                for t in range(NT):
                    pool.indirect_dma_start(xg_dram.rearrange("j p d -> (j p) d"),
                                            bass.IndirectOffsetOnAxis(ap=slot[:, k, t:t + 1], axis=0),
                                            xn[:, t, :], None).then_inc(s_sct, 16)

            def store(j, par):
                pool.wait_ge(s_yc, j + 1 + NT)
                pool.dma_start(yg_dram[bass.ds(j, 1)].rearrange("o p d -> (o p) d"), yo[:, par])\
                    .then_inc(s_yst[par], 16)

            pool.wait_ge(s_y, NT)
            pool.memset(va[:, :, :, HD:VW], 1.0).then_inc(s_one, 1)
            with pool.Fori(0, ST // 2) as i:
                for par in range(2):
                    store(i * 2 + par, par)
            store(ST - 1, 0)
            pool.wait_ge(s_yst[0], 16 * (ST - ST // 2))
            pool.wait_ge(s_yst[1], 16 * (ST // 2))
            for t in range(NT):
                if t >= 2:
                    pool.wait_ge(s_cmb, 2 * (t - 1))
                for k in range(2):
                    pool.indirect_dma_start(yk[:, t % 2, k, :], None, yg_dram.rearrange("j p d -> (j p) d"),
                                            bass.IndirectOffsetOnAxis(ap=slot[:, k, t:t + 1], axis=0))\
                        .then_inc(s_gat[t % 2], 16)

        def silu_step(act, n, par):
            act.wait_ge(s_gu, n + 1)
            act.activation(sg[:, par], pgu[par][:, 0:F], ACT.Silu).then_inc(s_sg, 1)

        @block.scalar
        def _(act):
            act.wait_ge(s_ln, LN_VAR)
            act.activation(rstd[:], rstd[:], ACT.Sqrt).then_inc(s_sd, 1)
            act.wait_ge(s_ln, LN_READY)
            for t in range(NT):
                act.activation(xn[:, t], x_sb[:, t], ACT.Identity, scale=rstd[:, t:t + 1], bias=nmr[:, t:t + 1])\
                    .then_inc(s_xn, 1)
            act.wait_ge(s_lg, 1)
            act.activation(score[:], prt[:, 0], ACT.Sigmoid).then_inc(s_sc, 1)
            for t in range(NT):
                if t >= 2:
                    act.wait_ge(s_hm, t - 1)
                silu_step(act, t, t % 2)

            def load(j, par):
                act.dma_start(xg[:, par], xg_dram[bass.ds(j, 1)].rearrange("o p d -> (o p) d"))\
                    .then_inc(s_ld[par], 16)

            def tile(j, par, more=True):
                act.wait_ge(s_xt, NT + 1 + j)
                act.wait_ge(s_gu, NT + j - 1)
                act.activation(xgT[:, par], pxt[par][:], ACT.Copy).then_inc(s_xtc, 1)
                if more:
                    load(j + 2, par)

            def silu(j, par):
                act.wait_ge(s_hm, NT + j - 1)
                silu_step(act, NT + j, par)

            act.wait_ge(s_sct, 16 * 2 * NT)
            load(0, 0)
            load(1, 1)
            tile(0, 0)
            silu(0, 0)
            tile(1, 1)
            with act.Fori(0, (ST - 5) // 2) as i:
                for m in range(2):
                    silu(i * 2 + (m + 1), (m + 1) % 2)
                    tile(i * 2 + (m + 2), m)
            for j in range(ST - 3, ST):
                silu(j - 1, (j - 1) % 2)
                tile(j, j % 2, more=(j < ST - 2))
            silu(ST - 1, 0)
            act.wait_ge(s_one, 1)
            for t in range(NT):
                act.wait_ge(s_vm, t + 1)
                if t >= 2:
                    act.wait_ge(s_vs[t % 2], 16 * (t // 2))
                act.activation(va[:, t % 2, :, 0:HD], pxt[t % 2][:].rearrange("p k c -> p (k c)")
                               .rearrange("p (h d) -> p h d", h=NH), ACT.Copy).then_inc(s_vc, 1)

        @block.vector
        def _(dve):
            for t in range(NT):
                dve.bn_stats(stats[:, t], x_sb[:, t]).then_inc(s_ln, 1)
            dve.wait_ge(s_ln, NT)
            for t in range(NT):
                dve.bn_aggr(mv[:, t], stats[:, t]).then_inc(s_ln, 1)
            dve.wait_ge(s_ln, 2 * NT)
            dve.tensor_scalar(rstd[:], mv[:, :, 1], EPS, None, ALU.add).then_inc(s_ln, 1)
            dve.wait_ge(s_sd, 1)
            dve.reciprocal(rstd[:], rstd[:]).then_inc(s_ln, 1)
            dve.wait_ge(s_ln, LN_RSTD)
            dve.scalar_tensor_tensor(nmr[:], mv[:, :, 0], -1.0, rstd[:], ALU.mult, ALU.mult).then_inc(s_ln, 1)
            dve.wait_ge(s_w, 16 * 7)
            dve.tensor_copy(tri[:, 0], lower[:]).then_inc(s_tri, 1)
            dve.memset(tri[:, 1], 1.0).then_inc(s_tri, 1)
            for t in range(NT):
                dve.wait_ge(s_xt, t + 1)
                dve.tensor_copy(xnT[:, :, t * P:(t + 1) * P], pxt[t % 2][:]).then_inc(s_xtc, 1)

            step = [0]

            def done(ins):
                step[0] += 1
                ins.then_inc(s_r, 1)
                dve.wait_ge(s_r, step[0])

            dve.wait_ge(s_sc, 1)
            done(dve.tensor_tensor(biased[:], score[:], bias[:].unsqueeze(1).broadcast_to([P, NT, NE]), ALU.add))
            for t in range(NT):
                last = dve.max(top8[:, t], biased[:, t])
            done(last)
            for t in range(NT):
                last = dve.max_index(idx8[:, t], top8[:, t], biased[:, t])
            done(last)
            done(dve.tensor_copy(idxf[:], idx8[:, :, 0:2]))
            for k in range(2):
                last = dve.tensor_tensor(onehot[:, k], iota[:, 0:NE].unsqueeze(1).broadcast_to([P, NT, NE]),
                                         idxf[:, :, k:k + 1].broadcast_to([P, NT, NE]), ALU.is_equal)
            done(last)
            done(dve.tensor_tensor(member[:], onehot[:, 0], onehot[:, 1], ALU.add))
            dve.wait_ge(s_cnt, 1)
            dve.memset(cum[:, 0], 0.0)
            done(dve.tensor_copy(tot[:], prt[:, 1]))
            for t in range(NT):
                done(dve.tensor_tensor(cum[:, t + 1], cum[:, t], tot[:, t], ALU.add))
            done(dve.tensor_scalar(cnti[:, 0], cum[:, NT], float(P - 1), None, ALU.add))
            done(dve.tensor_scalar(cnti[:, 1], cnti[:, 0], 7, None, ALU.logical_shift_right))
            done(dve.tensor_copy(cnt[:, 0], cnti[:, 1]))
            done(dve.memset(cnt[:, 3], 1.0))
            done(dve.tensor_tensor_scan(cnt[:, 1], cnt[:, 3], cnt[:, 0], 0.0, ALU.mult, ALU.add))
            done(dve.tensor_tensor(cnt[:, 2], cnt[:, 1], cnt[:, 0], ALU.subtract))
            done(dve.tensor_scalar(cnt[:, 2], cnt[:, 2], float(P), None, ALU.mult))
            done(dve.tensor_tensor(over[:], iota[:, 0:ST + 1].unsqueeze(2).broadcast_to([P, ST + 1, NE]),
                                   cnt[:, 1].unsqueeze(1).broadcast_to([P, ST + 1, NE]), ALU.is_ge))
            done(dve.tensor_reduce(ejf[:], over[:], AX.X, ALU.add))
            dve.tensor_scalar(ej[:], ejf[:], float(NE - 1), None, ALU.min).then_inc(s_ej, 1)
            dve.tensor_scalar(ends[:], cnt[:, 1], float(NT), None, ALU.add).then_inc(s_ej, 1)
            done(dve.tensor_tensor(pos[:], prt[:, 0], cum[:, 0:NT], ALU.add))
            done(dve.tensor_tensor(pos[:], pos[:], cnt[:, 2].unsqueeze(1).broadcast_to([P, NT, NE]), ALU.add))
            for k in range(2):
                dve.tensor_tensor(prod[:, k], onehot[:, k], pos[:], ALU.mult)
                last = dve.tensor_tensor(prod[:, 2 + k], onehot[:, k], score[:], ALU.mult)
            done(last)
            for k in range(2):
                dve.tensor_reduce(slotf[:, k], prod[:, k], AX.X, ALU.add)
                last = dve.tensor_reduce(sk[:, k], prod[:, 2 + k], AX.X, ALU.add)
            done(last)
            dve.tensor_copy(slot[:], slotf[:]).then_inc(s_slot, 1)
            done(dve.tensor_tensor(den[:], sk[:, 0], sk[:, 1], ALU.add))
            done(dve.tensor_scalar(den[:], den[:], 1e-20, None, ALU.add))
            done(dve.reciprocal(den[:], den[:]))
            for k in range(2):
                last = dve.scalar_tensor_tensor(wk[:, k], sk[:, k], tg[:, 0:1], den[:], ALU.mult, ALU.mult)
            done(last)

            def hidden(n, par):
                dve.wait_ge(s_sg, n + 1)
                if not (isinstance(n, int) and n < 2):
                    dve.wait_ge(s_ht, n - 1)
                dve.tensor_tensor(hm[:, par], sg[:, par], pgu[par][:, F:2 * F], ALU.mult).then_inc(s_hm, 1)

            def hidden_copy(n, par):
                dve.wait_ge(s_ht, n + 1)
                if not (isinstance(n, int) and n < 2):
                    dve.wait_ge(s_y, n - 1)
                dve.tensor_copy(hT[:, par], pht[:, 2 * par:2 * par + 2]).then_inc(s_htc, 1)

            def shared_out(t):
                dve.wait_ge(s_y, t + 1)
                dve.scalar_tensor_tensor(x_sb[:, t], pyo[t % 2][:], tg[:, 0:1], x_sb[:, t], ALU.mult, ALU.add)\
                    .then_inc(s_yc, 1)

            hidden(0, 0)
            for t in range(1, NT):
                hidden_copy(t - 1, (t - 1) % 2)
                hidden(t, t % 2)
                shared_out(t - 1)
            hidden_copy(NT - 1, 1)
            shared_out(NT - 1)

            def step_dve(i2, m, first=False):
                j = i2 + m
                hidden_copy(NT + j - 1, (m - 1) % 2)
                hidden(NT + j, m % 2)
                dve.wait_ge(s_y, NT + j)
                if not first:
                    dve.wait_ge(s_yst[(m - 1) % 2], i2 * 8 + ((m - 1) // 2) * 16)
                dve.tensor_copy(yo[:, (m - 1) % 2], pyo[(m - 1) % 2][:]).then_inc(s_yc, 1)

            hidden(NT, 0)
            step_dve(0, 1, True)
            step_dve(0, 2, True)
            with dve.Fori(1, ST // 2) as i:
                step_dve(i * 2, 1)
                step_dve(i * 2, 2)
            hidden_copy(NT + ST - 1, 0)
            dve.wait_ge(s_y, NT + ST)
            dve.wait_ge(s_yst[0], 16 * (ST // 2))
            dve.tensor_copy(yo[:, 0], pyo[0][:]).then_inc(s_yc, 1)
            for t in range(NT):
                dve.wait_ge(s_gat[t % 2], 32 * (t // 2 + 1))
                for k in range(2):
                    if k == 1:
                        dve.wait_ge(s_cmb, 2 * t + 1)
                    dve.scalar_tensor_tensor(x_sb[:, t], yk[:, t % 2, k], wk[:, k, t:t + 1], x_sb[:, t],
                                             ALU.mult, ALU.add).then_inc(s_cmb, 1)

        def logits_tile(pe, t):
            pe.wait_ge(s_xtc, t + 1)
            for k in range(KD):
                last = pe.matmul(prt[:, 0, t], xnT[:, k, t * P:(t + 1) * P], w_gate[:, k], start=(k == 0),
                                 stop=(k == KD - 1))
            return last

        @block.tensor
        def _(pe):
            pe.wait_ge(s_w, 16 * 7)
            for t in range(NT):
                pe.wait_ge(s_xn, t + 1)
                if t >= 2:
                    pe.wait_ge(s_xtc, t - 1)
                for k in range(KD):
                    last = pe.transpose(pxt[t % 2][:, k], xn[:, t, k * P:(k + 1) * P], ident[:])
                last.then_inc(s_xt, 1)
                if t >= 1:
                    logits_tile(pe, t - 1)
            logits_tile(pe, NT - 1).then_inc(s_lg, 1)

            def up(n, lhs, rhs, par):
                if not (isinstance(n, int) and n < 2):
                    pe.wait_ge(s_hm, n - 1)
                for k in range(KD):
                    last = pe.matmul(pgu[par][:], lhs(k), rhs(k), start=(k == 0), stop=(k == KD - 1))
                last.then_inc(s_gu, 1)

            def turn(n, par):
                pe.wait_ge(s_hm, n + 1)
                if not (isinstance(n, int) and n < 2):
                    pe.wait_ge(s_htc, n)
                for k in range(KF):
                    last = pe.transpose(pht[:, 2 * par + k], hm[:, par, k * P:(k + 1) * P], ident[:])
                last.then_inc(s_ht, 1)

            def down(n, rhs, par):
                pe.wait_ge(s_htc, n + 1)
                if not (isinstance(n, int) and n < 2):
                    pe.wait_ge(s_yc, n - 1)
                for k in range(KF):
                    last = pe.matmul(pyo[par][:], hT[:, par, k], rhs(k), start=(k == 0), stop=(k == KF - 1))
                last.then_inc(s_y, 1)

            def shared_up(t):
                up(t, lambda k: xnT[:, k, t * P:(t + 1) * P], lambda k: ws1[:, k], t % 2)

            pe.wait_ge(s_tri, 2)
            shared_up(0)
            shared_up(1)
            pe.wait_ge(s_r, 6)
            pe.matmul(prt[:, 0].rearrange("p t e -> p (t e)"), tri[:, 0], member[:].rearrange("p t e -> p (t e)"),
                      start=True, stop=True)
            pe.matmul(prt[:, 1].rearrange("p t e -> p (t e)"), tri[:, 1], member[:].rearrange("p t e -> p (t e)"),
                      start=True, stop=True, skip_group_check=True).then_inc(s_cnt, 1)
            turn(0, 0)
            for t in range(1, NT):
                if t >= 2:
                    shared_up(t)
                down(t - 1, lambda k: ws2[:, k], (t - 1) % 2)
                turn(t, t % 2)
            down(NT - 1, lambda k: ws2[:, k], 1)

            def fetch(j, par, nload):
                pe.wait_ge(s_ld[par], nload)
                if not (isinstance(j, int) and j < 2):
                    pe.wait_ge(s_xtc, NT + j - 1)
                for k in range(KD):
                    last = pe.transpose(pxt[par][:, k], xg[:, par, k * P:(k + 1) * P], ident[:])
                last.then_inc(s_xt, 1)

            def routed_up(j, par, e):
                pe.wait_ge(s_wr, e + 1)
                pe.wait_ge(s_xtc, NT + j + 1)
                up(NT + j, lambda k: xgT[:, par, k],
                   lambda k: w1[:, bass.ds(e % RING, 1), k].rearrange("p o f -> p (o f)"), par)

            def routed_down(j, par, e):
                down(NT + j, lambda k: w2[:, bass.ds(e % RING, 1), k].rearrange("p o f -> p (o f)"), par)

            def expert(j):
                return pe.value_load(ej[0:1, bass.ds(j, 1)], min_val=0, max_val=NE - 1)

            def step(i, m, before, e, last=False):
                turn(NT + i * 2 + (m - 1), (m - 1) % 2)
                routed_up(i * 2 + m, m % 2, e)
                if not last:
                    fetch(i * 2 + (m + 1), (m + 1) % 2, (i + (m + 1) // 2) * 16 + 16)
                routed_down(i * 2 + (m - 1), (m - 1) % 2, before)

            def pair(i, last=False):
                before, e1 = expert(i * 2), expert(i * 2 + 1)
                step(i, 1, before, e1)
                e2 = expert(i * 2 + 2)
                step(i, 2, e1, e2, last)

            fetch(0, 0, 16)
            pe.wait_ge(s_ej, 2)
            routed_up(0, 0, expert(0))
            fetch(1, 1, 16)
            with pe.Fori(0, (ST - 1) // 2 - 1) as i:
                pair(i)
            pair((ST - 1) // 2 - 1, last=True)
            e = expert(ST - 1)
            turn(NT + ST - 1, 0)
            routed_down(ST - 1, 0, e)
            pe.wait_ge(s_cx, 32)
            pe.wait_ge(s_xtc, NT + ST)
            for t in range(NT):
                if t >= 2:
                    pe.wait_ge(s_vc, t - 1)
                for k in range(KC):
                    last = pe.matmul(pxt[t % 2][:].rearrange("p k c -> p (k c)"), ctxT[:, k, t * P:(t + 1) * P],
                                     wv[:, k], start=(k == 0), stop=(k == KC - 1))
                last.then_inc(s_vm, 1)


NH, HD = 32, 16
G4 = 4
NG = B * NH // G4
SCALE = HD ** -0.5
TURN_HIGH = 6.28125
TURN_LOW = float(2 * np.pi - TURN_HIGH)
TWO_PI = float(2 * np.pi)
SIN_MAX = 3.1415925
MAGIC = 12582912.0
VW = HD + 1


def attention_inputs(nc, x_sb, ident, a, qk_dram):
    ITEMS = 2 * KD
    N = B * ITEMS
    with ExitStack() as ctx:
        def sb(name, shape, dt=F32):
            return ctx.enter_context(nc.sbuf_tensor("q_" + name, shape, dt))

        def sem(name):
            return ctx.enter_context(nc.semaphore("q_" + name))

        stats = sb("stats", [P, NT, 6])
        mv = sb("mv", [P, NT, 2])
        rstd = sb("rstd", [P, NT])
        nmr = sb("nmr", [P, NT])
        xn = sb("xn", [P, 2, D])
        xnT = sb("xnT", [P, KD, T])
        ctxT = sb("ctxT", [P, KC, T])
        wq = sb("wq", [P, KD, D])
        wk = sb("wk", [P, KC, D])
        posT = sb("posT", [2, T])
        freq = sb("freq", [2, P])
        swap = sb("swap", [P, P])
        sign = sb("sign", [P, 1])
        ang = sb("ang", [P, 2, T])
        turns = sb("turns", [P, 2, T])
        qs = sb("qs", [P, 4, L])
        t1 = sb("t1", [P, 4, L])
        t2 = sb("t2", [P, 4, L])
        qr = sb("qr", [P, 4, L])
        r1 = sb("r1", [P, 4, L])
        parts = sb("parts", [P, 4, 3, L], BF16)

        pxt = [ctx.enter_context(nc.psum_tensor(f"q_xt{i}", [P, KD, P], F32)) for i in range(2)]
        pq = [ctx.enter_context(nc.psum_tensor(f"q_q{i}", [P, L], F32)) for i in range(2)]
        pw = [ctx.enter_context(nc.psum_tensor(f"q_w{i}", [P, L], F32)) for i in range(2)]

        s_w0 = sem("tables_loaded")
        s_w = sem("weights_loaded")
        s_ln = sem("ln_steps")
        s_sd = sem("ln_std")
        s_xn = sem("normalised")
        s_xt = sem("x_transposed")
        s_xtc = sem("x_transposed_copied")
        s_ang = sem("angles")
        s_ar = sem("angles_read")
        s_a = sem("angle_steps")
        s_sin = sem("sines")
        s_tab = sem("tables_ready")
        s_qm = sem("projected")
        s_qc = sem("projection_copied")
        s_sw = sem("swapped")
        s_t1 = sem("cos_term")
        s_t2 = sem("sin_term")
        s_qr = sem("rotated")
        s_p1 = sem("part1")
        s_r1 = sem("rest1")
        s_p2 = sem("part2")
        s_p3 = sem("part3")
        s_ps = [sem(f"parts_stored{i}") for i in range(4)]

        block = ctx.enter_context(nc.Block())

        def late(n, k):
            return not isinstance(n, int) or n >= k

        @block.sync
        def _(sp):
            sp.dma_start(posT[:], a["posT"]).then_inc(s_w0, 16)
            sp.dma_start(freq[:], a["freq"]).then_inc(s_w0, 16)
            sp.dma_start(swap[:], a["swap"]).then_inc(s_w0, 16)
            sp.dma_start(sign[:], a["sign"]).then_inc(s_w0, 16)
            sp.dma_start(ctxT[:], a["ctxT"].rearrange("(k p) t -> p k t", p=P)).then_inc(s_w, 16)
            sp.dma_start(wk[:], a["wkv"][:, 0:D].rearrange("(k p) e -> p k e", p=P)).then_inc(s_w, 16)
            sp.dma_start(wq[:], a["wq"].rearrange("(k p) e -> p k e", p=P)).then_inc(s_w, 16)

            def store(i, m):
                n = i * ITEMS + m
                sp.wait_ge(s_p3, n + 1)
                dst = qk_dram[m % 2, :, bass.ds(i, 1), m // 2].rearrange("a o p t -> p (a o) t")
                sp.dma_start(dst, parts[:, m % 4]).then_inc(s_ps[m % 4], 16)

            with sp.Fori(0, B) as i:
                for m in range(ITEMS):
                    store(i, m)
            for r in range(4):
                sp.wait_ge(s_ps[r], 16 * N // 4)

        def run(eng, steps, lag):
            for m in range(ITEMS):
                steps(0, m)
            with eng.Fori(1, B) as i:
                for m in range(ITEMS):
                    steps(i, m)
            for m in range(lag):
                steps(B, m)

        def at(i, m, k):
            if m >= k:
                return (i, m - k) if not isinstance(i, int) or i < B else None
            if isinstance(i, int) and i == 0:
                return None
            return i - 1, m - k + ITEMS

        @block.gpsimd
        def _(pool):
            def steps(i, m):
                if it := at(i, m, 2):
                    n, r = it[0] * ITEMS + it[1], it[1] % 4
                    pool.wait_ge(s_p1, n + 1)
                    if late(n, 4):
                        pool.wait_ge(s_p3, n - 3)
                    pool.tensor_tensor(r1[:, r], qr[:, r], parts[:, r, 0], ALU.subtract).then_inc(s_r1, 1)
                if it := at(i, m, 3):
                    n, r = it[0] * ITEMS + it[1], it[1] % 4
                    pool.wait_ge(s_p2, n + 1)
                    pool.tensor_tensor(parts[:, r, 2], r1[:, r], parts[:, r, 1], ALU.subtract).then_inc(s_p3, 1)

            run(pool, steps, 3)

        @block.scalar
        def _(act):
            act.wait_ge(s_ln, LN_VAR)
            act.activation(rstd[:], rstd[:], ACT.Sqrt).then_inc(s_sd, 1)
            act.wait_ge(s_ln, LN_READY)

            def copy_turned(t):
                act.wait_ge(s_xt, t + 1)
                act.activation(xnT[:, :, t * P:(t + 1) * P], pxt[t % 2][:], ACT.Copy).then_inc(s_xtc, 1)

            for t in range(NT):
                if t >= 2:
                    act.wait_ge(s_xt, t - 1)
                act.activation(xn[:, t % 2], x_sb[:, t], ACT.Identity, scale=rstd[:, t:t + 1], bias=nmr[:, t:t + 1])\
                    .then_inc(s_xn, 1)
                if t >= 1:
                    copy_turned(t - 1)
            copy_turned(NT - 1)
            act.wait_ge(s_a, 5)
            act.activation(ang[:], ang[:], ACT.Sin).then_inc(s_sin, 1)

            def steps(i, m):
                if at(i, m, 0):
                    n = i * ITEMS + m
                    act.wait_ge(s_qm, n + 1)
                    if late(n, 4):
                        act.wait_ge(s_sw, n - 3)
                        act.wait_ge(s_t1, n - 3)
                    act.activation(qs[:, m % 4], pq[m % 2][:], ACT.Copy, scale=SCALE if m % 2 == 0 else 1.0)\
                        .then_inc(s_qc, 1)
                if it := at(i, m, 2):
                    n, r = it[0] * ITEMS + it[1], it[1] % 4
                    act.wait_ge(s_qr, n + 1)
                    if late(n, 4):
                        act.wait_ge(s_ps[r], 16 * (it[0] * 2 + it[1] // 4))
                    act.activation(parts[:, r, 0], qr[:, r], ACT.Copy).then_inc(s_p1, 1)
                if it := at(i, m, 3):
                    n, r = it[0] * ITEMS + it[1], it[1] % 4
                    act.wait_ge(s_r1, n + 1)
                    act.activation(parts[:, r, 1], r1[:, r], ACT.Copy).then_inc(s_p2, 1)

            run(act, steps, 3)

        @block.vector
        def _(dve):
            for t in range(NT):
                dve.bn_stats(stats[:, t], x_sb[:, t]).then_inc(s_ln, 1)
            dve.wait_ge(s_ln, NT)
            for t in range(NT):
                dve.bn_aggr(mv[:, t], stats[:, t]).then_inc(s_ln, 1)
            dve.wait_ge(s_ln, 2 * NT)
            dve.tensor_scalar(rstd[:], mv[:, :, 1], EPS, None, ALU.add).then_inc(s_ln, 1)
            dve.wait_ge(s_sd, 1)
            dve.reciprocal(rstd[:], rstd[:]).then_inc(s_ln, 1)
            dve.wait_ge(s_ln, LN_RSTD)
            dve.scalar_tensor_tensor(nmr[:], mv[:, :, 0], -1.0, rstd[:], ALU.mult, ALU.mult).then_inc(s_ln, 1)
            for b in range(B):
                dve.wait_ge(s_ang, b + 1)
                cols = slice(b * L, (b + 1) * L)
                dve.tensor_copy(ang[:, 1, cols], pw[b % 2][:])
                dve.tensor_scalar(ang[:, 0, cols], pw[b % 2][:], float(np.pi / 2), None, ALU.add).then_inc(s_ar, 1)
            dve.wait_ge(s_ar, B)
            dve.tensor_scalar(turns[:], ang[:], 1.0 / TWO_PI, MAGIC, ALU.mult, ALU.add).then_inc(s_a, 1)
            dve.wait_ge(s_a, 1)
            dve.tensor_scalar(turns[:], turns[:], MAGIC, None, ALU.subtract).then_inc(s_a, 1)
            dve.wait_ge(s_a, 2)
            dve.scalar_tensor_tensor(ang[:], turns[:], -TURN_HIGH, ang[:], ALU.mult, ALU.add).then_inc(s_a, 1)
            dve.wait_ge(s_a, 3)
            dve.scalar_tensor_tensor(ang[:], turns[:], -TURN_LOW, ang[:], ALU.mult, ALU.add).then_inc(s_a, 1)
            dve.wait_ge(s_a, 4)
            dve.tensor_scalar(ang[:], ang[:], SIN_MAX, -SIN_MAX, ALU.min, ALU.max).then_inc(s_a, 1)
            dve.wait_ge(s_sin, 1)
            dve.tensor_scalar(ang[:, 1], ang[:, 1], sign[:, 0:1], None, ALU.mult).then_inc(s_tab, 1)
            dve.wait_ge(s_tab, 1)

            def steps(i, m):
                if it := at(i, m, 0):
                    n = i * ITEMS + m
                    dve.wait_ge(s_qc, n + 1)
                    if late(n, 4):
                        dve.wait_ge(s_qr, n - 3)
                    dve.tensor_tensor(t1[:, m % 4], qs[:, m % 4], ang[:, 0, bass.ds(i * L, L)], ALU.mult)\
                        .then_inc(s_t1, 1)
                if it := at(i, m, 1):
                    n, r = it[0] * ITEMS + it[1], it[1] % 4
                    dve.wait_ge(s_sw, n + 1)
                    dve.tensor_tensor(t2[:, r], pw[r % 2][:], ang[:, 1, bass.ds(it[0] * L, L)], ALU.mult)\
                        .then_inc(s_t2, 1)
                    dve.wait_ge(s_t2, n + 1)
                    if late(n, 4):
                        dve.wait_ge(s_r1, n - 3)
                    dve.tensor_tensor(qr[:, r], t1[:, r], t2[:, r], ALU.add).then_inc(s_qr, 1)

            run(dve, steps, 1)

        @block.tensor
        def _(pe):
            pe.wait_ge(s_w0, 16 * 4)
            for b in range(B):
                if b >= 2:
                    pe.wait_ge(s_ar, b - 1)
                pe.matmul(pw[b % 2][:], freq[:], posT[:, b * L:(b + 1) * L], start=True, stop=True).then_inc(s_ang, 1)
            pe.wait_ge(s_w, 16 * 3)
            for t in range(NT):
                pe.wait_ge(s_xn, t + 1)
                if t >= 2:
                    pe.wait_ge(s_xtc, t - 1)
                for k in range(KD):
                    last = pe.transpose(pxt[t % 2][:, k], xn[:, t % 2, k * P:(k + 1) * P], ident[:])
                last.then_inc(s_xt, 1)
            pe.wait_ge(s_xtc, NT)
            pe.wait_ge(s_tab, 1)

            def steps(i, m):
                if at(i, m, 0):
                    n = i * ITEMS + m
                    ft = slice(m // 2 * P, (m // 2 + 1) * P)
                    if late(n, 2):
                        pe.wait_ge(s_qc, n - 1)
                    w, src, kn = (wq, xnT, KD) if m % 2 == 0 else (wk, ctxT, KC)
                    for k in range(kn):
                        last = pe.matmul(pq[m % 2][:], w[:, k, ft], src[:, k, bass.ds(i * L, L)], start=(k == 0),
                                         stop=(k == kn - 1))
                    last.then_inc(s_qm, 1)
                if it := at(i, m, 1):
                    n, r = it[0] * ITEMS + it[1], it[1] % 4
                    pe.wait_ge(s_qc, n + 1)
                    if late(n, 2):
                        pe.wait_ge(s_t2, n - 1)
                    pe.matmul(pw[r % 2][:], swap[:], qs[:, r], start=True, stop=True).then_inc(s_sw, 1)

            run(pe, steps, 1)


Q_PART = (0, 0, 1, 1, 0, 2)
K_PART = (0, 1, 0, 1, 2, 0)
KR = HD * len(Q_PART)
KM = KR + 3


def attention(nc, ident, identb, a, qk_dram, v_dram, m_dram, at_dram, wo, bo, w1, s_last):
    RG = 4
    with ExitStack() as ctx:
        def sb(name, shape, dt=F32):
            return ctx.enter_context(nc.sbuf_tensor("a_" + name, shape, dt))

        def sem(name):
            return ctx.enter_context(nc.semaphore("a_" + name))

        qs = sb("qs", [P, RG, G4, L], BF16)
        ks = sb("ks", [P, RG, G4, L], BF16)
        va = sb("va", [P, RG, TB, G4 * VW])
        pr = sb("pr", [P, 2, G4, TB, L])
        mx = sb("mx", [P, 2, G4 * TB])
        mr = sb("mr", [P, 2, G4 * TB])
        m3 = sb("m3", [P, 2, P // (G4 * TB), G4 * TB], BF16)
        mT = sb("mT", [3 * G4 * TB, 2, P], BF16)
        sel = sb("sel", [P, P])
        ones = sb("ones", [P, L])
        aT = sb("aT", [P, 2, L])
        rd = sb("rd", [P, 2, TB, G4])
        rw = sb("rw", [P, 2, TB, G4, 32])
        an = sb("an", [P, 2, L])

        psc = [ctx.enter_context(nc.psum_tensor(f"a_s{i}", [P, 2, L], F32)) for i in range(2)]
        pst = [ctx.enter_context(nc.psum_tensor(f"a_t{i}", [P, L], F32)) for i in range(2)]
        ppv = ctx.enter_context(nc.psum_tensor("a_pv", [P, L], F32))
        pmi = ctx.enter_context(nc.psum_tensor("a_mi", [P, L], F32))
        pmt = pmi[:].bitcast(BF16)[:, 0:P]

        s_sel = sem("sel_loaded")
        s_one = sem("ones_and_zeros_set")
        s_ld = [sem(f"operands_loaded{i}") for i in range(RG)]
        s_lv = [sem(f"values_loaded{i}") for i in range(RG)]
        s_s = sem("scores_by_query")
        s_mx = sem("maxima")
        s_n = sem("minus_max_parts")
        s_mt = sem("maxima_transposed")
        s_mc = sem("maxima_copied")
        s_md = sem("maxima_in_dram")
        s_mq = [sem(f"maxima_loaded{i}") for i in range(RG)]
        s_t = sem("scores_by_key")
        s_e = sem("exps")
        s_pv = sem("values_summed")
        s_pc = sem("values_copied")
        s_d = sem("denominators")
        s_r = sem("reciprocals")
        s_rw = sem("reciprocals_repeated")
        s_w = sem("reciprocals_spread")
        s_a = sem("normalised")
        s_o = [sem(f"stored{i}") for i in range(2)]

        block = ctx.enter_context(nc.Block())

        def no(i, r):
            return i * RG + r

        def after(i, r, k):
            return not isinstance(i, int) or no(i, r) >= k

        def run(eng, step):
            for r in range(RG):
                step(0, r)
            with eng.Fori(1, NG // RG - 1) as i:
                for r in range(RG):
                    step(i, r)
            for r in range(RG):
                step(NG // RG - 1, r)

        def inside(i, r):
            return not isinstance(i, int) or 0 <= no(i, r) < NG

        @block.sync
        def _(sp):
            sp.dma_start(sel[:], a["sel"]).then_inc(s_sel, 16)

            def load_qk(i, r):
                g = no(i, r)
                if after(i, r, RG):
                    sp.wait_ge(s_t, 16 * (g - RG + 1))
                for j, (qp, kp) in enumerate(zip(Q_PART, K_PART)):
                    rows = slice(j * HD, (j + 1) * HD)
                    for m, (dst, part) in enumerate(((qs, qp), (ks, kp))):
                        src = qk_dram[m, part].rearrange("b f (h d) t -> (b f h) d t", d=HD)[bass.ds(g * G4, G4)]
                        sp.dma_start(dst[rows, r % RG], src.rearrange("h d t -> d h t")).then_inc(s_ld[r % RG], 16)

            def load_v(i, r):
                g = no(i, r)
                if after(i, r, RG):
                    sp.wait_ge(s_pv, g - RG + 1)
                sp.dma_start(va[:, r % RG], v_dram[bass.ds(g, 1)].rearrange("o p k c -> p (o k) c"))\
                    .then_inc(s_lv[r % RG], 16)

            def maxima(i, r):
                g = no(i, r)
                sp.wait_ge(s_mc, g + 1)
                sp.dma_start(m_dram[bass.ds(g, 1)].rearrange("o r c -> (o r) c"), mT[:, r % 2]).then_inc(s_md, 16)
                sp.wait_ge(s_md, 16 * g + 16)
                sp.dma_start(qs[KR:KM, r % RG].rearrange("a h t -> a (h t)"),
                             m_dram[bass.ds(g, 1)].rearrange("o (a r) c -> (o a) (r c)", a=3))\
                    .then_inc(s_mq[r % RG], 16)

            def step(i, r):
                if inside(i, r + 3):
                    load_qk(i, r + 3)
                if inside(i, r + 1):
                    load_v(i, r + 1)
                    if after(i, r, 1):
                        maxima(i, r + 1)

            for g in range(3):
                load_qk(0, g)
            load_v(0, 0)
            for g in range(2):
                maxima(0, g)
            sp.dma_start(wo[:], a["wo"].rearrange("(k p) e -> p k e", p=P)).then_inc(s_last, 16)
            sp.dma_start(bo[:], a["bo"].partition_broadcast(P)).then_inc(s_last, 16)
            sp.dma_start(w1[:], a["w1T"].rearrange("(k p) e -> p k e", p=P)).then_inc(s_last, 16)
            run(sp, step)

        @block.gpsimd
        def _(pool):
            pool.memset(ks[KR:P, :, :, :], 1.0).then_inc(s_one, 1)
            pool.wait_ge(s_one, 3)
            pool.memset(ones[:], 1.0).then_inc(s_one, 1)
            pool.wait_ge(s_one, 4)

            def repeat(i, r):
                g = no(i, r)
                pool.wait_ge(s_r, g + 1)
                if after(i, r, 2):
                    pool.wait_ge(s_w, g - 1)
                pool.tensor_tensor(rw[:, r % 2], rd[:, r % 2].unsqueeze(3).broadcast_to([P, TB, G4, 32]),
                                   ones[:].rearrange("p (t h c) -> p t h c", t=TB, h=G4), ALU.mult).then_inc(s_rw, 1)

            def step(i, r):
                g, r2 = no(i, r), r % 2
                repeat(i, r)
                pool.wait_ge(s_a, g + 1)
                for j in range(G4):
                    dst = at_dram.rearrange("b (h d) t -> (b h) d t", d=HD)[bass.ds(g * G4 + j, 1)]
                    pool.dma_start(dst.rearrange("o d t -> (o d) t"), an[32 * j:32 * j + HD, r2])\
                        .then_inc(s_o[r2], 16)

            run(pool, step)
            for r2 in range(2):
                pool.wait_ge(s_o[r2], 64 * NG // 2)

        @block.scalar
        def _(act):
            def copy_max(i, r):
                g = no(i, r)
                act.wait_ge(s_mt, g + 1)
                if after(i, r, 2):
                    act.wait_ge(s_md, 16 * (g - 1))
                act.activation(mT[:, r % 2], pmt[0:3 * G4 * TB], ACT.Copy).then_inc(s_mc, 1)

            def exps(i, r, h):
                g = no(i, r)
                for kt in range(TB):
                    act.wait_ge(s_t, g * 16 + (h * TB + kt + 1))
                    if h == 0 and kt == 0 and after(i, r, 2):
                        act.wait_ge(s_pv, g - 1)
                    act.activation(pr[:, r % 2, h, kt], pst[kt % 2][:], ACT.Exp).then_inc(s_e, 1)

            def copy_values(i, r):
                g = no(i, r)
                act.wait_ge(s_pv, g + 1)
                if after(i, r, 2):
                    act.wait_ge(s_d, g - 1)
                    act.wait_ge(s_a, g - 1)
                act.activation(aT[:, r % 2], ppv[:], ACT.Copy).then_inc(s_pc, 1)

            def step(i, r):
                for h in range(G4):
                    exps(i, r, h)
                    if h == 0 and after(i, r, 1) and inside(i, r + 1):
                        copy_max(i, r + 1)
                if after(i, r, 1):
                    copy_values(i, r - 1)

            copy_max(0, 0)
            copy_max(0, 1)
            run(act, step)
            copy_values(NG // RG, -1)

        @block.vector
        def _(dve):
            dve.memset(m3[:], 0.0).then_inc(s_one, 1)
            dve.memset(ppv[:], 0.0).then_inc(s_one, 1)
            dve.wait_ge(s_one, 3)

            def maxes(i, r, h):
                g = no(i, r)
                for c in range(2):
                    dve.wait_ge(s_s, g * 8 + (h * 2 + c + 1))
                    dve.tensor_reduce(mx[:, r % 2, h * TB + 2 * c:h * TB + 2 * c + 2], psc[c][:], AX.X, ALU.max)\
                        .then_inc(s_mx, 1)

            def split(i, r):
                g, r2 = no(i, r), r % 2
                dve.wait_ge(s_mx, g * 8 + 8)
                if after(i, r, 2):
                    dve.wait_ge(s_mt, g - 1)
                dve.tensor_scalar(m3[:, r2, 0], mx[:, r2], -1.0, None, ALU.mult).then_inc(s_n, 1)
                dve.wait_ge(s_n, g * 4 + 1)
                dve.scalar_tensor_tensor(mr[:, r2], mx[:, r2], -1.0, m3[:, r2, 0], ALU.mult, ALU.subtract)\
                    .then_inc(s_n, 1)
                dve.wait_ge(s_n, g * 4 + 2)
                dve.tensor_copy(m3[:, r2, 1], mr[:, r2]).then_inc(s_n, 1)
                dve.wait_ge(s_n, g * 4 + 3)
                dve.tensor_tensor(m3[:, r2, 2], mr[:, r2], m3[:, r2, 1], ALU.subtract).then_inc(s_n, 1)

            def recip(i, r):
                g = no(i, r)
                dve.wait_ge(s_d, g + 1)
                if after(i, r, 2):
                    dve.wait_ge(s_rw, g - 1)
                dve.reciprocal(rd[:, r % 2], pmi[:, 0:TB * G4].rearrange("p (t h) -> p t h", h=G4)).then_inc(s_r, 1)

            def normalise(i, r):
                g, r2 = no(i, r), r % 2
                dve.wait_ge(s_w, g + 1)
                if after(i, r, 2):
                    dve.wait_ge(s_o[r2], 64 * (i * (RG // 2) + r // 2))
                dve.tensor_tensor(an[:, r2], aT[:, r2], pmi[:], ALU.mult).then_inc(s_a, 1)

            def step(i, r):
                for h in range(G4):
                    if inside(i, r + 2):
                        maxes(i, r + 2, h)
                    if h == 1 and after(i, r, 2):
                        recip(i, r - 2)
                    if h == 2 and after(i, r, 2):
                        normalise(i, r - 2)
                if inside(i, r + 2):
                    split(i, r + 2)

            for g in range(2):
                for h in range(G4):
                    maxes(0, g, h)
                split(0, g)
            run(dve, step)
            for r in (-2, -1):
                recip(NG // RG, r)
                normalise(NG // RG, r)

        @block.tensor
        def _(pe):
            pe.wait_ge(s_sel, 16)

            def scores(i, r, h, c):
                g, ring = no(i, r), r % RG
                if h == 0 and c == 0:
                    pe.wait_ge(s_ld[ring], (i + r // RG) * 192 + 192)
                if h >= 1 or after(i, r, 1):
                    pe.wait_ge(s_mx, g * 8 + (h * 2 + c - 1))
                for q in range(2):
                    qt = 2 * c + q
                    last = pe.matmul(psc[c][:, q], qs[0:KR, ring, h, qt * P:(qt + 1) * P], ks[0:KR, ring, h],
                                     start=True, stop=True)
                last.then_inc(s_s, 1)

            def turn(i, r):
                g = no(i, r)
                pe.wait_ge(s_n, g * 4 + 4)
                if after(i, r, 1):
                    pe.wait_ge(s_mc, g)
                if after(i, r, 4):
                    pe.wait_ge(s_a, g - 3)
                pe.transpose(pmt, m3[:, r % 2].rearrange("p a c -> p (a c)"), identb[:]).then_inc(s_mt, 1)

            def by_key(i, r, h, kt):
                g, ring = no(i, r), r % RG
                if h == 0 and kt == 0:
                    pe.wait_ge(s_mq[ring], (i + r // RG) * 16 + 16)
                if h >= 1 or kt >= 2 or after(i, r, 1):
                    pe.wait_ge(s_e, g * 16 + (h * TB + kt - 1))
                pe.matmul(pst[kt % 2][:], ks[0:KM, ring, h, kt * P:(kt + 1) * P], qs[0:KM, ring, h],
                          start=True, stop=True).then_inc(s_t, 1)

            def values(i, r, kt):
                g, ring = no(i, r), r % RG
                if kt == 0:
                    pe.wait_ge(s_lv[ring], (i + r // RG) * 16 + 16)
                    pe.wait_ge(s_e, g * 16 + 16)
                    if after(i, r, 1):
                        pe.wait_ge(s_pc, g)
                for h in range(G4):
                    last = pe.matmul(ppv[32 * h:32 * h + VW], va[:, ring, kt, h * VW:(h + 1) * VW],
                                     pr[:, r % 2, h, kt], start=(kt == 0), stop=(kt == TB - 1),
                                     tile_position=(0, 32 * h))
                if kt == TB - 1:
                    last.then_inc(s_pv, 1)

            def denominators(i, r):
                g = no(i, r)
                pe.wait_ge(s_pc, g + 1)
                pe.wait_ge(s_mc, min(g + 4, NG) if isinstance(g, int) else g + 4)
                if after(i, r, 1):
                    pe.wait_ge(s_a, g)
                for t in range(TB):
                    last = pe.matmul(pmi[:, t * G4:(t + 1) * G4], aT[:, r % 2, t * P:(t + 1) * P],
                                     sel[:, 0:P:32], start=True, stop=True, skip_group_check=True)
                last.then_inc(s_d, 1)

            def spread(i, r):
                pe.wait_ge(s_rw, no(i, r) + 1)
                for t in range(TB):
                    last = pe.matmul(pmi[:, t * P:(t + 1) * P], rw[:, r % 2, t].rearrange("p h c -> p (h c)"),
                                     ident[:], start=True, stop=True, skip_group_check=True)
                last.then_inc(s_w, 1)

            def step(i, r):
                for h in range(G4):
                    for kt in range(TB):
                        by_key(i, r, h, kt)
                        if kt == 1 and after(i, r, 1):
                            values(i, r - 1, h)
                        if kt % 2 == 0 and inside(i, r + 2):
                            scores(i, r + 2, h, kt // 2)
                    if h == 0 and after(i, r, 1) and inside(i, r + 1):
                        turn(i, r + 1)
                    if h == 1 and after(i, r, 2):
                        denominators(i, r - 2)
                    if h == 2 and after(i, r, 2):
                        spread(i, r - 2)

            for g in range(2):
                for h in range(G4):
                    for c in range(2):
                        scores(0, g, h, c)
                if g == 0:
                    pe.wait_ge(s_one, 4)
                turn(0, g)
            run(pe, step)
            for kt in range(TB):
                values(NG // RG, -1, kt)
            for r in (-2, -1):
                denominators(NG // RG, r)
                spread(NG // RG, r)


FF = 2048
KH = FF // P
QMAX, QMIN = 127.0, -128.0


def attention_out_and_ffn(nc, x_sb, ident, identb, tg, a, wo, bo, w1, s_w, at_dram, out):
    with ExitStack() as ctx:
        def sb(name, shape, dt=F32):
            return ctx.enter_context(nc.sbuf_tensor("f_" + name, shape, dt))

        def sem(name):
            return ctx.enter_context(nc.semaphore("f_" + name))

        at = sb("at", [P, 2, KD, L])
        w2 = sb("w2", [P, KH, D])
        w1q = sb("w1q", [P, KD, FF], BF16)
        w2q = sb("w2q", [P, KH, D], BF16)
        ones = sb("ones", [P, P])
        ssq = sb("ssq", [P, 2])
        sd = sb("sd", [P, 2])
        rms = sb("rms", [P, 2])
        back = sb("back", [P, 2])
        stats = sb("stats", [P, NT, 6])
        mv = sb("mv", [P, NT, 2])
        rstd = sb("rstd", [P, NT])
        nmr = sb("nmr", [P, NT])
        xn = w1[:].rearrange("p k (t d) -> p (k t) d", d=D)
        am = sb("am", [P, NT + 2])
        c1r = sb("c1r", [P, 2])
        sc = sb("sc", [P, NT])
        magic = sb("magic", [P, 2])
        xq = w2[:].rearrange("p t d -> p (t d)").bitcast(BF16)[:, 0:NT * D].rearrange("p (t d) -> p t d", d=D)
        xqT = sb("xqT", [P, KD, T], BF16)
        h = sb("h", [P, 2, FF])
        am2 = sb("am2", [P, 2, 1])
        sc2 = sb("sc2", [P, 2, 1])
        c2 = sb("c2", [P, 2, 1])
        hq = sb("hq", [P, 2, FF], BF16)
        hqT = sb("hqT", [P, 2, KH, P], BF16)

        pup = [ctx.enter_context(nc.psum_tensor(f"f_u{i}", [P, 2, L], F32)) for i in range(2)]
        pht = ctx.enter_context(nc.psum_tensor("f_t", [P, KH, P], BF16))
        pdn = [ctx.enter_context(nc.psum_tensor(f"f_d{i}", [P, D], F32)) for i in range(2)]

        s_w2 = sem("w2_loaded")
        s_at = [sem(f"attention_loaded{i}") for i in range(2)]
        s_c = sem("constants_set")
        s_xb = sem("bias_added")
        s_po = sem("attention_projected")
        s_xa = sem("attention_added")
        s_sq = sem("squares_summed")
        s_ms = sem("mean_squares")
        s_sd = sem("weight_std")
        s_k = sem("scale_steps")
        s_q = sem("weight_rounding")
        s_ln = sem("ln_steps")
        s_lsd = sem("ln_std")
        s_inv = sem("ln_columns")
        s_xn = sem("normalised")
        s_am = sem("token_scale_steps")
        s_c1 = sem("first_scale")
        s_xs = sem("x_scaled")
        s_xq = sem("x_rounded")
        s_xt = sem("x_transposed")
        s_xtc = sem("x_transposed_copied")
        s_up = sem("up_done")
        s_h = sem("gelu_done")
        s_a2 = sem("hidden_scale_steps")
        s_v = sem("hidden_scaled")
        s_cl = sem("hidden_clamped")
        s_hq = sem("hidden_rounded")
        s_ht = sem("hidden_transposed")
        s_htc = sem("hidden_copied")
        s_dn = sem("down_done")
        s_x = sem("x_ready")
        s_o = sem("stored")

        SEQ = 2 * TB + 1
        RMS_AT = 6

        block = ctx.enter_context(nc.Block())

        def run(eng, step, lag):
            for i in range(lag // 2 + 1):
                for r in range(2):
                    step(i, r)
            with eng.Fori(lag // 2 + 1, NT // 2) as i:
                for r in range(2):
                    step(i, r)
            for i in range(NT // 2, NT // 2 + lag // 2):
                for r in range(2):
                    step(i, r)

        def has(i, r, k):
            return not isinstance(i, int) or 0 <= i * 2 + r - k < NT


        @block.sync
        def _(sp):
            for b in range(2):
                sp.dma_start(at[:, b], at_dram[b].rearrange("(k p) t -> p k t", p=P)).then_inc(s_at[b], 16)
            sp.dma_start(w2[:], a["w2T"].rearrange("(k p) e -> p k e", p=P)).then_inc(s_w2, 16)
            for b in range(2, B):
                sp.wait_ge(s_po, TB * (b - 1))
                sp.dma_start(at[:, b % 2], at_dram[b].rearrange("(k p) t -> p k t", p=P)).then_inc(s_at[b % 2], 16)

            with sp.Fori(0, NT) as t:
                sp.wait_ge(s_x, t + 1)
                sp.dma_start(out.rearrange("(t p) d -> t p d", p=P)[bass.ds(t, 1)].rearrange("o p d -> (o p) d"),
                             x_sb[:, bass.ds(t, 1), :].rearrange("p o d -> p (o d)")).then_inc(s_o, 16)
            sp.wait_ge(s_o, 16 * NT)

        @block.gpsimd
        def _(pool):
            pool.memset(ones[:], 1.0).then_inc(s_c, 1)
            pool.memset(magic[:, 0:1], MAGIC).then_inc(s_c, 1)
            pool.memset(magic[:, 1:2], -MAGIC).then_inc(s_c, 1)
            pool.wait_ge(s_k, 1)
            for t in range(NT):
                pool.tensor_tensor(x_sb[:, t], x_sb[:, t], bo[:], ALU.add).then_inc(s_xb, 1)

        @block.scalar
        def _(act):
            act.wait_ge(s_w, 48)
            act.activation(w1q[:], w1[:], ACT.Square, accum_out=ssq[:, 0:1]).then_inc(s_sq, 1)
            act.wait_ge(s_w2, 16)
            act.activation(w2q[:], w2[:], ACT.Square, accum_out=ssq[:, 1:2]).then_inc(s_sq, 1)
            act.wait_ge(s_k, 2)
            act.activation(sd[:], sd[:], ACT.Sqrt).then_inc(s_sd, 1)
            act.wait_ge(s_k, 3)
            act.wait_ge(s_c, 3)
            for n, (w, wq) in enumerate(((w1, w1q), (w2, w2q))):
                act.activation(w[:], w[:], ACT.Identity, scale=rms[:, n:n + 1], bias=magic[:, 0:1]).then_inc(s_q, 1)
                act.wait_ge(s_q, 2 * n + 1)
                act.activation(wq[:], w[:], ACT.Sign, bias=magic[:, 1:2]).then_inc(s_q, 1)
            def normalise(b):
                for t in range(b * TB, (b + 1) * TB):
                    act.activation(xn[:, t], x_sb[:, t], ACT.Identity, scale=rstd[:, t:t + 1], bias=nmr[:, t:t + 1])\
                        .then_inc(s_xn, 1)

            def scale(b):
                act.wait_ge(s_am, 4 * b + 4)
                for t in range(b * TB, (b + 1) * TB):
                    act.activation(xn[:, t], xn[:, t], ACT.Identity, scale=sc[:, t:t + 1], bias=magic[:, 0:1])\
                        .then_inc(s_xs, 1)

            def copy_x(b):
                for t in range(b * TB, (b + 1) * TB):
                    act.wait_ge(s_xt, t + 1)
                    act.activation(xqT[:, :, t * P:(t + 1) * P],
                                   pht[:, KH // 2 * (t % 2):KH // 2 * (t % 2) + KD], ACT.Copy).then_inc(s_xtc, 1)

            act.wait_ge(s_ln, SEQ * B)
            act.activation(rstd[:], rstd[:], ACT.Sqrt).then_inc(s_lsd, 1)
            act.wait_ge(s_inv, 2)
            for b in range(B + 2):
                if b < B:
                    normalise(b)
                if 1 <= b <= B:
                    scale(b - 1)
                if b >= 2:
                    copy_x(b - 2)

            def step(i, r):
                t, v, u = i * 2 + r, i * 2 + (r - 1), i * 2 + (r - 2)
                if has(i, r, 2):
                    act.wait_ge(s_ht, u + 1)
                    if has(i, r, 4):
                        act.wait_ge(s_dn, u - 1)
                    act.activation(hqT[:, r], pht[:], ACT.Copy).then_inc(s_htc, 1)
                if has(i, r, 1):
                    act.wait_ge(s_a2, v * 5 + 4)
                    act.activation(h[:, 1 - r], h[:, 1 - r], ACT.Identity, scale=sc2[:, 1 - r], bias=magic[:, 0:1])\
                        .then_inc(s_v, 1)
                if has(i, r, 0):
                    for c in range(2):
                        act.wait_ge(s_c1, t + 1)
                        act.wait_ge(s_up, t * 2 + (c + 1))
                        if c == 0 and has(i, r, 2):
                            act.wait_ge(s_hq, t - 1)
                        act.activation(h[:, r, c * 2 * L:(c + 1) * 2 * L], pup[c][:].rearrange("p a l -> p (a l)"),
                                       ACT.Gelu, scale=c1r[:, r:r + 1]).then_inc(s_h, 1)

            run(act, step, 2)

        @block.vector
        def _(dve):
            dve.wait_ge(s_w, 48)
            dve.tensor_scalar(bo[:], bo[:], tg[:, 0:1], None, ALU.mult).then_inc(s_k, 1)
            dve.memset(am[:, NT:NT + 2], 1.0)

            def add(t):
                dve.wait_ge(s_po, t + 1)
                dve.wait_ge(s_xb, t + 1)
                dve.scalar_tensor_tensor(x_sb[:, t], pdn[t % 2][:], tg[:, 0:1], x_sb[:, t], ALU.mult, ALU.add)\
                    .then_inc(s_xa, 1)

            def weight_rms():
                dve.wait_ge(s_ms, 1)
                dve.tensor_scalar(sd[:], pup[0][:, 0, 0:2], 1.0 / (D * FF), EPS, ALU.mult, ALU.max).then_inc(s_k, 1)
                dve.wait_ge(s_sd, 1)
                dve.reciprocal(rms[:], sd[:]).then_inc(s_k, 1)
                dve.tensor_scalar(back[:], sd[:], 1.0 / QMAX, None, ALU.mult).then_inc(s_k, 1)
                dve.wait_ge(s_k, 4)
                dve.tensor_scalar(back[:, 1:2], back[:, 1:2], tg[:, 1:2], None, ALU.mult).then_inc(s_k, 1)

            def variance(b):
                tiles = range(b * TB, (b + 1) * TB)
                dve.wait_ge(s_xa, (b + 1) * TB)
                for t in tiles:
                    dve.bn_stats(stats[:, t], x_sb[:, t]).then_inc(s_ln, 1)
                dve.wait_ge(s_ln, SEQ * b + TB)
                for t in tiles:
                    dve.bn_aggr(mv[:, t], stats[:, t]).then_inc(s_ln, 1)
                dve.wait_ge(s_ln, SEQ * b + 2 * TB)
                cols = slice(b * TB, (b + 1) * TB)
                dve.tensor_scalar(rstd[:, cols], mv[:, cols, 1], EPS, None, ALU.add).then_inc(s_ln, 1)

            def scales(b):
                for t in range(b * TB, (b + 1) * TB):
                    dve.wait_ge(s_xn, t + 1)
                    last = dve.tensor_reduce(am[:, t:t + 1], xn[:, t], AX.X, ALU.max, apply_absolute_value=True)
                last.then_inc(s_am, 1)
                cols = slice(b * TB, (b + 1) * TB)
                dve.wait_ge(s_am, 4 * b + 1)
                dve.tensor_scalar(am[:, cols], am[:, cols], EPS, None, ALU.max).then_inc(s_am, 1)
                dve.wait_ge(s_am, 4 * b + 2)
                dve.reciprocal(sc[:, cols], am[:, cols]).then_inc(s_am, 1)
                dve.wait_ge(s_am, 4 * b + 3)
                dve.tensor_scalar(sc[:, cols], sc[:, cols], QMAX, None, ALU.mult).then_inc(s_am, 1)

            def rounded(b):
                tiles = range(b * TB, (b + 1) * TB)
                for t in tiles:
                    dve.wait_ge(s_xs, t + 1)
                    dve.tensor_scalar(xn[:, t], xn[:, t], MAGIC + QMAX, MAGIC + QMIN, ALU.min, ALU.max).then_inc(s_xq, 1)
                for k, t in enumerate(tiles):
                    dve.wait_ge(s_xq, 2 * TB * b + k + 1)
                    dve.tensor_scalar(xq[:, t], xn[:, t], MAGIC, None, ALU.subtract).then_inc(s_xq, 1)

            for b in range(B):
                for t in range(b * TB, (b + 1) * TB):
                    add(t)
                    if t == RMS_AT:
                        weight_rms()
                if b >= 1:
                    variance(b - 1)
            variance(B - 1)
            dve.wait_ge(s_lsd, 1)
            dve.reciprocal(rstd[:], rstd[:]).then_inc(s_inv, 1)
            dve.wait_ge(s_inv, 1)
            dve.scalar_tensor_tensor(nmr[:], mv[:, :, 0], -1.0, rstd[:], ALU.mult, ALU.mult).then_inc(s_inv, 1)
            for b in range(B + 1):
                if b < B:
                    scales(b)
                if b >= 1:
                    rounded(b - 1)
            dve.wait_ge(s_k, 5)
            dve.tensor_scalar(c1r[:], am[:, 0:2], back[:, 0:1], None, ALU.mult).then_inc(s_c1, 2)

            def step(i, r):
                t, v, u = i * 2 + r, i * 2 + (r - 1), i * 2 + (r - 2)
                if has(i, r, 1):
                    q = 1 - r
                    dve.wait_ge(s_v, v + 1)
                    dve.tensor_scalar(h[:, q], h[:, q], MAGIC + QMAX, MAGIC + QMIN, ALU.min, ALU.max).then_inc(s_cl, 1)
                    dve.wait_ge(s_cl, v + 1)
                    if has(i, r, 3):
                        dve.wait_ge(s_ht, v - 1)
                    dve.tensor_scalar(hq[:, q], h[:, q], MAGIC, None, ALU.subtract).then_inc(s_hq, 1)
                if has(i, r, 2):
                    dve.wait_ge(s_dn, u + 1)
                    xt = x_sb[:, bass.ds(u, 1), :].rearrange("p o d -> p (o d)")
                    dve.scalar_tensor_tensor(xt, pdn[r][:], c2[:, r], xt, ALU.mult, ALU.add).then_inc(s_x, 1)
                if has(i, r, 0):
                    dve.wait_ge(s_h, t * 2 + 2)
                    if has(i, r, -2):
                        dve.tensor_tensor(c1r[:, r:r + 1], am[:, bass.ds(t + 2, 1)], back[:, 0:1], ALU.mult)\
                            .then_inc(s_c1, 1)
                    if has(i, r, 2):
                        dve.wait_ge(s_v, t - 1)
                    dve.tensor_reduce(am2[:, r], h[:, r], AX.X, ALU.max, apply_absolute_value=True).then_inc(s_a2, 1)
                    dve.wait_ge(s_a2, t * 5 + 1)
                    dve.tensor_scalar(am2[:, r], am2[:, r], EPS, None, ALU.max).then_inc(s_a2, 1)
                    dve.wait_ge(s_a2, t * 5 + 2)
                    dve.reciprocal(sc2[:, r], am2[:, r]).then_inc(s_a2, 1)
                    dve.wait_ge(s_a2, t * 5 + 3)
                    dve.tensor_scalar(sc2[:, r], sc2[:, r], QMAX, None, ALU.mult).then_inc(s_a2, 1)
                    if has(i, r, 2):
                        dve.wait_ge(s_x, t - 1)
                    dve.tensor_scalar(c2[:, r], am2[:, r], back[:, 1:2], None, ALU.mult).then_inc(s_a2, 1)

            run(dve, step, 2)

        @block.tensor
        def _(pe):
            pe.wait_ge(s_w, 48)
            pe.wait_ge(s_c, 3)
            for t in range(NT):
                b = t // TB
                if t % TB == 0:
                    pe.wait_ge(s_at[b % 2], 16 * (b // 2 + 1))
                if t >= 2:
                    pe.wait_ge(s_xa, t - 1)
                for k in range(KD):
                    last = pe.matmul(pdn[t % 2][:], at[:, b % 2, k, (t % TB) * P:(t % TB + 1) * P], wo[:, k],
                                     start=(k == 0), stop=(k == KD - 1))
                last.then_inc(s_po, 1)
                if t == RMS_AT:
                    pe.wait_ge(s_sq, 2)
                    pe.matmul(pup[0][:, 0, 0:2], ones[:], ssq[:], start=True, stop=True).then_inc(s_ms, 1)
            for t in range(NT):
                pe.wait_ge(s_xq, 2 * TB * (t // TB) + TB + t % TB + 1)
                if t >= 2:
                    pe.wait_ge(s_xtc, t - 1)
                for k in range(KD):
                    last = pe.transpose(pht[:, KH // 2 * (t % 2) + k], xq[:, t, k * P:(k + 1) * P], identb[:])
                last.then_inc(s_xt, 1)
            pe.wait_ge(s_xtc, NT)

            def step(i, r):
                t, u = i * 2 + r, i * 2 + (r - 2)
                if has(i, r, 2):
                    pe.wait_ge(s_hq, u + 1)
                    if has(i, r, 3):
                        pe.wait_ge(s_htc, u)
                    for k in range(KH):
                        last = pe.transpose(pht[:, k], hq[:, r, k * P:(k + 1) * P], identb[:])
                    last.then_inc(s_ht, 1)
                if has(i, r, 0):
                    for c in range(2):
                        if has(i, r, 1):
                            pe.wait_ge(s_h, t * 2 + (c - 1))
                        for q in range(2):
                            f = (2 * c + q) * L
                            for k in range(KD):
                                last = pe.matmul(pup[c][:, q], xqT[:, k, bass.ds(t * P, P)], w1q[:, k, f:f + L],
                                                 start=(k == 0), stop=(k == KD - 1))
                        last.then_inc(s_up, 1)
                if has(i, r, 2):
                    pe.wait_ge(s_htc, u + 1)
                    if has(i, r, 4):
                        pe.wait_ge(s_x, u - 1)
                    for k in range(KH):
                        last = pe.matmul(pdn[r][:], hqT[:, r, k], w2q[:, k], start=(k == 0), stop=(k == KH - 1))
                    last.then_inc(s_dn, 1)

            run(pe, step, 2)


def build(nc, a, out):
    def dram(name, shape, dt=F32):
        return nc.dram_tensor(name, shape, dt, kind="Internal").ap()

    bc_dram = dram("bc_dram", (B, 2 * NS, L))
    xg_dram = dram("xg_dram", (ST, P, D))
    yg_dram = dram("yg_dram", (ST, P, D))
    qk_dram = dram("qk_dram", (2, 3, B, KD, P, L), BF16)
    v_dram = dram("v_dram", (NG, P, TB, G4 * VW))
    m_dram = dram("m_dram", (NG, 3 * G4 * TB, P), BF16)
    at_dram = dram("at_dram", (B, D, L))

    with ExitStack() as ctx:
        x_sb = ctx.enter_context(nc.sbuf_tensor("x_sb", [P, NT, D], F32))
        ident = ctx.enter_context(nc.sbuf_tensor("ident_sb", [P, P], F32))
        identb = ctx.enter_context(nc.sbuf_tensor("identb_sb", [P, P], BF16))
        tg = ctx.enter_context(nc.sbuf_tensor("tg_sb", [P, 4], F32))
        zeros = ctx.enter_context(nc.sbuf_tensor("zeros_sb", [P, D // 2], F32))
        s_x = ctx.enter_context(nc.semaphore("gates_loaded"))
        s_zero = ctx.enter_context(nc.semaphore("slots_zeroed"))

        with nc.Block() as block:
            @block.gpsimd
            def _(pool):
                pool.memset(zeros[:], 0.0)

            @block.sync
            def _(sp):
                sp.dma_start(tg[:, 0:2], a["g_xattn"].partition_broadcast(P)).then_inc(s_x, 16)
                sp.dma_start(tg[:, 2:4], a["g_ffn"].partition_broadcast(P)).then_inc(s_x, 16)
                sp.dma_start(ident[:], a["ident"]).then_inc(s_x, 16)

            @block.scalar
            def _(act):
                act.wait_ge(s_x, 48)
                act.activation(tg[:], tg[:], ACT.Tanh)
                act.activation(identb[:], ident[:], ACT.Copy)

        mamba(nc, x_sb, ident, tg[:, 0:1], a, bc_dram, xg_dram, zeros, s_zero)
        moe(nc, x_sb, ident, tg[:, 2:3], a, xg_dram, yg_dram, s_zero, v_dram)
        mark = ctx.enter_context(nc.semaphore("first_after_moe"))
        with nc.Block() as block:
            @block.gpsimd
            def _(pool):
                pool.sem_clear(range(s_zero.num + 1, mark.num))

        attention_inputs(nc, x_sb, ident, a, qk_dram)
        wo = ctx.enter_context(nc.sbuf_tensor("wo_sb", [P, KD, D], F32))
        bo = ctx.enter_context(nc.sbuf_tensor("bo_sb", [P, D], F32))
        w1 = ctx.enter_context(nc.sbuf_tensor("w1_sb", [P, KD, FF], F32))
        s_last = ctx.enter_context(nc.semaphore("last_weights_loaded"))
        attention(nc, ident, identb, a, qk_dram, v_dram, m_dram, at_dram, wo, bo, w1, s_last)
        attention_out_and_ffn(nc, x_sb, ident, identb, tg[:, 1:4:2], a, wo, bo, w1, s_last, at_dram, out)


def laid_out(z):
    def cols(v):
        return v.reshape(E4, P).T

    return {
        "x": z["x"].reshape(T, D),
        "ctxT": z["ctx_1024"].reshape(T, DC).T,
        "posT": z["fside_BxSx2_0"].reshape(T, 2).T,
        "g_xattn": z["g_xattn"],
        "g_ffn": z["g_ffn"],
        "in_wT": z["L0_xattn_in_proj_w"].T,
        "conv_w": z["L0_xattn_conv_w"],
        "conv_b": cols(z["L0_xattn_conv_b"]),
        "xp_wT": z["L0_xattn_x_proj_w"].T,
        "dt_wT": z["L0_xattn_dt_proj_w"].T,
        "dt_b": cols(z["L0_xattn_dt_proj_b"]),
        "A_log": z["L0_xattn_A_log"],
        "Dv": cols(z["L0_xattn_D"]),
        "gate_w": z["L0_ffn_gate_w"],
        "ex_bias": z["L0_ffn_expert_bias"],
        "sh_gate": z["L0_ffn_shared_gate_w"],
        "sh_up": z["L0_ffn_shared_up_w"],
        "sh_down": z["L0_ffn_shared_down_w"],
        "ex_gu": z["L0_ffn_experts_gate_up"],
        "ex_dn": z["L0_ffn_experts_down"],
        "wq": z["L1_xattn_Wq"],
        "wkv": z["L1_xattn_Wkv"],
        "wo": z["L1_xattn_Wout"],
        "bo": z["L1_xattn_bout"],
        "w1T": z["L1_ffn_w1"].T,
        "w2T": z["L1_ffn_w2"].T,
    }


def constants():
    f = np.arange(P)
    d = f % HD
    half = HD // 4
    freqs = (10000.0 ** (-np.arange(half) / half)).astype(np.float32)
    freq = np.zeros((2, P), np.float32)
    freq[d // (HD // 2), f] = freqs[d % (HD // 2) // 2]
    swap = np.zeros((P, P), np.float32)
    swap[f ^ 1, f] = 1
    sel = np.zeros((P, P), np.float32)
    sel[f // 32 * 32 + HD, f] = 1
    return {
        "ident": np.eye(P, dtype=np.float32),
        "lower": np.triu(np.ones((P, P), np.float32), 1),
        "iota": np.arange(64, dtype=np.float32),
        "freq": freq,
        "swap": swap,
        "sign": np.where(f % 2, 1, -1).astype(np.float32).reshape(P, 1),
        "sel": sel,
    }


def kernel(**inputs):
    import concourse.bacc as bacc
    from concourse.bass_utils import run_bass_kernel_spmd

    nc = bacc.Bacc("TRN2", target_bir_lowering=False, num_devices=1)
    host = {**laid_out({k: np.asarray(v) for k, v in inputs.items()}), **constants()}
    arrays = {f"in_{k}": np.ascontiguousarray(v) for k, v in host.items()}
    a = {k: nc.dram_tensor(f"in_{k}", host[k].shape, mybir.dt.from_np(host[k].dtype), kind="ExternalInput").ap()
         for k in host}
    out = nc.dram_tensor("out_0", (T, D), F32, kind="ExternalOutput").ap()
    build(nc, a, out)
    r = run_bass_kernel_spmd(nc, [arrays], core_ids=[0])
    return r.results[0]["out_0"].reshape(B, L, D)
```
